# Optimizing a Trainium2 kernel written in Bass

```python
import numpy as np
import jax
import jax.numpy as jnp

def _softmax(x, axis=-1):
    return jax.nn.softmax(x, axis=axis)

def _gelu(x):
    return jax.nn.gelu(x, approximate=True)

def _silu(x):
    return jax.nn.silu(x)

def _sigmoid(x):
    return jax.nn.sigmoid(x)

def _layernorm(x, axis=-1, eps=1e-05):
    m = jnp.mean(x, axis=axis, keepdims=True)
    v = jnp.var(x, axis=axis, keepdims=True)
    return (x - m) / jnp.sqrt(v + eps)

def _scatter_add(tgt, idx, src, axis=0):
    return tgt.at[idx].add(src)

def _segment_sum(src, seg, n):
    return jax.ops.segment_sum(src, seg, n)
kernel_name = 'mk_decoder_preln_d2_seqx_r4_d93380'

def setup_inputs(seed: int=0):
    np.random.seed(seed)
    _w = jnp.asarray

    def _rec_inputs():
        import jax
        import jax.numpy as jnp
        _rk = jax.random.key(seed)
        x = -0.0002928 + 1 * jax.random.normal(jax.random.fold_in(_rk, 1), (16, 256, 256), jnp.float32)
        _lenS = 256 - jax.random.randint(jax.random.fold_in(_rk, 7), (16,), 0, max(1, 256 // 4) + 1, jnp.int32)
        _lenS2 = 120 - jax.random.randint(jax.random.fold_in(_rk, 8), (16,), 0, max(1, 120 // 4) + 1, jnp.int32)
        _ctx_1024P = jax.random.normal(jax.random.fold_in(_rk, 11), (16, 16, 256), jnp.float32)
        _ctx_1024c = jax.random.dirichlet(jax.random.fold_in(_rk, 511), 0.3 * jnp.ones((16,), jnp.float32), (16, 120))
        _ctx_1024t = jnp.einsum('bsk,bkd->bsd', _ctx_1024c, _ctx_1024P)
        _ctx_1024t = _ctx_1024t * jax.lax.rsqrt(jnp.mean(jnp.square(_ctx_1024t)) + 1e-12) * 0.953939
        ctx_1024 = -1.39393e-06 + 0.999914 * (_ctx_1024t + 0.3 * jax.random.normal(jax.random.fold_in(_rk, 611), (16, 120, 256), jnp.float32))
        return (x, ctx_1024)
    x, ctx_1024 = _rec_inputs()

    def _L0_attn_setup():
        import jax, jax.numpy as jnp
        import numpy as np
        from math import sqrt
        D_MODEL = 256
        NUM_HEADS = 16
        D_HEAD = D_MODEL // NUM_HEADS
        THETA = 10000.0

        def _rope(x, freqs):
            xr = x[..., ::2]
            xi = x[..., 1::2]
            cos = jnp.cos(freqs)
            sin = jnp.sin(freqs)
            yr = xr * cos - xi * sin
            yi = xr * sin + xi * cos
            return jnp.stack([yr, yi], axis=-1).reshape(x.shape)
        key = jax.random.key(seed)
        k1, k2, k3 = jax.random.split(key, 3)
        X = jax.random.normal(k1, (4, 512, D_MODEL), dtype=jnp.float32)
        std_kqv = sqrt(2.0 / (D_MODEL + 3 * D_MODEL))
        W_KQV = std_kqv * jax.random.truncated_normal(k2, -3.0, 3.0, (3 * D_MODEL, D_MODEL), dtype=jnp.float32)
        std_o = sqrt(2.0 / (D_MODEL + D_MODEL))
        W_O = std_o * jax.random.truncated_normal(k3, -3.0, 3.0, (D_MODEL, D_MODEL), dtype=jnp.float32)
        return {'X': X, 'W_KQV': W_KQV, 'W_O': W_O}
    _L0_attn_all = _L0_attn_setup()
    _L0_attn_in = {k: v for k, v in _L0_attn_all.items() if k in ('W_KQV', 'W_O')}
    del _L0_attn_all

    def _L0_xattn_setup():
        import jax, jax.numpy as jnp
        import numpy as np
        EMBED_DIM = 256
        NUM_HEADS = 16
        HEAD_DIM = EMBED_DIM // NUM_HEADS

        def _split_heads(x):
            B, T, C = x.shape
            return x.reshape(B, T, NUM_HEADS, HEAD_DIM).transpose(0, 2, 1, 3)
        key = jax.random.key(seed)
        ks = jax.random.split(key, 11)
        B, T, C = (2, 512, EMBED_DIM)
        s = 1.0 / np.sqrt(C)
        inp = {'q': jax.random.normal(ks[0], (B, T, C), jnp.float32), 'k': jax.random.normal(ks[1], (B, T, C), jnp.float32), 'v': jax.random.normal(ks[2], (B, T, C), jnp.float32), 'Wq': jax.random.normal(ks[3], (C, C), jnp.float32) * s, 'bq': jax.random.normal(ks[4], (C,), jnp.float32) * s, 'Wk': jax.random.normal(ks[5], (C, C), jnp.float32) * s, 'bk': jax.random.normal(ks[6], (C,), jnp.float32) * s, 'Wv': jax.random.normal(ks[7], (C, C), jnp.float32) * s, 'bv': jax.random.normal(ks[8], (C,), jnp.float32) * s, 'Wo': jax.random.normal(ks[9], (C, C), jnp.float32) * s, 'bo': jax.random.normal(ks[10], (C,), jnp.float32) * s}
        return inp
    _L0_xattn_all = _L0_xattn_setup()
    _L0_xattn_in = {k: v for k, v in _L0_xattn_all.items() if k in ('Wq', 'bq', 'Wk', 'bk', 'Wv', 'bv', 'Wo', 'bo')}
    del _L0_xattn_all

    def _L0_ffn_setup():
        import jax, jax.numpy as jnp
        import numpy as np
        D_IN = 256
        D_OUT = 256
        D_QUERY = 64
        N_HEADS = 8
        N_EXPERTS = 16384
        N_SQRT = 64
        TOPK = 10
        DQ_HALF = D_QUERY // 2
        key = jax.random.key(seed)
        ks = jax.random.split(key, 7)
        B, S = (2, 256)
        x = jax.random.normal(ks[0], (B, S, D_IN), dtype=jnp.float32)
        Wq = jax.random.normal(ks[1], (D_IN, D_QUERY * N_HEADS), dtype=jnp.float32) / np.sqrt(D_IN)
        bq = jnp.zeros((D_QUERY * N_HEADS,), dtype=jnp.float32)
        K1 = jax.random.normal(ks[2], (N_SQRT, DQ_HALF), dtype=jnp.float32)
        K2 = jax.random.normal(ks[3], (N_SQRT, DQ_HALF), dtype=jnp.float32)
        W_up = jax.random.normal(ks[4], (N_EXPERTS, D_OUT), dtype=jnp.float32)
        W_down = jax.random.normal(ks[5], (N_EXPERTS, D_IN), dtype=jnp.float32)
        return {'x': x, 'Wq': Wq, 'bq': bq, 'K1': K1, 'K2': K2, 'W_up': W_up, 'W_down': W_down}
    _L0_ffn_all = _L0_ffn_setup()
    _L0_ffn_in = {k: v for k, v in _L0_ffn_all.items() if k in ('Wq', 'bq', 'K1', 'K2', 'W_up', 'W_down')}
    del _L0_ffn_all

    def _L1_attn_setup():
        import jax, jax.numpy as jnp
        import numpy as np
        import math
        D_MODEL = 256
        N_HEADS = 16
        HEAD_DIM = D_MODEL // N_HEADS
        BAND_RADIUS = 2
        BAND_VAL = 0.1

        def _band_mask(S, dtype):
            i = jnp.arange(S)
            band = (jnp.abs(i[:, None] - i[None, :]) <= BAND_RADIUS).astype(dtype) * BAND_VAL
            return band[None, None, :, :]
        key = jax.random.key(seed)
        ks = jax.random.split(key, 12)
        B, S = (4, 512)
        scale = 1.0 / math.sqrt(D_MODEL)
        inp = {'x': jax.random.normal(ks[0], (B, S, D_MODEL), dtype=jnp.float32), 'ocr_context': jax.random.normal(ks[1], (B, S, D_MODEL), dtype=jnp.float32), 'Wq': jax.random.normal(ks[2], (D_MODEL, D_MODEL), dtype=jnp.float32) * scale, 'bq': jnp.zeros((D_MODEL,), dtype=jnp.float32), 'Wk': jax.random.normal(ks[3], (D_MODEL, D_MODEL), dtype=jnp.float32) * scale, 'bk': jnp.zeros((D_MODEL,), dtype=jnp.float32), 'Wv': jax.random.normal(ks[4], (D_MODEL, D_MODEL), dtype=jnp.float32) * scale, 'bv': jnp.zeros((D_MODEL,), dtype=jnp.float32), 'Wo': jax.random.normal(ks[5], (D_MODEL, D_MODEL), dtype=jnp.float32) * scale, 'bo': jnp.zeros((D_MODEL,), dtype=jnp.float32), 'ocr_bias': jax.random.normal(ks[6], (D_MODEL,), dtype=jnp.float32)}
        return inp
    _L1_attn_all = _L1_attn_setup()
    _L1_attn_in = {k: v for k, v in _L1_attn_all.items() if k in ('ocr_context', 'Wq', 'bq', 'Wk', 'bk', 'Wv', 'bv', 'Wo', 'bo', 'ocr_bias')}
    del _L1_attn_all

    def _L1_xattn_setup():
        import jax, jax.numpy as jnp
        import numpy as np
        B, C_LEN, Q_LEN, D = (8, 512, 128, 256)
        key = jax.random.key(seed)
        ks = jax.random.split(key, 10)
        scale = 1.0 / np.sqrt(D)
        return {'c': jax.random.normal(ks[0], (B, C_LEN, D), dtype=jnp.float32), 'q': jax.random.normal(ks[1], (B, Q_LEN, D), dtype=jnp.float32), 'w_cq': jax.random.normal(ks[2], (D,), dtype=jnp.float32) * scale, 'b_cq': jax.random.normal(ks[3], (), dtype=jnp.float32) * scale, 'w_c': jax.random.normal(ks[4], (D,), dtype=jnp.float32) * scale, 'b_c': jax.random.normal(ks[5], (), dtype=jnp.float32) * scale, 'w_q': jax.random.normal(ks[6], (D,), dtype=jnp.float32) * scale, 'b_q': jax.random.normal(ks[7], (), dtype=jnp.float32) * scale, 'W_l': jax.random.normal(ks[8], (D, 4 * D), dtype=jnp.float32) * (1.0 / np.sqrt(4 * D)), 'b_l': jax.random.normal(ks[9], (D,), dtype=jnp.float32) * (1.0 / np.sqrt(4 * D))}
    _L1_xattn_all = _L1_xattn_setup()
    _L1_xattn_in = {k: v for k, v in _L1_xattn_all.items() if k in ('w_cq', 'b_cq', 'w_c', 'b_c', 'w_q', 'b_q', 'W_l', 'b_l')}
    del _L1_xattn_all

    def _L1_ffn_setup():
        import jax, jax.numpy as jnp
        import numpy as np
        B, S, D = (4, 512, 256)
        EXP = 4
        H = EXP * D
        E = 8
        TOP_K = 2
        key = jax.random.key(seed)
        ks = jax.random.split(key, 8)
        scale1 = 1.0 / np.sqrt(D)
        scale2 = 1.0 / np.sqrt(H)
        x = jax.random.normal(ks[0], (B, S, D), dtype=jnp.float32)
        W1 = jax.random.uniform(ks[1], (E, D, H), jnp.float32, -scale1, scale1)
        b1 = jax.random.uniform(ks[2], (E, H), jnp.float32, -scale1, scale1)
        W2 = jax.random.uniform(ks[3], (E, H, D), jnp.float32, -scale2, scale2)
        b2 = jax.random.uniform(ks[4], (E, D), jnp.float32, -scale2, scale2)
        Wr = jax.random.uniform(ks[5], (D, E), jnp.float32, -scale1, scale1)
        br = jax.random.uniform(ks[6], (E,), jnp.float32, -scale1, scale1)
        return {'input_emb': x, 'W1': W1, 'b1': b1, 'W2': W2, 'b2': b2, 'Wr': Wr, 'br': br}
    _L1_ffn_all = _L1_ffn_setup()
    _L1_ffn_in = {k: v for k, v in _L1_ffn_all.items() if k in ('W1', 'b1', 'W2', 'b2', 'Wr', 'br')}
    del _L1_ffn_all
    return {'x': x, 'ctx_1024': ctx_1024, 'L0_attn_W_KQV': _L0_attn_in['W_KQV'], 'L0_attn_W_O': _L0_attn_in['W_O'], 'L0_xattn_Wq': _L0_xattn_in['Wq'], 'L0_xattn_bq': _L0_xattn_in['bq'], 'L0_xattn_Wk': _L0_xattn_in['Wk'], 'L0_xattn_bk': _L0_xattn_in['bk'], 'L0_xattn_Wv': _L0_xattn_in['Wv'], 'L0_xattn_bv': _L0_xattn_in['bv'], 'L0_xattn_Wo': _L0_xattn_in['Wo'], 'L0_xattn_bo': _L0_xattn_in['bo'], 'L0_ffn_Wq': _L0_ffn_in['Wq'], 'L0_ffn_bq': _L0_ffn_in['bq'], 'L0_ffn_K1': _L0_ffn_in['K1'], 'L0_ffn_K2': _L0_ffn_in['K2'], 'L0_ffn_W_up': _L0_ffn_in['W_up'], 'L0_ffn_W_down': _L0_ffn_in['W_down'], 'L1_attn_ocr_context': _L1_attn_in['ocr_context'], 'L1_attn_Wq': _L1_attn_in['Wq'], 'L1_attn_bq': _L1_attn_in['bq'], 'L1_attn_Wk': _L1_attn_in['Wk'], 'L1_attn_bk': _L1_attn_in['bk'], 'L1_attn_Wv': _L1_attn_in['Wv'], 'L1_attn_bv': _L1_attn_in['bv'], 'L1_attn_Wo': _L1_attn_in['Wo'], 'L1_attn_bo': _L1_attn_in['bo'], 'L1_attn_ocr_bias': _L1_attn_in['ocr_bias'], 'L1_xattn_w_cq': _L1_xattn_in['w_cq'], 'L1_xattn_b_cq': _L1_xattn_in['b_cq'], 'L1_xattn_w_c': _L1_xattn_in['w_c'], 'L1_xattn_b_c': _L1_xattn_in['b_c'], 'L1_xattn_w_q': _L1_xattn_in['w_q'], 'L1_xattn_b_q': _L1_xattn_in['b_q'], 'L1_xattn_W_l': _L1_xattn_in['W_l'], 'L1_xattn_b_l': _L1_xattn_in['b_l'], 'L1_ffn_W1': _L1_ffn_in['W1'], 'L1_ffn_b1': _L1_ffn_in['b1'], 'L1_ffn_W2': _L1_ffn_in['W2'], 'L1_ffn_b2': _L1_ffn_in['b2'], 'L1_ffn_Wr': _L1_ffn_in['Wr'], 'L1_ffn_br': _L1_ffn_in['br']}

def reference(x, ctx_1024, L0_attn_W_KQV, L0_attn_W_O, L0_xattn_Wq, L0_xattn_bq, L0_xattn_Wk, L0_xattn_bk, L0_xattn_Wv, L0_xattn_bv, L0_xattn_Wo, L0_xattn_bo, L0_ffn_Wq, L0_ffn_bq, L0_ffn_K1, L0_ffn_K2, L0_ffn_W_up, L0_ffn_W_down, L1_attn_ocr_context, L1_attn_Wq, L1_attn_bq, L1_attn_Wk, L1_attn_bk, L1_attn_Wv, L1_attn_bv, L1_attn_Wo, L1_attn_bo, L1_attn_ocr_bias, L1_xattn_w_cq, L1_xattn_b_cq, L1_xattn_w_c, L1_xattn_b_c, L1_xattn_w_q, L1_xattn_b_q, L1_xattn_W_l, L1_xattn_b_l, L1_ffn_W1, L1_ffn_b1, L1_ffn_W2, L1_ffn_b2, L1_ffn_Wr, L1_ffn_br):
    import jax
    import jax.numpy as jnp

    def _L0_attn_ref(X, W_KQV, W_O):
        import jax, jax.numpy as jnp
        import numpy as np
        from math import sqrt
        D_MODEL = 256
        NUM_HEADS = 16
        D_HEAD = D_MODEL // NUM_HEADS
        THETA = 10000.0

        def _rope(x, freqs):
            xr = x[..., ::2]
            xi = x[..., 1::2]
            cos = jnp.cos(freqs)
            sin = jnp.sin(freqs)
            yr = xr * cos - xi * sin
            yi = xr * sin + xi * cos
            return jnp.stack([yr, yi], axis=-1).reshape(x.shape)
        B, S, D = X.shape
        H, d = (NUM_HEADS, D_HEAD)
        KQV = jnp.einsum('bsd,ed->bse', X, W_KQV)
        K, Q, V = jnp.split(KQV, [D, 2 * D], axis=-1)

        def to_heads(t):
            return t.reshape(B, S, H, d).transpose(0, 2, 1, 3)
        K, Q, V = (to_heads(K), to_heads(Q), to_heads(V))
        inv_freq = 1.0 / THETA ** (jnp.arange(0, d, 2, dtype=jnp.float32) / d)
        pos = jnp.arange(S, dtype=jnp.float32)
        freqs = pos[:, None] * inv_freq[None, :]
        Q = _rope(Q, freqs)
        K = _rope(K, freqs)
        scores = jnp.einsum('bhqd,bhkd->bhqk', Q, K) / sqrt(d)
        causal = jnp.triu(jnp.ones((S, S), dtype=bool), k=1)
        scores = jnp.where(causal, -jnp.inf, scores)
        probs = jax.nn.softmax(scores, axis=-1)
        heads = jnp.einsum('bhqk,bhkd->bhqd', probs, V)
        acts = heads.transpose(0, 2, 1, 3).reshape(B, S, D)
        return jnp.einsum('bsd,ed->bse', acts, W_O)

    def _L0_xattn_ref(q, k, v, Wq, bq, Wk, bk, Wv, bv, Wo, bo):
        import jax, jax.numpy as jnp
        import numpy as np
        EMBED_DIM = 256
        NUM_HEADS = 16
        HEAD_DIM = EMBED_DIM // NUM_HEADS

        def _split_heads(x):
            B, T, C = x.shape
            return x.reshape(B, T, NUM_HEADS, HEAD_DIM).transpose(0, 2, 1, 3)
        B, Tq, C = q.shape
        qh = _split_heads(q @ Wq.T + bq)
        kh = _split_heads(k @ Wk.T + bk)
        vh = _split_heads(v @ Wv.T + bv)
        scale = 1.0 / np.sqrt(HEAD_DIM).astype(np.float32)
        logits = jnp.einsum('bhqd,bhkd->bhqk', qh, kh) * scale
        attn = jax.nn.softmax(logits, axis=-1)
        out = jnp.einsum('bhqk,bhkd->bhqd', attn, vh)
        out = out.transpose(0, 2, 1, 3).reshape(B, Tq, C)
        return out @ Wo.T + bo

    def _L0_ffn_ref(x, Wq, bq, K1, K2, W_up, W_down):
        import jax, jax.numpy as jnp
        import numpy as np
        D_IN = 256
        D_OUT = 256
        D_QUERY = 64
        N_HEADS = 8
        N_EXPERTS = 16384
        N_SQRT = 64
        TOPK = 10
        DQ_HALF = D_QUERY // 2
        B, S, _ = x.shape
        q = (x @ Wq + bq).reshape(B, S, N_HEADS, D_QUERY)
        q1, q2 = (q[..., :DQ_HALF], q[..., DQ_HALF:])
        s1 = jnp.einsum('bshd,nd->bshn', q1, K1)
        s2 = jnp.einsum('bshd,nd->bshn', q2, K2)
        v1, i1 = jax.lax.top_k(s1, TOPK)
        v2, i2 = jax.lax.top_k(s2, TOPK)
        all_scores = (v1[..., :, None] + v2[..., None, :]).reshape(B, S, N_HEADS, TOPK * TOPK)
        all_indices = (i1[..., :, None] * N_SQRT + i2[..., None, :]).reshape(B, S, N_HEADS, TOPK * TOPK)
        vals, best = jax.lax.top_k(all_scores, TOPK)
        expert_idx = jnp.take_along_axis(all_indices, best, axis=-1)
        w_down = W_down[expert_idx]
        w_up = W_up[expert_idx]
        scores = jax.nn.softmax(vals, axis=-1)
        h = jnp.einsum('bsd,bshkd->bshk', x, w_down)
        h = jax.nn.gelu(h, approximate=False) * scores
        out = jnp.einsum('bshk,bshkd->bsd', h, w_up)
        return out

    def _L1_attn_ref(x, ocr_context, Wq, bq, Wk, bk, Wv, bv, Wo, bo, ocr_bias):
        import jax, jax.numpy as jnp
        import numpy as np
        import math
        D_MODEL = 256
        N_HEADS = 16
        HEAD_DIM = D_MODEL // N_HEADS
        BAND_RADIUS = 2
        BAND_VAL = 0.1

        def _band_mask(S, dtype):
            i = jnp.arange(S)
            band = (jnp.abs(i[:, None] - i[None, :]) <= BAND_RADIUS).astype(dtype) * BAND_VAL
            return band[None, None, :, :]
        B, S, _ = x.shape
        q = x @ Wq.T + bq + ocr_bias
        k = x @ Wk.T + bk
        v = x @ Wv.T + bv
        q = q.reshape(B, S, N_HEADS, HEAD_DIM).transpose(0, 2, 1, 3)
        k = k.reshape(B, S, N_HEADS, HEAD_DIM).transpose(0, 2, 1, 3)
        v = v.reshape(B, S, N_HEADS, HEAD_DIM).transpose(0, 2, 1, 3)
        scores = jnp.einsum('bhsd,bhtd->bhst', q, k) / math.sqrt(HEAD_DIM)
        scores = scores + _band_mask(S, scores.dtype)
        attn = jax.nn.softmax(scores, axis=-1)
        out = jnp.einsum('bhst,bhtd->bhsd', attn, v)
        out = out.transpose(0, 2, 1, 3).reshape(B, S, D_MODEL)
        return out @ Wo.T + bo

    def _L1_xattn_ref(c, q, w_cq, b_cq, w_c, b_c, w_q, b_q, W_l, b_l):
        import jax, jax.numpy as jnp
        import numpy as np
        B, C_LEN, Q_LEN, D = (8, 512, 128, 256)
        cq = jnp.einsum('bcd,bqd,d->bcq', c, q, w_cq) + b_cq
        s = (c @ w_c + b_c)[:, :, None] + (q @ w_q + b_q)[:, None, :] + cq
        a = jax.nn.softmax(s, axis=2)
        c2q_att = jnp.einsum('bcq,bqd->bcd', a, q)
        b_att = jax.nn.softmax(jnp.max(s, axis=2), axis=1)
        q2c_att = jnp.einsum('bc,bcd->bd', b_att, c)[:, None, :]
        x = jnp.concatenate([c, c2q_att, c * c2q_att, c * q2c_att], axis=-1)
        z = x @ W_l.T + b_l
        return z

    def _L1_ffn_ref(input_emb, W1, b1, W2, b2, Wr, br):
        import jax, jax.numpy as jnp
        import numpy as np
        B, S, D = (4, 512, 256)
        EXP = 4
        H = EXP * D
        E = 8
        TOP_K = 2
        logits = jnp.einsum('bsd,de->bse', input_emb, Wr) + br
        route_w = jax.nn.softmax(logits, axis=-1)
        _, topk_idx = jax.lax.top_k(route_w, TOP_K)
        mask = jax.nn.one_hot(topk_idx, E, dtype=route_w.dtype).sum(-2)
        routed = route_w * mask
        routed = routed / routed.sum(axis=-1, keepdims=True)
        h = jax.nn.relu(jnp.einsum('bsd,edh->ebsh', input_emb, W1) + b1[:, None, None, :])
        expert_out = jnp.einsum('ebsh,ehd->ebsd', h, W2) + b2[:, None, None, :]
        return jnp.einsum('bse,ebsd->bsd', routed, expert_out)
    x = x + _L0_attn_ref(_layernorm(x, axis=-1), L0_attn_W_KQV, L0_attn_W_O)
    x = x + _L0_xattn_ref(_layernorm(x, axis=-1), ctx_1024, ctx_1024, L0_xattn_Wq, L0_xattn_bq, L0_xattn_Wk, L0_xattn_bk, L0_xattn_Wv, L0_xattn_bv, L0_xattn_Wo, L0_xattn_bo)
    x = x + _L0_ffn_ref(_layernorm(x, axis=-1), L0_ffn_Wq, L0_ffn_bq, L0_ffn_K1, L0_ffn_K2, L0_ffn_W_up, L0_ffn_W_down)
    x = x + _L1_attn_ref(_layernorm(x, axis=-1), L1_attn_ocr_context, L1_attn_Wq, L1_attn_bq, L1_attn_Wk, L1_attn_bk, L1_attn_Wv, L1_attn_bv, L1_attn_Wo, L1_attn_bo, L1_attn_ocr_bias)
    x = x + _L1_xattn_ref(_layernorm(x, axis=-1), ctx_1024, L1_xattn_w_cq, L1_xattn_b_cq, L1_xattn_w_c, L1_xattn_b_c, L1_xattn_w_q, L1_xattn_b_q, L1_xattn_W_l, L1_xattn_b_l)
    x = x + _L1_ffn_ref(_layernorm(x, axis=-1), L1_ffn_W1, L1_ffn_b1, L1_ffn_W2, L1_ffn_b2, L1_ffn_Wr, L1_ffn_br)
    return x

_drawn_inputs = setup_inputs


def setup_inputs(seed=0):
    import zlib

    import numpy as np

    out = dict(_drawn_inputs(seed))
    spreads = {'L0_ffn_bq': (0.0, 0.1),
     'L1_attn_bq': (0.0, 0.8),
     'L1_attn_bk': (0.0, 2.0),
     'L1_attn_bv': (0.0, 0.8),
     'L1_attn_bo': (0.0, 0.8)}
    factors = {'L0_xattn_bk': 64.0,
     'L1_attn_Wq': 7.833,
     'L1_attn_Wk': 5.976,
     'L1_attn_Wv': 5.088,
     'L1_attn_Wo': 4.484,
     'L1_attn_ocr_bias': 7.418,
     'L1_xattn_w_cq': 6.16,
     'L1_xattn_w_c': 13.537,
     'L1_xattn_w_q': 6.488,
     'L1_xattn_b_l': 38.169,
     'L1_ffn_W1': 8.0,
     'L1_ffn_b1': 21.496,
     'L1_ffn_W2': 6.745,
     'L1_ffn_b2': 64.0,
     'L1_ffn_Wr': 7.621,
     'L1_ffn_br': 8.0}
    for name, (base, spread) in spreads.items():
        noise = np.random.default_rng([zlib.crc32(name.encode()), seed]).standard_normal(out[name].shape)
        drawn = base * np.exp(spread * noise) if base else spread * noise
        out[name] = jnp.asarray(drawn.astype(out[name].dtype))
    for name, factor in factors.items():
        out[name] = (out[name] * factor).astype(out[name].dtype)
    return out
```

```python
from contextlib import ExitStack

import concourse.bass as bass
from concourse import mybir

P = 128
ALU = mybir.AluOpType
ACT = mybir.ActivationFunctionType
AX = mybir.AxisListType
F32 = mybir.dt.float32
BF16 = mybir.dt.bfloat16
U32 = mybir.dt.uint32
I32 = mybir.dt.int32

B, S, D = 16, 256, 256
CTX = 120
HEADS, HD = 16, 16
SLOT = 32
QUADS = HEADS // 4
TT = S // P
TILES = B * TT
DC = D // P
EPS = 1e-5


def wait(eng, sem, value):
    if isinstance(value, int) and value <= 0:
        return
    eng.wait_ge(sem, value)


class Steps:

    def __init__(self, eng, sem):
        self.eng, self.sem, self.n = eng, sem, 0

    def link(self, instruction):
        self.n += 1
        instruction.then_inc(self.sem, 1)
        self.eng.wait_ge(self.sem, self.n)

    def again(self):
        if self.n:
            self.eng.sem_clear(self.sem)
            self.n = 0


class Room:

    def __init__(self, nc, ctx, stage):
        self.nc, self.ctx, self.stage = nc, ctx, stage
        self.sems = []
        ctx.callback(self.close)

    def close(self):
        self.nc.clear_and_free_semaphores(self.sems)
        self.nc.all_engine_barrier()

    def sb(self, name, shape, dt=F32):
        return self.ctx.enter_context(self.nc.sbuf_tensor(f"{self.stage}_{name}", shape, dt))

    def ps(self, name, shape, dt=F32):
        return self.ctx.enter_context(self.nc.psum_tensor(f"{self.stage}_{name}", shape, dt))

    def sem(self, name):
        self.sems.append(self.nc.alloc_semaphore(f"{self.stage}_{name}"))
        return self.sems[-1]


def load_stage(nc, x_all, ident, d):
    with ExitStack() as ctx:
        r = Room(nc, ctx, "load")
        loaded = r.sem("loaded")
        block = ctx.enter_context(nc.Block())

        @block.sync
        def _(sp):
            xv = d["x"].rearrange("b (t p) c -> p (b t) c", p=P)
            for k in range(4):
                n = TILES // 4
                sp.dma_start(x_all[:, k * n:(k + 1) * n, :], xv[:, k * n:(k + 1) * n, :]).then_inc(loaded, 16)
            sp.dma_start(ident[:], d["ident"]).then_inc(loaded, 16)
            sp.wait_ge(loaded, 16 * 5)


def norm_stage(nc, name, x_all, mean, rstd):
    with ExitStack() as ctx:
        r = Room(nc, ctx, name)
        moments = r.sb("moments", [P, 6])
        mv = r.sb("mv", [P, 2])
        var = r.sb("var", [P, TILES, 1])
        root = r.sb("root", [P, TILES, 1])
        guess = r.sb("guess", [P, TILES, 1])
        t0 = r.sb("t0", [P, TILES, 1])
        step = r.sem("step")
        var_ready = r.sem("var_ready")
        root_ready = r.sem("root_ready")
        block = ctx.enter_context(nc.Block())

        @block.scalar
        def _(act):
            act.wait_ge(var_ready, 1)
            nc.scalar.activation(root[:], var[:], ACT.Sqrt).then_inc(root_ready, 1)

        @block.vector
        def _(dve):
            steps = Steps(dve, step)
            with dve.Fori(0, TILES) as t:
                steps.link(nc.vector.bn_stats(moments[:], x_all[:, t, :]))
                steps.link(nc.vector.bn_aggr(mv[:], moments[:]))
                steps.link(nc.vector.tensor_copy(mean[:, t, :], mv[:, 0:1]))
                steps.link(nc.vector.tensor_scalar(var[:, t, :], mv[:, 1:2], EPS, None, ALU.add))
                steps.again()
            nc.vector.drain().then_inc(var_ready, 1)
            dve.wait_ge(root_ready, 1)
            steps.link(nc.vector.reciprocal(guess[:], root[:]))
            steps.link(nc.vector.tensor_tensor(t0[:], guess[:], guess[:], ALU.mult))
            steps.link(nc.vector.tensor_tensor(root[:], t0[:], var[:], ALU.mult))
            steps.link(nc.vector.tensor_scalar(t0[:], root[:], -0.5, 1.5, ALU.mult, ALU.add))
            steps.link(nc.vector.tensor_tensor(rstd[:], guess[:], t0[:], ALU.mult))


def attention_stage(nc, kind, x_all, mean, rstd, ident, d):
    rope = kind == "causal"
    cross = kind == "cross"
    KN = CTX if cross else P
    KT = 1 if cross else TT
    KS = KT * KN
    if kind == "causal":
        blocks = [(0, 0), (1, 0), (1, 1)]
    else:
        blocks = [(q, k) for q in range(TT) for k in range(KT)]
    col = {blk: n * KN for n, blk in enumerate(blocks)}
    span = {q: (min(col[b] for b in blocks if b[0] == q), KN * sum(b[0] == q for b in blocks)) for q in range(TT)}
    COLS = len(blocks) * KN
    NPROJ = 2 * QUADS

    with ExitStack() as ctx:
        r = Room(nc, ctx, kind)
        sb, ps, sem = r.sb, r.ps, r.sem
        names = ["wq", "wqs", "wk", "wks"] if rope else ["wq", "wk"]
        w = {n: sb(n, [P, DC, QUADS * P]) for n in names}
        w |= {n: sb(n, [P, DC, D]) for n in ("wv", "wo")}
        nload = len(w)
        if rope:
            tab = {n: sb(n, [P, S]) for n in ("cosq", "sinq", "cosk", "sink")}
            ident16 = sb("ident16", [P, P], BF16)
            mask = sb("mask", [P, P], BF16)
            maskf = sb("maskf", [P, P])
            rot = sb("rot", [P, 2, 2, S])
            nload += 5
        else:
            bq = sb("bq", [P, QUADS])
            bk = sb("bk", [P, QUADS])
            bv = sb("bv", [P, D])
            bo = sb("bo", [P, D])
            nload += 4
        if kind == "band":
            bias2 = sb("bias2", [P, QUADS])
            band = sb("band", [P, TT, S])
            nload += 2
        if cross:
            ctx_sb = sb("ctx", [P, 2, D])
            ctxT = sb("ctxT", [P, DC, CTX])
        xn = sb("xn", [P, TT, D])
        xnT = sb("xnT", [P, DC, S])
        qT = sb("qT", [P, 2, QUADS, S])
        kT = sb("kT", [P, 2, QUADS, KS])
        va = sb("va", [P, 2, KT, HEADS, HD + 1])
        nmax = sb("nmax", [P, 2, TT])
        prob = sb("prob", [P, 2, COLS])
        probT = sb("probT", [P, 2, len(blocks), P])
        rsum = sb("rsum", [P, TT, HEADS])
        on = sb("on", [P, TT, D])
        onT = sb("onT", [P, DC, S])
        ytmp = sb("ytmp", [P, TT, D])
        warm = sb("warm", [P, 1])

        ps_s = ps("ps_s", [P, 2, 512])
        ps_t = ps("ps_t", [P, 2, 512])
        ps_o = ps("ps_o", [P, TT, 512])
        ps_p = ps("ps_p", [P, 2, 512])

        weights = sem("weights")
        ready = sem("ready")
        ctx_in = sem("ctx_in")
        xn_ready = sem("xn_ready")
        xt_done = sem("xt_done")
        xt_used = sem("xt_used")
        proj_done = sem("proj_done")
        proj_used = sem("proj_used")
        v_done = sem("v_done")
        v_used = sem("v_used")
        s_done = sem("s_done")
        nmax_ready = sem("nmax_ready")
        p_ready = sem("p_ready")
        pt_done = sem("pt_done")
        pt_used = sem("pt_used")
        pv_done = sem("pv_done")
        o_used = sem("o_used")
        ot_done = sem("ot_done")
        ot_used = sem("ot_used")
        y_done = sem("y_done")
        y_used = sem("y_used")
        step = sem("step")
        block = ctx.enter_context(nc.Block())

        @block.sync
        def _(sp):
            def chunks(ap):
                return ap.rearrange("(c p) n -> p c n", p=P)
            for n in w:
                sp.dma_start(w[n][:], chunks(d[f"{kind}_{n}"])).then_inc(weights, 16)
            if rope:
                for n in tab:
                    sp.dma_start(tab[n][:], d[f"{n}"]).then_inc(weights, 16)
                sp.dma_start(maskf[:], d["mask"]).then_inc(weights, 16)
            else:
                sp.dma_start(bq[:], d[f"{kind}_bq"]).then_inc(weights, 16)
                sp.dma_start(bk[:], d[f"{kind}_bk"]).then_inc(weights, 16)
                sp.dma_start(bv[:], d[f"{kind}_bv"].partition_broadcast(P)).then_inc(weights, 16)
                sp.dma_start(bo[:], d[f"{kind}_bo"].partition_broadcast(P)).then_inc(weights, 16)
            if kind == "band":
                sp.dma_start(bias2[:], d["band_bias"]).then_inc(weights, 16)
                sp.dma_start(band[:], d["band"].rearrange("(c p) n -> p c n", p=P)).then_inc(weights, 16)
            if cross:
                def fetch(b, par):
                    wait(sp, v_done, b - 1)
                    wait(sp, ctx_in, 16 * b)
                    sp.dma_start(ctx_sb[0:CTX, par, :], d["ctx"][b]).then_inc(ctx_in, 16)
                for b in range(B):
                    fetch(b, b % 2)
            sp.wait_ge(weights, 16 * nload)


        def schedule(prologue, heads, epilogue):
            def beside(b, par, first=False, last=False):
                parts = []
                if not first:
                    parts += epilogue(b - 1, 1 - par)
                if not last:
                    parts += prologue(b + 1, 1 - par)
                heads(b, par, parts)
            for p in prologue(0, 0):
                p()
            beside(0, 0, first=True)
            return beside

        def run(eng, prologue, heads, epilogue):
            beside = schedule(prologue, heads, epilogue)
            with eng.Fori(0, B // 2 - 1) as i:
                beside(2 * i + 1, 1)
                beside(2 * i + 2, 0)
            beside(B - 1, 1, last=True)
            for p in epilogue(B - 1, 1):
                p()

        @block.tensor
        def _(pe):
            pe.wait_ge(weights, 16 * nload)
            pe.wait_ge(ready, 1)

            def prologue(b, par):
                def transposes():
                    pe.wait_ge(xn_ready, b + 1)
                    wait(pe, proj_used, NPROJ * b)
                    for t in range(TT):
                        for c in range(DC):
                            mm = nc.tensor.transpose(ps_p[:, 0, c * S + t * P:c * S + (t + 1) * P],
                                                     xn[:, t, c * P:(c + 1) * P], ident[:])
                    mm.then_inc(xt_done, 1)
                    if cross:
                        pe.wait_ge(ctx_in, 16 * (b + 1))
                        wait(pe, v_used, b)
                        wait(pe, y_used, b - 1)
                        for c in range(DC):
                            mm = nc.tensor.transpose(ps_p[:, 1, c * CTX:(c + 1) * CTX],
                                                     ctx_sb[0:CTX, par, c * P:(c + 1) * P], ident[0:CTX, 0:CTX])
                        mm.then_inc(xt_done, 1)

                def project(j):
                    def go():
                        if j == 0:
                            pe.wait_ge(xt_used, (2 if cross else 1) * (b + 1))
                            wait(pe, v_used, b)
                            wait(pe, y_used, b - 1)
                        if j >= 2:
                            pe.wait_ge(proj_used, NPROJ * b + j - 1)
                        isq, quad = j < QUADS, j % QUADS
                        src, n = (ctxT, CTX) if cross and not isq else (xnT, S)
                        for k, name in enumerate(([("wq", "wqs"), ("wk", "wks")] if rope else [("wq",), ("wk",)])[0 if isq else 1]):
                            for c in range(DC):
                                mm = nc.tensor.matmul(ps_p[:, (j + 1) % 2, k * S:k * S + n],
                                                      w[name][:, c, quad * P:(quad + 1) * P], src[:, c, :],
                                                      start=(c == 0), stop=(c == DC - 1))
                        mm.then_inc(proj_done, 1)
                    return go

                def values():
                    pe.wait_ge(proj_used, NPROJ * b + NPROJ - 1)
                    src = ctxT if cross else xnT
                    for k in range(KT):
                        for c in range(DC):
                            mm = nc.tensor.matmul(ps_p[0:KN, 1, k * D:(k + 1) * D], src[:, c, k * KN:(k + 1) * KN],
                                                  w["wv"][:, c, :], start=(c == 0), stop=(c == DC - 1))
                    mm.then_inc(v_done, 1)
                return [transposes] + [project(j) for j in range(NPROJ)] + [values]

            def epilogue(b, par):
                def transposes():
                    pe.wait_ge(o_used, b + 1)
                    if isinstance(b, int) and b == B - 1:
                        pe.wait_ge(proj_used, NPROJ * B)
                    else:
                        pe.wait_ge(proj_used, NPROJ * (b + 2))
                    for t in range(TT):
                        for c in range(DC):
                            mm = nc.tensor.transpose(ps_p[:, 0, c * S + t * P:c * S + (t + 1) * P],
                                                     on[:, t, c * P:(c + 1) * P], ident[:])
                    mm.then_inc(ot_done, 1)

                def out():
                    pe.wait_ge(ot_used, b + 1)
                    if isinstance(b, int) and b == B - 1:
                        pe.wait_ge(v_used, B)
                    else:
                        pe.wait_ge(v_used, b + 2)
                    if isinstance(b, int) is False or b > 0:
                        wait(pe, y_used, b)
                    for t in range(TT):
                        for c in range(DC):
                            mm = nc.tensor.matmul(ps_p[:, 1, t * D:(t + 1) * D], onT[:, c, t * P:(t + 1) * P],
                                                  w["wo"][:, c, :], start=(c == 0), stop=(c == DC - 1))
                    mm.then_inc(y_done, 1)
                return [transposes, out]

            def heads(b, par, parts):
                def scores(h):
                    if h == 0:
                        pe.wait_ge(proj_used, NPROJ * (b + 1))
                    wait(pe, p_ready, HEADS * b + h - 1)
                    j, g = h // 4, h % 4
                    rows = slice(SLOT * g, SLOT * g + HD)
                    for q in range(TT):
                        c0, n = span[q]
                        mm = nc.tensor.matmul(ps_s[:, h % 2, c0:c0 + n], qT[rows, par, j, q * P:(q + 1) * P],
                                              kT[rows, par, j, 0:n], start=True, stop=not rope)
                        if rope:
                            mm = nc.tensor.matmul(ps_s[:, h % 2, col[q, q]:col[q, q] + P], ident16[:], mask[:],
                                                  start=False, stop=True)
                    mm.then_inc(s_done, 1)

                def turn(h):
                    pe.wait_ge(p_ready, HEADS * b + h + 1)
                    wait(pe, pt_used, HEADS * b + h - 1)
                    for n in range(len(blocks)):
                        mm = nc.tensor.transpose(ps_t[0:KN, h % 2, n * P:(n + 1) * P],
                                                 prob[:, h % 2, n * KN:(n + 1) * KN], ident[:])
                    mm.then_inc(pt_done, 1)

                def weigh(h):
                    if h == 0:
                        pe.wait_ge(v_used, b + 1)
                        wait(pe, o_used, b)
                    pe.wait_ge(pt_used, HEADS * b + h + 1)
                    for q in range(TT):
                        mine = [n for n, blk in enumerate(blocks) if blk[0] == q]
                        for n in mine:
                            mm = nc.tensor.matmul(ps_o[:, q, h * (HD + 1):(h + 1) * (HD + 1)],
                                                  probT[0:KN, h % 2, n, :], va[0:KN, par, blocks[n][1], h, :],
                                                  start=(n == mine[0]), stop=(n == mine[-1]))
                    mm.then_inc(pv_done, 1)

                for s in range(HEADS + 2):
                    if s < HEADS:
                        scores(s)
                    if s < len(parts):
                        parts[s]()
                    if s >= 2:
                        weigh(s - 2)
                    if 1 <= s <= HEADS:
                        turn(s - 1)

            run(pe, prologue, heads, epilogue)

        @block.scalar
        def _(act):
            act.wait_ge(weights, 16 * nload)
            act.wait_ge(ready, 1)
            nc.scalar.activation(warm[:], ident[:, 0:1], ACT.Exp)

            def prologue(b, par):
                def transposes():
                    act.wait_ge(xt_done, (2 if cross else 1) * b + 1)
                    nc.scalar.activation(xnT[:].rearrange("p c s -> p (c s)"), ps_p[:, 0, :], ACT.Copy).then_inc(xt_used, 1)
                    if cross:
                        act.wait_ge(xt_done, 2 * b + 2)
                        nc.scalar.activation(ctxT[:].rearrange("p c s -> p (c s)"), ps_p[:, 1, 0:DC * CTX],
                                             ACT.Copy).then_inc(xt_used, 1)

                def project(j):
                    def go():
                        if rope:
                            return
                        if j == 0:
                            wait(act, s_done, HEADS * (b - 1))
                        act.wait_ge(proj_done, NPROJ * b + j + 1)
                        isq, quad = j < QUADS, j % QUADS
                        n = S if isq else KS
                        dst = (qT if isq else kT)[:, par, quad, :]
                        nc.scalar.activation(dst, ps_p[:, (j + 1) % 2, 0:n], ACT.Identity,
                                             bias=(bq if isq else bk)[:, quad:quad + 1],
                                             scale=0.25 if isq else 1.0).then_inc(proj_used, 1)
                    return go

                def values():
                    if not rope:
                        return
                    act.wait_ge(v_done, b + 1)
                    wait(act, pv_done, HEADS * (b - 1))
                    for k in range(KT):
                        ins = nc.scalar.activation(va[:, par, k, :, 0:HD],
                                                   ps_p[:, 1, k * D:(k + 1) * D].rearrange("p (h e) -> p h e", h=HEADS),
                                                   ACT.Copy)
                    ins.then_inc(v_used, 1)
                return [transposes] + [project(j) for j in range(NPROJ)] + [values]

            def epilogue(b, par):
                def transposes():
                    act.wait_ge(ot_done, b + 1)
                    nc.scalar.activation(onT[:].rearrange("p c s -> p (c s)"), ps_p[:, 0, :], ACT.Copy).then_inc(ot_used, 1)
                return [transposes, lambda: None]

            def heads(b, par, parts):
                def exps(h):
                    act.wait_ge(nmax_ready, HEADS * b + h + 1)
                    wait(act, pt_done, HEADS * b + h - 1)
                    for q in range(TT):
                        c0, n = span[q]
                        ins = nc.scalar.activation(prob[:, h % 2, c0:c0 + n], ps_s[:, h % 2, c0:c0 + n], ACT.Exp,
                                                   bias=nmax[:, h % 2, q:q + 1])
                    ins.then_inc(p_ready, 1)

                for s in range(HEADS + 2):
                    if s < HEADS:
                        exps(s)
                    if s < len(parts):
                        parts[s]()

            run(act, prologue, heads, epilogue)

        @block.vector
        def _(dve):
            dve.wait_ge(weights, 16 * nload)
            steps = Steps(dve, step)
            if rope:
                steps.link(nc.vector.tensor_copy(ident16[:], ident[:]))
                steps.link(nc.vector.tensor_copy(mask[:], maskf[:]))
            else:
                if kind == "band":
                    steps.link(nc.vector.tensor_tensor(bq[:], bq[:], bias2[:], ALU.add))
                steps.link(nc.vector.tensor_scalar(bq[:], bq[:], 0.25, None, ALU.mult))
            nc.vector.memset(va[:], 1.0).then_inc(ready, 1)
            dve.wait_ge(ready, 1)
            steps.again()

            def prologue(b, par):
                def transposes():
                    wait(dve, xt_done, (2 if cross else 1) * b)
                    for t in range(TT):
                        ins = nc.vector.tensor_scalar(xn[:, t, :], x_all[:, b * TT + t, :], mean[:, b * TT + t, :],
                                                      rstd[:, b * TT + t, :], ALU.subtract, ALU.mult)
                    ins.then_inc(xn_ready, 1)

                def project(j):
                    def go():
                        if not rope:
                            return
                        if j == 0:
                            wait(dve, s_done, HEADS * (b - 1))
                        dve.wait_ge(proj_done, NPROJ * b + j + 1)
                        isq, quad = j < QUADS, j % QUADS
                        bank = ps_p[:, (j + 1) % 2, :]
                        cs, sn = ("cosq", "sinq") if isq else ("cosk", "sink")
                        wait(dve, proj_used, NPROJ * b + j - 1)
                        nc.vector.tensor_tensor(rot[:, j % 2, 0, :], bank[:, 0:S], tab[cs][:], ALU.mult)
                        steps.link(nc.vector.tensor_tensor(rot[:, j % 2, 1, :], bank[:, S:2 * S], tab[sn][:], ALU.mult))
                        nc.vector.tensor_tensor((qT if isq else kT)[:, par, quad, :], rot[:, j % 2, 0, :], rot[:, j % 2, 1, :],
                                                ALU.add).then_inc(proj_used, 1)
                    return go

                def values():
                    if rope:
                        return
                    dve.wait_ge(v_done, b + 1)
                    wait(dve, pv_done, HEADS * (b - 1))
                    for k in range(KT):
                        ins = nc.vector.tensor_tensor(
                            va[0:KN, par, k, :, 0:HD],
                            ps_p[0:KN, 1, k * D:(k + 1) * D].rearrange("p (h e) -> p h e", h=HEADS),
                            bv[0:KN, :].rearrange("p (h e) -> p h e", h=HEADS), ALU.add)
                    ins.then_inc(v_used, 1)
                return [transposes] + [project(j) for j in range(NPROJ)] + [values]

            def epilogue(b, par):
                def out():
                    dve.wait_ge(y_done, b + 1)
                    wait(dve, y_used, b)
                    for t in range(TT):
                        src = ps_p[:, 1, t * D:(t + 1) * D]
                        if not rope:
                            steps.link(nc.vector.tensor_tensor(ytmp[:, t, :], src, bo[:], ALU.add))
                            src = ytmp[:, t, :]
                        xt = x_all[:, b * TT + t, :]
                        ins = nc.vector.tensor_tensor(xt, src, xt, ALU.add)
                    ins.then_inc(y_used, 1)
                return [lambda: None, out]

            def heads(b, par, parts):
                def rowmax(h):
                    dve.wait_ge(s_done, HEADS * b + h + 1)
                    if kind == "causal":
                        for q in range(TT):
                            c0, n = span[q]
                            ins = nc.vector.tensor_reduce(nmax[:, h % 2, q:q + 1], ps_s[:, h % 2, c0:c0 + n],
                                                          AX.X, ALU.max, negate=True)
                    else:
                        ins = nc.vector.tensor_reduce(nmax[:, h % 2, :],
                                                      ps_s[:, h % 2, 0:COLS].rearrange("p (q k) -> p q k", q=TT),
                                                      AX.X, ALU.max, negate=True)
                    ins.then_inc(nmax_ready, 1)

                def take(h):
                    dve.wait_ge(pt_done, HEADS * b + h + 1)
                    wait(dve, pv_done, HEADS * b + h - 1)
                    src = ps_t[0:KN, h % 2, 0:len(blocks) * P]
                    dst = probT[0:KN, h % 2, :, :].rearrange("p n q -> p (n q)")
                    if kind == "band":
                        for q in range(TT):
                            ins = nc.vector.tensor_tensor(
                                probT[:, h % 2, q * KT:(q + 1) * KT, :],
                                src[:, q * KT * P:(q + 1) * KT * P].rearrange("p (k q) -> p k q", k=KT),
                                band[:, :, q * P:(q + 1) * P], ALU.mult)
                    else:
                        ins = nc.vector.tensor_copy(dst, src)
                    ins.then_inc(pt_used, 1)

                for s in range(HEADS + 1):
                    if s < HEADS:
                        rowmax(s)
                    if s < len(parts):
                        parts[s]()
                    if s >= 1:
                        take(s - 1)
                dve.wait_ge(pv_done, HEADS * (b + 1))
                acc = ps_o[:, :, 0:HEADS * (HD + 1)].rearrange("p t (h e) -> p t h e", h=HEADS)
                wait(dve, o_used, b)
                steps.link(nc.vector.reciprocal(rsum[:], acc[:, :, :, HD]))
                steps.again()
                wait(dve, ot_done, b)
                for t in range(TT):
                    ins = nc.vector.tensor_tensor(on[:, t, :].rearrange("p (h e) -> p h e", h=HEADS), acc[:, t, :, 0:HD],
                                                  rsum[:, t, :].unsqueeze(2).broadcast_to((P, HEADS, HD)), ALU.mult)
                ins.then_inc(o_used, 1)

            run(dve, prologue, heads, epilogue)


NQ = 8
HALF = 32
KEYS = 64
TOP = 10
EXPERTS = KEYS * KEYS
EV = 32
CHUNK = 16
NCH = P // CHUNK
PAIRS = [TOP // (a + 1) for a in range(TOP)]
NPAIR = sum(PAIRS)
LOW = -3.0e38


def peer_stage(nc, x_all, mean, rstd, ident, d):
    with ExitStack() as ctx:
        r = Room(nc, ctx, "peer")
        sb, ps, sem = r.sb, r.ps, r.sem
        SEL = NQ * TOP
        wq = sb("wq", [P, DC, 2 * NQ * HALF])
        bq = sb("bq", [P, 4])
        keys = sb("keys", [P, 4 * KEYS])
        down = sb("down", [P, DC, EV, P])
        up = sb("up", [P, EV, D])
        iota = sb("iota", [P, P])
        xn = sb("xn", [P, D])
        xnT = sb("xnT", [P, 2, DC, P])
        qT = sb("qT", [P, 4, P])
        s = sb("s", [P, 2 * NQ, KEYS])
        s2 = sb("s2", [P, 2 * NQ, KEYS])
        best = sb("best", [P, 2 * NQ, 16])
        besti = sb("besti", [P, 2 * NQ, 16], U32)
        i64 = sb("i64", [P, NQ, TOP])
        cand = sb("cand", [P, NQ, NPAIR])
        cand2 = sb("cand2", [P, NQ, NPAIR])
        code = sb("code", [P, NQ, NPAIR])
        tv = sb("tv", [P, NQ, 16])
        tp = sb("tp", [P, NQ, 16], U32)
        tpf = sb("tpf", [P, NQ, 16])
        eq = sb("eq", [P, NQ, TOP, NPAIR])
        ef = sb("ef", [P, SEL])
        ei = sb("ei", [P, SEL], I32)
        uvi = sb("uvi", [P, 2, SEL], I32)
        ew = sb("ew", [P, NQ, TOP])
        es = sb("es", [P, NQ, 1])
        er = sb("er", [P, NQ, 1])
        uvw = sb("uvw", [P, 3, SEL])
        uvT = sb("uvT", [P, 2, P], BF16)
        wT = sb("wT", [P, P])
        rest = sb("rest", [P, 2, P])
        parts = sb("parts", [P, 3, P], BF16)
        count = sb("count", [P, P, CHUNK], BF16)
        hot_u = sb("hot_u", [P, 2, P, CHUNK], BF16)
        hot_e = sb("hot_e", [P, 2, EV, CHUNK], BF16)
        hot_v = sb("hot_v", [P, 2, 3, EV, CHUNK], BF16)
        g = sb("g", [P, 2, EV, P])
        warm = sb("warm", [P, 1])

        ps_q = ps("ps_q", [P, 512])
        ps_s = ps("ps_s", [P, 2, 512])
        ps_h = ps("ps_h", [P, 2, 512])
        ps_w = ps("ps_w", [P, 2, 512])
        ps_u = ps("ps_u", [P, D])

        loaded = sem("loaded")
        xn_ready = sem("xn_ready")
        xt_done = sem("xt_done")
        xt_used = sem("xt_used")
        q_done = sem("q_done")
        q_used = sem("q_used")
        s_done = sem("s_done")
        s_used = sem("s_used")
        halves_done = sem("halves_done")
        exp_in = sem("exp_in")
        exp_out = sem("exp_out")
        sel_in = sem("sel_in")
        sel_out = sem("sel_out")
        uvw_ready = sem("uvw_ready")
        uvw_done = sem("uvw_done")
        uvw_used = sem("uvw_used")
        h_done = sem("h_done")
        g_ready = sem("g_ready")
        u_ready = sem("u_ready")
        e_ready = sem("e_ready")
        v_ready = sem("v_ready")
        w_done = sem("w_done")
        gw_ready = sem("gw_ready")
        up_done = sem("up_done")
        x_used = sem("x_used")
        step = sem("step")
        pstep = sem("pstep")
        block = ctx.enter_context(nc.Block())
        NLOAD = 6

        @block.sync
        def _(sp):
            for dst, name in ((wq, "peer_wq"), (down, "peer_down")):
                pat = "(c p) n -> p c n" if name == "peer_wq" else "(c p) v u -> p c v u"
                sp.dma_start(dst[:], d[name].rearrange(pat, p=P)).then_inc(loaded, 16)
            for dst, name in ((bq, "peer_bq"), (keys, "peer_keys"), (up, "peer_up"), (iota, "iota")):
                sp.dma_start(dst[:], d[name]).then_inc(loaded, 16)
            sp.wait_ge(loaded, 16 * NLOAD)

        def run(eng, first, macro):
            first()
            macro(0, 0, False)
            with eng.Fori(0, TILES // 2 - 1) as i:
                macro(2 * i + 1, 1, False)
                macro(2 * i + 2, 0, False)
            macro(TILES - 1, 1, True)

        @block.tensor
        def _(pe):
            pe.wait_ge(loaded, 16 * NLOAD)

            def turn_x(t):
                pe.wait_ge(xn_ready, t + 1)
                wait(pe, uvw_used, t)
                for c in range(DC):
                    mm = nc.tensor.transpose(ps_q[:, c * P:(c + 1) * P], xn[:, c * P:(c + 1) * P], ident[:])
                mm.then_inc(xt_done, 1)

            def queries(t, par):
                pe.wait_ge(xt_used, t + 1)
                for k in range(4):
                    for c in range(DC):
                        mm = nc.tensor.matmul(ps_q[:, k * P:(k + 1) * P], wq[:, c, k * P:(k + 1) * P],
                                              xnT[:, par, c, :], start=(c == 0), stop=(c == DC - 1))
                mm.then_inc(q_done, 1)

            def scores(t):
                pe.wait_ge(q_used, t + 1)
                wait(pe, s_used, t)
                for k in range(4):
                    mm = nc.tensor.matmul(ps_s[:, k // 2, (k % 2) * 256:(k % 2 + 1) * 256], qT[:, k, :], keys[:],
                                          start=True, stop=True)
                mm.then_inc(s_done, 1)

            def hidden(t, par, n):
                pe.wait_ge(xt_used, t + 1)
                wait(pe, g_ready, NCH * t + n - 1)
                for k in range(4):
                    for c in range(DC):
                        mm = nc.tensor.matmul(ps_h[:, n % 2, k * P:(k + 1) * P], down[:, c, 4 * n + k, :],
                                              xnT[:, par, c, :], start=(c == 0), stop=(c == DC - 1))
                mm.then_inc(h_done, 1)

            def weights(t, n):
                pe.wait_ge(u_ready, NCH * t + n + 1)
                pe.wait_ge(v_ready, NCH * t + n + 1)
                wait(pe, gw_ready, NCH * t + n - 1)
                for k in range(CHUNK):
                    for part in range(3):
                        mm = nc.tensor.matmul(ps_w[:, n % 2, k * EV:(k + 1) * EV], hot_u[0:SEL, n % 2, :, k],
                                              hot_v[0:SEL, n % 2, part, :, k], start=(part == 0), stop=(part == 2))
                mm.then_inc(w_done, 1)

            def output(t, par, a, b):
                if a == 0:
                    pe.wait_ge(gw_ready, NCH * (t + 1))
                    wait(pe, x_used, t)
                for v in range(a, b):
                    mm = nc.tensor.matmul(ps_u[:], g[:, par, v, :], up[:, v, :], start=(v == 0), stop=(v == EV - 1))
                if b == EV:
                    mm.then_inc(up_done, 1)

            def turn_uvw(t):
                pe.wait_ge(uvw_ready, t + 1)
                pe.wait_ge(q_used, t + 1)
                for k in range(3):
                    mm = nc.tensor.transpose(ps_q[0:SEL, k * P:(k + 1) * P], uvw[:, k, :], ident[:])
                mm.then_inc(uvw_done, 1)

            def first():
                turn_x(0)
                queries(0, 0)
                scores(0)
                for n in range(NCH):
                    hidden(0, 0, n)
                turn_uvw(0)

            def macro(t, par, last):
                for n in range(NCH):
                    if not last:
                        if n == 0:
                            turn_x(t + 1)
                        if n == 1:
                            queries(t + 1, 1 - par)
                        if n == 2:
                            scores(t + 1)
                        if n >= 2:
                            hidden(t + 1, 1 - par, n - 2)
                    weights(t, n)
                if not last:
                    hidden(t + 1, 1 - par, NCH - 2)
                    hidden(t + 1, 1 - par, NCH - 1)
                output(t, par, 0, 20)
                if not last:
                    turn_uvw(t + 1)
                output(t, par, 20, EV)

            run(pe, first, macro)

        @block.scalar
        def _(act):
            act.wait_ge(loaded, 16 * NLOAD)

            def take_x(t, par):
                act.wait_ge(xt_done, t + 1)
                nc.scalar.activation(xnT[:, par, :, :].rearrange("p c s -> p (c s)"), ps_q[:, 0:DC * P],
                                     ACT.Copy).then_inc(xt_used, 1)

            def take_q(t):
                act.wait_ge(q_done, t + 1)
                for k in range(4):
                    ins = nc.scalar.activation(qT[:, k, :], ps_q[:, k * P:(k + 1) * P], ACT.Identity, bias=bq[:, k:k + 1])
                ins.then_inc(q_used, 1)

            def take_s(t):
                act.wait_ge(s_done, t + 1)
                wait(act, halves_done, t)
                nc.scalar.activation(s[:].rearrange("p g k -> p (g k)"), ps_s[:].rearrange("p a k -> p (a k)"),
                                     ACT.Copy).then_inc(s_used, 1)

            def gelu(t, par, n):
                act.wait_ge(h_done, NCH * t + n + 1)
                wait(act, up_done, t - 1)
                nc.scalar.activation(g[:, par, 4 * n:4 * n + 4, :].rearrange("p v s -> p (v s)"), ps_h[:, n % 2, :],
                                     ACT.Gelu).then_inc(g_ready, 1)

            def exps(t):
                act.wait_ge(exp_in, t + 1)
                nc.scalar.activation(ew[:], ew[:], ACT.Exp).then_inc(exp_out, 1)

            def take_uvw(t):
                act.wait_ge(uvw_done, t + 1)
                wait(act, u_ready, NCH * t)
                wait(act, v_ready, NCH * t)
                nc.scalar.activation(uvT[0:SEL, :, :].rearrange("p k s -> p (k s)"), ps_q[0:SEL, 0:2 * P], ACT.Copy)
                nc.scalar.activation(parts[0:SEL, 0, :], ps_q[0:SEL, 2 * P:3 * P], ACT.Copy)
                nc.scalar.activation(wT[0:SEL, :], ps_q[0:SEL, 2 * P:3 * P], ACT.Copy).then_inc(uvw_used, 1)

            def choices(t, par):
                take_x(t, par)
                take_q(t)
                take_s(t)
                for n in range(NCH):
                    gelu(t, par, n)
                exps(t)
                take_uvw(t)

            def macro(t, par, last):
                if not last:
                    choices(t + 1, 1 - par)

            run(act, lambda: choices(0, 0), macro)

        @block.gpsimd
        def _(pool):
            pool.wait_ge(loaded, 16 * NLOAD)
            steps = Steps(pool, pstep)

            def split(t):
                pool.wait_ge(uvw_used, t + 1)
                steps.link(nc.gpsimd.tensor_tensor(rest[0:SEL, 0, :], wT[0:SEL, :], parts[0:SEL, 0, :], ALU.subtract))
                steps.link(nc.gpsimd.tensor_copy(parts[0:SEL, 1, :], rest[0:SEL, 0, :]))
                steps.link(nc.gpsimd.tensor_tensor(rest[0:SEL, 1, :], rest[0:SEL, 0, :], parts[0:SEL, 1, :], ALU.subtract))
                steps.link(nc.gpsimd.tensor_copy(parts[0:SEL, 2, :], rest[0:SEL, 1, :]))

            def hots(t, n):
                if n == 0:
                    split(t)
                pool.wait_ge(e_ready, NCH * t + n + 1)
                wait(pool, w_done, NCH * t + n - 1)
                for part in range(3):
                    w = parts[0:SEL, part, n * CHUNK:(n + 1) * CHUNK].unsqueeze(1).broadcast_to((SEL, EV, CHUNK))
                    ins = nc.gpsimd.tensor_tensor(hot_v[0:SEL, n % 2, part, :, :], hot_e[0:SEL, n % 2, :, :], w, ALU.mult)
                ins.then_inc(v_ready, 1)

            def select(t):
                pool.wait_ge(sel_in, t + 1)
                value = code[:].unsqueeze(2).broadcast_to((P, NQ, TOP, NPAIR))
                nc.gpsimd.tensor_tensor(eq[:], eq[:], value, ALU.mult).then_inc(sel_out, 1)
                steps.again()

            def first():
                select(0)
                hots(0, 0)

            def macro(t, par, last):
                for n in range(1, NCH):
                    hots(t, n)
                if not last:
                    select(t + 1)
                    hots(t + 1, 0)

            run(pool, first, macro)

        @block.vector
        def _(dve):
            dve.wait_ge(loaded, 16 * NLOAD)
            steps = Steps(dve, step)
            steps.link(nc.vector.tensor_copy(count[:], iota[:].unsqueeze(2).broadcast_to((P, P, CHUNK))))
            steps.again()

            def norm(t):
                wait(dve, xt_done, t)
                nc.vector.tensor_scalar(xn[:], x_all[:, t, :], mean[:, t, :], rstd[:, t, :], ALU.subtract,
                                        ALU.mult).then_inc(xn_ready, 1)

            def hots(t, n):
                if n == 0:
                    dve.wait_ge(uvw_used, t + 1)
                wait(dve, v_ready, NCH * t + n - 1)
                vt = uvT[0:SEL, 1, n * CHUNK:(n + 1) * CHUNK].unsqueeze(1).broadcast_to((SEL, EV, CHUNK))
                nc.vector.tensor_tensor(hot_e[0:SEL, n % 2, :, :], count[0:SEL, 0:EV, :], vt,
                                        ALU.is_equal).then_inc(e_ready, 1)
                wait(dve, w_done, NCH * t + n - 1)
                ut = uvT[0:SEL, 0, n * CHUNK:(n + 1) * CHUNK].unsqueeze(1).broadcast_to((SEL, P, CHUNK))
                nc.vector.tensor_tensor(hot_u[0:SEL, n % 2, :, :], count[0:SEL, :, :], ut,
                                        ALU.is_equal).then_inc(u_ready, 1)

            def weigh(t, par, n):
                if n == 0:
                    dve.wait_ge(g_ready, NCH * (t + 1))
                dve.wait_ge(w_done, NCH * t + n + 1)
                gs = g[:, par, :, n * CHUNK:(n + 1) * CHUNK]
                nc.vector.tensor_tensor(gs, ps_w[:, n % 2, :].rearrange("p (k v) -> p v k", v=EV), gs,
                                        ALU.mult).then_inc(gw_ready, 1)

            def halves(t, a, b):
                gr = range(a, b)
                if a == 0:
                    dve.wait_ge(s_used, t + 1)
                    steps.link(nc.vector.memset(tv[:], 0.0))
                for q in gr:
                    ins = nc.vector.max(best[:, q, 0:8], s[:, q, :])
                steps.link(ins)
                for q in gr:
                    nc.vector.max_index(besti[:, q, 0:8], best[:, q, 0:8], s[:, q, :])
                for q in gr:
                    ins = nc.vector.match_replace(s2[:, q, :], best[:, q, 0:8], s[:, q, :], LOW)
                steps.link(ins)
                for q in gr:
                    ins = nc.vector.max(best[:, q, 8:16], s2[:, q, :])
                steps.link(ins)
                for q in gr:
                    ins = nc.vector.max_index(besti[:, q, 8:16], best[:, q, 8:16], s2[:, q, :])
                steps.link(ins)
                if b == 2 * NQ:
                    nc.vector.tensor_scalar(i64[:], besti[:, 0:2 * NQ:2, 0:TOP], float(KEYS), None,
                                            ALU.mult).then_inc(halves_done, 1)

            def pairs(dst, first, second):
                off = 0
                a = 0
                while a < TOP:
                    nb = PAIRS[a]
                    na = sum(x == nb for x in PAIRS)
                    ins = nc.vector.tensor_tensor(
                        dst[:, :, off:off + na * nb].rearrange("p h (a b) -> p h a b", b=nb),
                        first[:, :, a:a + na].unsqueeze(3).broadcast_to((P, NQ, na, nb)),
                        second[:, :, 0:nb].unsqueeze(2).broadcast_to((P, NQ, na, nb)), ALU.add)
                    off += na * nb
                    a += na
                return ins

            def choose_a(t):
                dve.wait_ge(halves_done, t + 1)
                wait(dve, sel_out, t)
                pairs(cand, best[:, 0:2 * NQ:2, :], best[:, 1:2 * NQ:2, :])
                steps.link(pairs(code, i64[:], besti[:, 1:2 * NQ:2, :]))
                for h in range(NQ):
                    ins = nc.vector.max(tv[:, h, 0:8], cand[:, h, :])
                steps.link(ins)
                for h in range(NQ):
                    nc.vector.max_index(tp[:, h, 0:8], tv[:, h, 0:8], cand[:, h, :])
                for h in range(NQ):
                    ins = nc.vector.match_replace(cand2[:, h, :], tv[:, h, 0:8], cand[:, h, :], LOW)
                steps.link(ins)
                for h in range(NQ):
                    ins = nc.vector.max(tv[:, h, 8:16], cand2[:, h, :])
                steps.link(ins)
                for h in range(NQ):
                    ins = nc.vector.max_index(tp[:, h, 8:16], tv[:, h, 8:16], cand2[:, h, :])
                steps.link(ins)
                steps.link(nc.vector.tensor_copy(tpf[:], tp[:]))
                where = tpf[:, :, 0:TOP].unsqueeze(3).broadcast_to((P, NQ, TOP, NPAIR))
                number = iota[:, 0:NPAIR].unsqueeze(1).unsqueeze(1).broadcast_to((P, NQ, TOP, NPAIR))
                nc.vector.tensor_tensor(eq[:], number, where, ALU.is_equal).then_inc(sel_in, 1)
                nc.vector.tensor_tensor(ew[:], tv[:, :, 0:TOP], tv[:, :, 0:1].broadcast_to((P, NQ, TOP)),
                                        ALU.subtract).then_inc(exp_in, 1)

            def choose_b(t):
                dve.wait_ge(exp_out, t + 1)
                wait(dve, uvw_done, t)
                steps.link(nc.vector.tensor_reduce(es[:], ew[:], AX.X, ALU.add))
                steps.link(nc.vector.reciprocal(er[:], es[:]))
                nc.vector.tensor_tensor(uvw[:, 2, :].rearrange("p (h k) -> p h k", h=NQ), ew[:],
                                        er[:].broadcast_to((P, NQ, TOP)), ALU.mult)
                dve.wait_ge(sel_out, t + 1)
                steps.link(nc.vector.tensor_reduce(ef[:].rearrange("p (h k) -> p h k", h=NQ), eq[:], AX.X, ALU.add))
                steps.link(nc.vector.tensor_copy(ei[:], ef[:]))
                nc.vector.tensor_scalar(uvi[:, 0, :], ei[:], 5, None, ALU.logical_shift_right)
                steps.link(nc.vector.tensor_scalar(uvi[:, 1, :], ei[:], EV - 1, None, ALU.bitwise_and))
                nc.vector.tensor_copy(uvw[:, 0:2, :], uvi[:]).then_inc(uvw_ready, 1)
                dve.wait_ge(uvw_ready, t + 1)

            def add(t):
                dve.wait_ge(up_done, t + 1)
                nc.vector.tensor_tensor(x_all[:, t, :], ps_u[:], x_all[:, t, :], ALU.add).then_inc(x_used, 1)

            def first():
                norm(0)
                for a in range(0, 2 * NQ, 4):
                    halves(0, a, a + 4)
                choose_a(0)
                choose_b(0)
                hots(0, 0)
                steps.again()

            def macro(t, par, last):
                if not last:
                    norm(t + 1)
                if not (isinstance(t, int) and t == 0):
                    add(t - 1)
                for n in range(NCH):
                    if n < NCH - 1:
                        hots(t, n + 1)
                    if n >= 1:
                        weigh(t, par, n - 1)
                    if n >= 3 and not last:
                        halves(t + 1, 3 * (n - 3), 3 * (n - 2))
                weigh(t, par, NCH - 1)
                if not last:
                    halves(t + 1, 15, 16)
                    choose_a(t + 1)
                    choose_b(t + 1)
                    hots(t + 1, 0)
                if last:
                    add(t)
                steps.again()

            run(dve, first, macro)


def bidaf_stage(nc, x_all, mean, rstd, ident, d):
    with ExitStack() as ctx:
        r = Room(nc, ctx, "bidaf")
        NS = 2
        wl = r.sb("wl", [P, 4 * DC, D])
        bl = r.sb("bl", [P, D])
        vec = r.sb("vec", [P, 3, DC])
        b3 = r.sb("b3", [1, 3])
        bsum = r.sb("bsum", [1, 1])
        ones = r.sb("ones", [1, P])
        warm = r.sb("warm", [P, 1])
        loaded = r.sem("loaded")
        ready = r.sem("ready")
        step = r.sem("step")
        astep = r.sem("astep")


        class Stream:
            def __init__(self, k):
                self.k = k
                self.q = r.sb(f"q{k}", [P, D])
                self.c = r.sb(f"c{k}", [P, TT, D])
                self.cT = r.sb(f"cT{k}", [P, DC, S])
                self.qT = r.sb(f"qT{k}", [P, DC, CTX])
                self.m = r.sb(f"m{k}", [P, DC, CTX])
                self.qrow = r.sb(f"qrow{k}", [1, CTX])
                self.nmax = r.sb(f"nmax{k}", [P, TT])
                self.prob = r.sb(f"prob{k}", [P, TT, CTX])
                self.rs = r.sb(f"rs{k}", [P, TT])
                self.ri = r.sb(f"ri{k}", [P, TT])
                self.probT = r.sb(f"probT{k}", [P, S])
                self.negtop = r.sb(f"negtop{k}", [1, 1])
                self.erow = r.sb(f"erow{k}", [1, S])
                self.es = r.sb(f"es{k}", [1, 1])
                self.ei = r.sb(f"ei{k}", [1, 1])
                self.arow = r.sb(f"arow{k}", [1, S])
                self.acol = r.sb(f"acol{k}", [P, TT])
                self.q2c = r.sb(f"q2c{k}", [P, DC])
                self.wad = r.sb(f"wad{k}", [P, DC, D])
                self.aT = r.sb(f"aT{k}", [P, DC, S])
                self.caT = r.sb(f"caT{k}", [P, DC, S])
                self.z = r.sb(f"z{k}", [P, TT, D])
                self.p0 = r.ps(f"p0{k}", [P, 512])
                self.p1 = r.ps(f"p1{k}", [P, 512])
                self.p2 = r.ps(f"p2{k}", [P, 512])
                self.p3 = r.ps(f"p3{k}", [P, 512])
                self.q_in = r.sem(f"q_in{k}")
                self.c_ready = r.sem(f"c_ready{k}")
                self.t_done = r.sem(f"t_done{k}")
                self.t_used = r.sem(f"t_used{k}")
                self.m_ready = r.sem(f"m_ready{k}")
                self.row_done = r.sem(f"row_done{k}")
                self.row_ready = r.sem(f"row_ready{k}")
                self.s_done = r.sem(f"s_done{k}")
                self.max_ready = r.sem(f"max_ready{k}")
                self.exp_ready = r.sem(f"exp_ready{k}")
                self.prob_ready = r.sem(f"prob_ready{k}")
                self.top_done = r.sem(f"top_done{k}")
                self.top_ready = r.sem(f"top_ready{k}")
                self.eexp_ready = r.sem(f"eexp_ready{k}")
                self.arow_ready = r.sem(f"arow_ready{k}")
                self.acol_done = r.sem(f"acol_done{k}")
                self.acol_ready = r.sem(f"acol_ready{k}")
                self.q2c_done = r.sem(f"q2c_done{k}")
                self.wad_ready = r.sem(f"wad_ready{k}")
                self.pt_done = r.sem(f"pt_done{k}")
                self.pt_used = r.sem(f"pt_used{k}")
                self.a_done = r.sem(f"a_done{k}")
                self.a_used = r.sem(f"a_used{k}")
                self.ca_ready = r.sem(f"ca_ready{k}")
                self.z_done = r.sem(f"z_done{k}")
                self.z_used = r.sem(f"z_used{k}")

        streams = [Stream(k) for k in range(NS)]
        block = ctx.enter_context(nc.Block())
        NLOAD = 4

        def each(eng, parts):
            def pair(n):
                for part in parts:
                    for z in streams:
                        part(z, n, NS * n + z.k)
            pair(0)
            with eng.Fori(1, B // NS) as n:
                pair(n)

        @block.sync
        def _(sp):
            sp.dma_start(wl[:], d["bidaf_wl"].rearrange("(c p) n -> p c n", p=P)).then_inc(loaded, 16)
            sp.dma_start(bl[:], d["bidaf_bl"].partition_broadcast(P)).then_inc(loaded, 16)
            sp.dma_start(vec[:], d["bidaf_vec"]).then_inc(loaded, 16)
            sp.dma_start(b3[:], d["bidaf_b"]).then_inc(loaded, 16)

            def fetch(z, n, b):
                wait(sp, z.a_done, n)
                sp.wait_ge(loaded, 16 * NLOAD)
                sp.dma_start(z.q[0:CTX, :], d["ctx"][b]).then_inc(z.q_in, 16)
            each(sp, [fetch])
            for z in streams:
                sp.wait_ge(z.q_in, 16 * (B // NS))

        @block.tensor
        def _(pe):
            pe.wait_ge(loaded, 16 * NLOAD)
            pe.wait_ge(ready, 1)

            def turn(z, n, b):
                pe.wait_ge(z.c_ready, n + 1)
                pe.wait_ge(z.q_in, 16 * (n + 1))
                wait(pe, z.a_used, n)
                wait(pe, z.acol_ready, n)
                for t in range(TT):
                    for c in range(DC):
                        nc.tensor.transpose(z.p0[:, c * S + t * P:c * S + (t + 1) * P], z.c[:, t, c * P:(c + 1) * P], ident[:])
                for c in range(DC):
                    mm = nc.tensor.transpose(z.p1[:, c * CTX:(c + 1) * CTX], z.q[0:CTX, c * P:(c + 1) * P],
                                             ident[0:CTX, 0:CTX])
                mm.then_inc(z.t_done, 1)

            def row(z, n, b):
                pe.wait_ge(z.t_used, n + 1)
                wait(pe, z.wad_ready, n)
                for c in range(DC):
                    mm = nc.tensor.matmul(z.p2[0:1, 0:CTX], vec[:, 2, c:c + 1], z.qT[:, c, :], start=(c == 0),
                                          stop=(c == DC - 1))
                mm.then_inc(z.row_done, 1)

            def scores(z, n, b):
                pe.wait_ge(z.row_ready, n + 1)
                pe.wait_ge(z.m_ready, n + 1)
                for t in range(TT):
                    for c in range(DC):
                        nc.tensor.matmul(z.p1[:, t * CTX:(t + 1) * CTX], z.cT[:, c, t * P:(t + 1) * P], z.m[:, c, :],
                                         start=(c == 0), stop=False)
                    mm = nc.tensor.matmul(z.p1[:, t * CTX:(t + 1) * CTX], ones[:], z.qrow[:], start=False, stop=True)
                mm.then_inc(z.s_done, 1)

            def top(z, n, b):
                pe.wait_ge(z.max_ready, n + 1)
                for t in range(TT):
                    mm = nc.tensor.matmul(z.p2[0:1, t * P:(t + 1) * P], z.nmax[:, t:t + 1], ident[:], start=True, stop=True)
                mm.then_inc(z.top_done, 1)

            def turn_prob(z, n, b):
                pe.wait_ge(z.prob_ready, n + 1)
                wait(pe, z.z_used, n)
                for t in range(TT):
                    mm = nc.tensor.transpose(z.p3[0:CTX, t * P:(t + 1) * P], z.prob[:, t, :], ident[:])
                mm.then_inc(z.pt_done, 1)

            def attend(z, n, b):
                pe.wait_ge(z.pt_used, n + 1)
                for c in range(DC):
                    mm = nc.tensor.matmul(z.p0[:, c * S:(c + 1) * S], z.q[0:CTX, c * P:(c + 1) * P], z.probT[0:CTX, :],
                                          start=True, stop=True)
                mm.then_inc(z.a_done, 1)

            def col(z, n, b):
                pe.wait_ge(z.arow_ready, n + 1)
                for t in range(TT):
                    mm = nc.tensor.matmul(z.p1[:, t:t + 1], z.arow[0:1, t * P:(t + 1) * P], ones[0:1, 0:1], start=True, stop=True)
                mm.then_inc(z.acol_done, 1)

            def q2c(z, n, b):
                pe.wait_ge(z.acol_ready, n + 1)
                for c in range(DC):
                    for t in range(TT):
                        mm = nc.tensor.matmul(z.p2[:, c:c + 1], z.c[:, t, c * P:(c + 1) * P], z.acol[:, t:t + 1],
                                              start=(t == 0), stop=(t == TT - 1))
                mm.then_inc(z.q2c_done, 1)

            def project(z, n, b):
                pe.wait_ge(z.wad_ready, n + 1)
                pe.wait_ge(z.a_used, n + 1)
                pe.wait_ge(z.ca_ready, n + 1)
                for t in range(TT):
                    ops = [(z.cT, z.wad, 0), (z.aT, wl, DC), (z.caT, wl, 2 * DC)]
                    for k, (lhs, w, off) in enumerate(ops):
                        for c in range(DC):
                            mm = nc.tensor.matmul(z.p3[:, t * D:(t + 1) * D], lhs[:, c, t * P:(t + 1) * P], w[:, off + c, :],
                                                  start=(k == 0 and c == 0), stop=(k == 2 and c == DC - 1))
                mm.then_inc(z.z_done, 1)

            each(pe, [turn, row, scores, top, turn_prob, attend, col, q2c, project])

        @block.scalar
        def _(act):
            act.wait_ge(loaded, 16 * NLOAD)
            act.wait_ge(ready, 1)
            nc.scalar.activation(warm[:], ident[:, 0:1], ACT.Exp)

            def take(z, n, b):
                act.wait_ge(z.t_done, n + 1)
                wait(act, z.z_done, n)
                nc.scalar.activation(z.cT[:].rearrange("p c s -> p (c s)"), z.p0[:], ACT.Copy)
                nc.scalar.activation(z.qT[:].rearrange("p c s -> p (c s)"), z.p1[:, 0:DC * CTX], ACT.Copy).then_inc(z.t_used, 1)

            def exps(z, n, b):
                act.wait_ge(z.max_ready, n + 1)
                for t in range(TT):
                    ins = nc.scalar.activation(z.prob[:, t, :], z.p1[:, t * CTX:(t + 1) * CTX], ACT.Exp,
                                               bias=z.nmax[:, t:t + 1], accum_out=z.rs[:, t:t + 1])
                ins.then_inc(z.exp_ready, 1)

            def eexp(z, n, b):
                act.wait_ge(z.top_ready, n + 1)
                nc.scalar.activation(z.erow[:], z.p2[0:1, 0:S], ACT.Exp, bias=z.negtop[:], scale=-1.0,
                                     accum_out=z.es[:]).then_inc(z.eexp_ready, 1)

            def take_prob(z, n, b):
                act.wait_ge(z.pt_done, n + 1)
                nc.scalar.activation(z.probT[0:CTX, :], z.p3[0:CTX, 0:S], ACT.Copy).then_inc(z.pt_used, 1)

            def take_a(z, n, b):
                act.wait_ge(z.a_done, n + 1)
                nc.scalar.activation(z.aT[:].rearrange("p c s -> p (c s)"), z.p0[:], ACT.Copy).then_inc(z.a_used, 1)

            each(act, [take, exps, eexp, take_prob, take_a])

        @block.vector
        def _(dve):
            dve.wait_ge(loaded, 16 * NLOAD)
            steps = Steps(dve, step)
            steps.link(nc.vector.tensor_reduce(bsum[:], b3[:], AX.X, ALU.add))
            nc.vector.memset(ones[:], 1.0).then_inc(ready, 1)
            dve.wait_ge(ready, 1)
            steps.again()

            def norm(z, n, b):
                wait(dve, z.q2c_done, n)
                for t in range(TT):
                    ins = nc.vector.tensor_scalar(z.c[:, t, :], x_all[:, b * TT + t, :], mean[:, b * TT + t, :],
                                                  rstd[:, b * TT + t, :], ALU.subtract, ALU.mult)
                ins.then_inc(z.c_ready, 1)

            def make_m(z, n, b):
                dve.wait_ge(z.t_used, n + 1)
                wait(dve, z.s_done, n)
                for c in range(DC):
                    ins = nc.vector.tensor_scalar(z.m[:, c, :], z.qT[:, c, :], vec[:, 0, c:c + 1],
                                                  vec[:, 1, c:c + 1], ALU.mult, ALU.add)
                ins.then_inc(z.m_ready, 1)

            def make_row(z, n, b):
                dve.wait_ge(z.row_done, n + 1)
                nc.vector.tensor_scalar(z.qrow[:], z.p2[0:1, 0:CTX], bsum[:], None, ALU.add).then_inc(z.row_ready, 1)

            def rowmax(z, n, b):
                dve.wait_ge(z.s_done, n + 1)
                nc.vector.tensor_reduce(z.nmax[:], z.p1[:, 0:TT * CTX].rearrange("p (t q) -> p t q", t=TT), AX.X,
                                        ALU.max, negate=True).then_inc(z.max_ready, 1)

            def find_top(z, n, b):
                dve.wait_ge(z.top_done, n + 1)
                nc.vector.tensor_reduce(z.negtop[:], z.p2[0:1, 0:S], AX.X, ALU.min).then_inc(z.top_ready, 1)

            def normalise(z, n, b):
                dve.wait_ge(z.exp_ready, n + 1)
                steps.link(nc.vector.reciprocal(z.ri[:], z.rs[:]))
                for t in range(TT):
                    ins = nc.vector.tensor_scalar(z.prob[:, t, :], z.prob[:, t, :], z.ri[:, t:t + 1], None, ALU.mult)
                ins.then_inc(z.prob_ready, 1)

            def batch_row(z, n, b):
                dve.wait_ge(z.eexp_ready, n + 1)
                steps.link(nc.vector.reciprocal(z.ei[:], z.es[:]))
                nc.vector.tensor_scalar(z.arow[:], z.erow[:], z.ei[:], None, ALU.mult).then_inc(z.arow_ready, 1)

            def take_col(z, n, b):
                dve.wait_ge(z.acol_done, n + 1)
                nc.vector.tensor_copy(z.acol[:], z.p1[:, 0:TT]).then_inc(z.acol_ready, 1)

            def make_wad(z, n, b):
                dve.wait_ge(z.q2c_done, n + 1)
                steps.link(nc.vector.tensor_copy(z.q2c[:], z.p2[:, 0:DC]))
                for c in range(DC):
                    ins = nc.vector.scalar_tensor_tensor(z.wad[:, c, :], wl[:, 3 * DC + c, :], z.q2c[:, c:c + 1],
                                                         wl[:, c, :], ALU.mult, ALU.add)
                ins.then_inc(z.wad_ready, 1)

            def product(z, n, b):
                dve.wait_ge(z.a_used, n + 1)
                nc.vector.tensor_tensor(z.caT[:], z.aT[:], z.cT[:], ALU.mult).then_inc(z.ca_ready, 1)

            def add(z, n, b):
                dve.wait_ge(z.z_done, n + 1)
                wait(dve, z.z_used, n)
                steps.link(nc.vector.tensor_tensor(z.z[:], z.p3[:].rearrange("p (t c) -> p t c", t=TT),
                                                   bl[:].unsqueeze(1).broadcast_to((P, TT, D)), ALU.add))
                for t in range(TT):
                    xt = x_all[:, b * TT + t, :]
                    ins = nc.vector.tensor_tensor(xt, z.z[:, t, :], xt, ALU.add)
                ins.then_inc(z.z_used, 1)
                if z.k == NS - 1:
                    steps.again()

            each(dve, [norm, make_m, make_row, rowmax, find_top, normalise, batch_row, product, take_col, make_wad, add])


E = 8
HID = 4 * D
HC = HID // P
GT = 4
YB = GT // 2


def moe_stage(nc, x_all, mean, rstd, ident, d):
    with ExitStack() as ctx:
        r = Room(nc, ctx, "moe")
        sb, ps, sem = r.sb, r.ps, r.sem
        w1 = sb("w1", [P, E, DC, HID])
        w2 = sb("w2", [P, E, HC, D])
        b1 = sb("b1", [P, E, HC])
        b2 = sb("b2", [E, D])
        wr = sb("wr", [P, DC, E])
        br = sb("br", [P, E])
        iota = sb("iota", [P, P])
        xn = sb("xn", [P, GT, D])
        xnT = sb("xnT", [P, DC, GT * P])
        hT = sb("hT", [P, HC, GT * P])
        logit = sb("logit", [P, GT, E])
        top = sb("top", [P, GT, 8])
        topi = sb("topi", [P, GT, 8], U32)
        topf = sb("topf", [P, GT, 8])
        hot = sb("hot", [P, GT, 2, E])
        ew = sb("ew", [P, GT, E])
        es = sb("es", [P, GT, 1])
        er = sb("er", [P, GT, 1])
        rw = sb("rw", [P, GT, E])
        rwT = sb("rwT", [E, GT, P])
        ps_t = ps("ps_t", [P, 2, 512])
        ps_h = ps("ps_h", [P, 2, 512])
        ps_y = ps("ps_y", [P, 4, D])
        ps_r = ps("ps_r", [P, 512])
        ps_b = ps("ps_b", [P, D])

        loaded = sem("loaded")
        loaded2 = sem("loaded2")
        xn_ready = sem("xn_ready")
        xt_done = sem("xt_done")
        xt_used = sem("xt_used")
        r_done = sem("r_done")
        exp_in = sem("exp_in")
        exp_out = sem("exp_out")
        rw_ready = sem("rw_ready")
        rwt_done = sem("rwt_done")
        rwt_used = sem("rwt_used")
        b_done = sem("b_done")
        b_used = sem("b_used")
        h_done = sem("h_done")
        h_used = sem("h_used")
        y_done = sem("y_done")
        y_used = sem("y_used")
        stored = sem("stored")
        step = sem("step")
        block = ctx.enter_context(nc.Block())
        NLOAD = 6
        G = TILES // GT

        @block.sync
        def _(sp):
            sp.dma_start(wr[:], d["moe_wr"].rearrange("(c p) n -> p c n", p=P)).then_inc(loaded, 16)
            sp.dma_start(br[:], d["moe_br"].partition_broadcast(P)).then_inc(loaded, 16)
            sp.dma_start(b1[:], d["moe_b1"]).then_inc(loaded, 16)
            sp.dma_start(b2[:], d["moe_b2"]).then_inc(loaded, 16)
            sp.dma_start(iota[:], d["iota"]).then_inc(loaded, 16)
            sp.wait_ge(loaded, 16 * 5)
            for e in range(E):
                sp.dma_start(w1[:, e], d["moe_w1"][e].rearrange("(c p) n -> p c n", p=P)).then_inc(loaded2, 16)
                sp.dma_start(w2[:, e], d["moe_w2"][e].rearrange("(c p) n -> p c n", p=P)).then_inc(loaded2, 16)
                sp.wait_ge(loaded2, 32 * (e + 1))
            out = d["out"].rearrange("b (t p) c -> p (b t) c", p=P)
            with sp.Fori(0, G) as g:
                sp.wait_ge(y_used, YB * E * (g + 1))
                sp.wait_ge(loaded, 16 * 5)
                sp.dma_start(out[:, bass.ds(g * GT, GT), :], x_all[:, bass.ds(g * GT, GT), :]).then_inc(stored, 16)
            sp.wait_ge(stored, 16 * G)

        def loop(eng, body):
            body(0)
            with eng.Fori(1, G) as g:
                body(g)

        @block.tensor
        def _(pe):
            pe.wait_ge(loaded, 16 * 5)

            def body(g):
                pe.wait_ge(xn_ready, g + 1)
                for c in range(DC):
                    for t in range(GT):
                        mm = nc.tensor.transpose(ps_t[:, c, t * P:(t + 1) * P], xn[:, t, c * P:(c + 1) * P], ident[:])
                mm.then_inc(xt_done, 1)
                pe.wait_ge(xt_used, g + 1)
                wait(pe, rwt_used, g)
                for t in range(GT):
                    for c in range(DC):
                        mm = nc.tensor.matmul(ps_r[:, t * E:(t + 1) * E], xnT[:, c, t * P:(t + 1) * P], wr[:, c, :],
                                              start=(c == 0), stop=(c == DC - 1))
                mm.then_inc(r_done, 1)

                def hidden(e):
                    if isinstance(g, int) and g == 0:
                        pe.wait_ge(loaded2, 32 * (e + 1))
                    for m in range(HC):
                        n = HC * E * g + HC * e + m
                        wait(pe, h_used, n - 1)
                        for c in range(DC):
                            mm = nc.tensor.matmul(ps_h[:, m % 2, :], w1[:, e, c, m * P:(m + 1) * P], xnT[:, c, :],
                                                  start=(c == 0), stop=(c == DC - 1))
                        mm.then_inc(h_done, 1)

                def outputs(e):
                    pe.wait_ge(h_used, HC * E * g + HC * (e + 1))
                    for t in range(GT):
                        if t % 2 == 0:
                            wait(pe, y_used, YB * (E * g + e - 1) + t // 2 + 1)
                        for m in range(HC):
                            mm = nc.tensor.matmul(ps_y[:, t, :], hT[:, m, t * P:(t + 1) * P], w2[:, e, m, :],
                                                  start=(m == 0), stop=(m == HC - 1))
                        if t % 2 == 1:
                            mm.then_inc(y_done, 1)

                for e in range(E):
                    hidden(e)
                    if e == 0:
                        pe.wait_ge(rw_ready, g + 1)
                        for t in range(GT):
                            mm = nc.tensor.transpose(ps_r[0:E, t * P:(t + 1) * P], rw[:, t, :], ident[:])
                        mm.then_inc(rwt_done, 1)
                        pe.wait_ge(rwt_used, g + 1)
                        for t in range(GT):
                            wait(pe, b_used, GT * g + t)
                            nc.tensor.matmul(ps_b[:], rwT[:, t, :], b2[:], start=True, stop=True).then_inc(b_done, 1)
                    outputs(e)

            loop(pe, body)

        @block.scalar
        def _(act):
            act.wait_ge(loaded, 16 * 5)
            nc.scalar.activation(es[:, 0, :], ident[:, 0:1], ACT.Exp)

            def body(g):
                act.wait_ge(xt_done, g + 1)
                for c in range(DC):
                    ins = nc.scalar.activation(xnT[:, c, :], ps_t[:, c, :], ACT.Copy)
                ins.then_inc(xt_used, 1)

                def relus(e):
                    for m in range(HC):
                        act.wait_ge(h_done, HC * E * g + HC * e + m + 1)
                        nc.scalar.activation(hT[:, m, :], ps_h[:, m % 2, :], ACT.Relu,
                                             bias=b1[:, e, m:m + 1]).then_inc(h_used, 1)
                act.wait_ge(exp_in, g + 1)
                nc.scalar.activation(ew[:], ew[:], ACT.Exp).then_inc(exp_out, 1)
                relus(0)
                act.wait_ge(rwt_done, g + 1)
                nc.scalar.activation(rwT[:].rearrange("p t s -> p (t s)"), ps_r[0:E, :], ACT.Copy).then_inc(rwt_used, 1)
                for e in range(1, E):
                    relus(e)

            loop(act, body)

        @block.vector
        def _(dve):
            dve.wait_ge(loaded, 16 * 5)
            steps = Steps(dve, step)

            def body(g):
                wait(dve, xt_done, g)
                for t in range(GT):
                    ins = nc.vector.tensor_scalar(xn[:, t, :], x_all[:, g * GT + t, :], mean[:, g * GT + t, :],
                                                  rstd[:, g * GT + t, :], ALU.subtract, ALU.mult)
                ins.then_inc(xn_ready, 1)
                dve.wait_ge(r_done, g + 1)
                steps.link(nc.vector.tensor_tensor(logit[:], ps_r[:, 0:GT * E].rearrange("p (t e) -> p t e", e=E),
                                                   br[:].unsqueeze(1).broadcast_to((P, GT, E)), ALU.add))
                for t in range(GT):
                    ins = nc.vector.max(top[:, t, :], logit[:, t, :])
                steps.link(ins)
                nc.vector.tensor_tensor(ew[:], logit[:], top[:, :, 0:1].broadcast_to((P, GT, E)),
                                        ALU.subtract).then_inc(exp_in, 1)
                for t in range(GT):
                    ins = nc.vector.max_index(topi[:, t, :], top[:, t, :], logit[:, t, :])
                steps.link(ins)
                steps.link(nc.vector.tensor_copy(topf[:], topi[:]))
                steps.link(nc.vector.tensor_tensor(hot[:], iota[:, 0:E].unsqueeze(1).unsqueeze(1).broadcast_to((P, GT, 2, E)),
                                                   topf[:, :, 0:2].unsqueeze(3).broadcast_to((P, GT, 2, E)), ALU.is_equal))
                steps.link(nc.vector.tensor_tensor(hot[:, :, 0, :], hot[:, :, 0, :], hot[:, :, 1, :], ALU.add))
                dve.wait_ge(exp_out, g + 1)
                steps.link(nc.vector.tensor_tensor(ew[:], ew[:], hot[:, :, 0, :], ALU.mult))
                steps.link(nc.vector.tensor_reduce(es[:], ew[:], AX.X, ALU.add))
                steps.link(nc.vector.reciprocal(er[:], es[:]))
                wait(dve, y_used, YB * E * g)
                nc.vector.tensor_tensor(rw[:], ew[:], er[:].broadcast_to((P, GT, E)), ALU.mult).then_inc(rw_ready, 1)
                for t in range(GT):
                    dve.wait_ge(b_done, GT * g + t + 1)
                    xt = x_all[:, g * GT + t, :]
                    nc.vector.tensor_tensor(xt, ps_b[:], xt, ALU.add).then_inc(b_used, 1)
                dve.wait_ge(rw_ready, g + 1)
                dve.wait_ge(b_used, GT * (g + 1))
                for e in range(E):
                    for t in range(GT):
                        if t % 2 == 0:
                            dve.wait_ge(y_done, YB * (E * g + e) + t // 2 + 1)
                            if e > 0:
                                dve.wait_ge(y_used, YB * (E * g + e - 1) + t // 2 + 1)
                        xt = x_all[:, g * GT + t, :]
                        ins = nc.vector.scalar_tensor_tensor(xt, ps_y[:, t, :], rw[:, t, e:e + 1], xt, ALU.mult, ALU.add)
                        if t % 2 == 1:
                            ins.then_inc(y_used, 1)
                steps.again()

            loop(dve, body)



def _padded_heads(np, wt):
    out = np.zeros((wt.shape[0], HEADS, SLOT), wt.dtype)
    out[:, :, :HD] = wt.reshape(wt.shape[0], HEADS, HD)
    return out.reshape(wt.shape[0], HEADS * SLOT)


def _padded_bias(np, b):
    out = np.zeros((HEADS, SLOT), b.dtype)
    out[:, :HD] = b.reshape(HEADS, HD)
    return out.reshape(QUADS, P).T


def _pairs_swapped(wt):
    return wt.reshape(wt.shape[0], -1, 2)[:, :, ::-1].reshape(wt.shape)


def _constants(np):
    f = np.float32
    c = {"ident": np.eye(P, dtype=f), "iota": np.tile(np.arange(P, dtype=f), (P, 1))}
    freq = (1.0 / np.power(f(10000.0), np.arange(0, HD, 2, dtype=f) / f(HD))).astype(f)
    angle = np.arange(S, dtype=f)[None, :] * freq[:, None]
    cos, sin = np.cos(angle).astype(f), np.sin(angle).astype(f)
    ct, st = np.zeros((SLOT, S), f), np.zeros((SLOT, S), f)
    ct[0:HD:2], ct[1:HD:2] = cos, cos
    st[0:HD:2], st[1:HD:2] = -sin, sin
    ct, st = np.tile(ct, (4, 1)), np.tile(st, (4, 1))
    c |= {"cosk": ct, "sink": st, "cosq": ct * f(0.25), "sinq": st * f(0.25)}
    c["mask"] = np.triu(np.full((P, P), -1e30, f), 1)
    i = np.arange(S)
    near = np.abs(i[:, None] - i[None, :]) <= 2
    c["band"] = np.where(near, f(np.exp(0.1)), f(1.0)).astype(f)
    return c


def _lay_out(np, v):
    a = _constants(np)
    a["x"] = v["x"]
    a["ctx"] = v["ctx_1024"]
    wk, wq, wv = (m.T for m in np.split(v["L0_attn_W_KQV"], 3, axis=0))
    a |= {"causal_wq": _padded_heads(np, wq), "causal_wk": _padded_heads(np, wk), "causal_wv": wv,
          "causal_wqs": _padded_heads(np, _pairs_swapped(wq)), "causal_wks": _padded_heads(np, _pairs_swapped(wk)),
          "causal_wo": v["L0_attn_W_O"].T}
    for kind, name in (("cross", "L0_xattn"), ("band", "L1_attn")):
        a |= {f"{kind}_wq": _padded_heads(np, v[f"{name}_Wq"].T), f"{kind}_wk": _padded_heads(np, v[f"{name}_Wk"].T),
              f"{kind}_wv": v[f"{name}_Wv"].T, f"{kind}_wo": v[f"{name}_Wo"].T,
              f"{kind}_bq": _padded_bias(np, v[f"{name}_bq"]), f"{kind}_bk": _padded_bias(np, v[f"{name}_bk"]),
              f"{kind}_bv": v[f"{name}_bv"], f"{kind}_bo": v[f"{name}_bo"]}
    a["band_bias"] = _padded_bias(np, v["L1_attn_ocr_bias"])
    k1, k2 = v["L0_ffn_K1"].T, v["L0_ffn_K2"].T
    keys = np.zeros((4, HALF, 4, KEYS), k1.dtype)
    for n in range(4):
        keys[n, :, n, :] = (k1, k2)[n % 2]
    a |= {"peer_wq": v["L0_ffn_Wq"], "peer_bq": v["L0_ffn_bq"].reshape(4, P).T, "peer_keys": keys.reshape(P, 4 * KEYS),
          "peer_down": v["L0_ffn_W_down"][:EXPERTS].reshape(P, EV, D).transpose(2, 1, 0),
          "peer_up": v["L0_ffn_W_up"][:EXPERTS].reshape(P, EV, D)}
    wl = v["L1_xattn_W_l"].T
    a |= {"bidaf_wl": wl, "bidaf_bl": v["L1_xattn_b_l"],
          "bidaf_vec": np.stack([v["L1_xattn_w_cq"], v["L1_xattn_w_c"], v["L1_xattn_w_q"]]).reshape(3, DC, P).transpose(2, 0, 1),
          "bidaf_b": np.stack([v["L1_xattn_b_cq"], v["L1_xattn_b_c"], v["L1_xattn_b_q"]]).reshape(1, 3)}
    a |= {"moe_w1": v["L1_ffn_W1"], "moe_w2": v["L1_ffn_W2"], "moe_b2": v["L1_ffn_b2"], "moe_wr": v["L1_ffn_Wr"],
          "moe_br": v["L1_ffn_br"], "moe_b1": v["L1_ffn_b1"].reshape(E, HC, P).transpose(2, 0, 1)}
    return {k: np.ascontiguousarray(x) for k, x in a.items()}



def decoder(nc, d):
    with ExitStack() as ctx:
        def sb(name, shape):
            return ctx.enter_context(nc.sbuf_tensor(name, shape, F32))
        x_all = sb("x_all", [P, TILES, D])
        ident = sb("ident", [P, P])
        mean = sb("mean", [P, TILES, 1])
        rstd = sb("rstd", [P, TILES, 1])
        load_stage(nc, x_all, ident, d)
        norm_stage(nc, "norm0", x_all, mean, rstd)
        attention_stage(nc, "causal", x_all, mean, rstd, ident, d)
        norm_stage(nc, "norm1", x_all, mean, rstd)
        attention_stage(nc, "cross", x_all, mean, rstd, ident, d)
        norm_stage(nc, "norm2", x_all, mean, rstd)
        peer_stage(nc, x_all, mean, rstd, ident, d)
        norm_stage(nc, "norm3", x_all, mean, rstd)
        attention_stage(nc, "band", x_all, mean, rstd, ident, d)
        norm_stage(nc, "norm4", x_all, mean, rstd)
        bidaf_stage(nc, x_all, mean, rstd, ident, d)
        norm_stage(nc, "norm5", x_all, mean, rstd)
        moe_stage(nc, x_all, mean, rstd, ident, d)


def kernel(**inputs):
    import numpy as np
    import concourse.bacc as bacc
    from concourse.bass_utils import run_bass_kernel_spmd

    arrays = {f"in_{k}": v for k, v in _lay_out(np, {k: np.asarray(v) for k, v in inputs.items()}).items()}
    nc = bacc.Bacc("TRN2", target_bir_lowering=False, num_devices=1)
    d = {k[3:]: nc.dram_tensor(k, v.shape, mybir.dt.from_np(v.dtype), kind="ExternalInput").ap() for k, v in arrays.items()}
    d["out"] = nc.dram_tensor("out", (B, S, D), F32, kind="ExternalOutput").ap()
    decoder(nc, d)
    return run_bass_kernel_spmd(nc, [arrays], core_ids=[0]).results[0]["out"]
```

```python
from contextlib import ExitStack

import concourse.bass as bass
from concourse import mybir

P = 128
ALU = mybir.AluOpType
ACT = mybir.ActivationFunctionType
AX = mybir.AxisListType
F32 = mybir.dt.float32
BF16 = mybir.dt.bfloat16
U32 = mybir.dt.uint32
I32 = mybir.dt.int32

B, S, D = 16, 256, 256
CTX = 120
HEADS, HD = 16, 16
SLOT = 32
QUADS = HEADS // 4
TT = S // P
TILES = B * TT
DC = D // P
EPS = 1e-5


def wait(eng, sem, value):
    if isinstance(value, int) and value <= 0:
        return
    eng.wait_ge(sem, value)


class Steps:

    def __init__(self, eng, sem):
        self.eng, self.sem, self.n = eng, sem, 0

    def link(self, instruction):
        self.n += 1
        instruction.then_inc(self.sem, 1)
        self.eng.wait_ge(self.sem, self.n)

    def again(self):
        if self.n:
            self.eng.sem_clear(self.sem)
            self.n = 0


class Room:

    def __init__(self, nc, ctx, stage):
        self.nc, self.ctx, self.stage = nc, ctx, stage
        self.sems = []
        ctx.callback(self.close)

    def close(self):
        self.nc.clear_and_free_semaphores(self.sems)
        self.nc.all_engine_barrier()

    def sb(self, name, shape, dt=F32):
        return self.ctx.enter_context(self.nc.sbuf_tensor(f"{self.stage}_{name}", shape, dt))

    def ps(self, name, shape, dt=F32):
        return self.ctx.enter_context(self.nc.psum_tensor(f"{self.stage}_{name}", shape, dt))

    def sem(self, name):
        self.sems.append(self.nc.alloc_semaphore(f"{self.stage}_{name}"))
        return self.sems[-1]


def load_stage(nc, x_all, ident, d):
    with ExitStack() as ctx:
        r = Room(nc, ctx, "load")
        loaded = r.sem("loaded")
        block = ctx.enter_context(nc.Block())

        @block.sync
        def _(sp):
            xv = d["x"].rearrange("b (t p) c -> p (b t) c", p=P)
            for k in range(4):
                n = TILES // 4
                sp.dma_start(x_all[:, k * n:(k + 1) * n, :], xv[:, k * n:(k + 1) * n, :]).then_inc(loaded, 16)
            sp.dma_start(ident[:], d["ident"]).then_inc(loaded, 16)
            sp.wait_ge(loaded, 16 * 5)


def norm_stage(nc, name, x_all, mean, rstd):
    with ExitStack() as ctx:
        r = Room(nc, ctx, name)
        moments = r.sb("moments", [P, TILES, 6])
        mv = r.sb("mv", [P, TILES, 2])
        var = r.sb("var", [P, TILES, 1])
        root = r.sb("root", [P, TILES, 1])
        guess = r.sb("guess", [P, TILES, 1])
        t0 = r.sb("t0", [P, TILES, 1])
        step = r.sem("step")
        var_ready = r.sem("var_ready")
        root_ready = r.sem("root_ready")
        block = ctx.enter_context(nc.Block())

        @block.scalar
        def _(act):
            act.wait_ge(var_ready, 1)
            nc.scalar.activation(root[:], var[:], ACT.Sqrt).then_inc(root_ready, 1)

        @block.vector
        def _(dve):
            steps = Steps(dve, step)
            with dve.Fori(0, TILES // 4) as i:
                for k in range(4):
                    t = 4 * i + k
                    nc.vector.bn_stats(moments[:, t, :], x_all[:, t, :])
            steps.link(nc.vector.drain())
            for t in range(TILES):
                ins = nc.vector.bn_aggr(mv[:, t, :], moments[:, t, :])
            steps.link(ins)
            nc.vector.tensor_copy(mean[:], mv[:, :, 0:1])
            nc.vector.tensor_scalar(var[:], mv[:, :, 1:2], EPS, None, ALU.add).then_inc(var_ready, 1)
            dve.wait_ge(root_ready, 1)
            steps.link(nc.vector.reciprocal(guess[:], root[:]))
            steps.link(nc.vector.tensor_tensor(t0[:], guess[:], guess[:], ALU.mult))
            steps.link(nc.vector.tensor_tensor(root[:], t0[:], var[:], ALU.mult))
            steps.link(nc.vector.tensor_scalar(t0[:], root[:], -0.5, 1.5, ALU.mult, ALU.add))
            steps.link(nc.vector.tensor_tensor(rstd[:], guess[:], t0[:], ALU.mult))


def attention_stage(nc, kind, x_all, mean, rstd, ident, d):
    rope = kind == "causal"
    cross = kind == "cross"
    KN = CTX if cross else P
    KT = 1 if cross else TT
    KS = KT * KN
    NQUAD = HEADS // 4
    CH = HEADS // DC
    JOBS = [(qk, c) for c in range(DC) for qk in range(2)]
    NJ = len(JOBS)
    QRUNS = [(0, 3, 0), (3, 2, 1), (5, 1, 2)]
    KRUNS = [(0, 3, 0), (3, 2, 0), (5, 1, 0)]
    ROWS = 6 * HD
    STACKED = 16 * (1 + len(KRUNS))
    qfrom = {k: (k * P if rope else 0) for k in range(KT)}
    kcol = {k: sum(S - qfrom[i] for i in range(k)) for k in range(KT)}
    seen = {q: ((q + 1) * P if rope else KS) for q in range(TT)}
    qcol = {q: sum(seen[i] for i in range(q)) for q in range(TT)}
    COLS = sum(S - qfrom[k] for k in range(KT))
    REACH = 2
    near = {k: (max(0, k * P - REACH), min(S, (k + 1) * P + REACH)) for k in range(KT)}

    with ExitStack() as ctx:
        r = Room(nc, ctx, kind)
        sb, ps, sem = r.sb, r.ps, r.sem
        names = ["wq", "wqs", "wk", "wks", "wv"] if rope else ["wq", "wk", "wv"]
        w = {n: sb(n, [P, DC, D]) for n in names}
        w["wo"] = sb("wo", [P, NQUAD, D])
        pack = sb("pack", [P, SLOT])
        spread = sb("spread", [P, NQUAD, P])
        nload = len(w) + 2
        if rope:
            tab = {n: sb(n, [P, S]) for n in ("cosq", "sinq", "cosk", "sink")}
            ident16 = sb("ident16", [P, P], BF16)
            mask = sb("mask", [P, 2, P], BF16)
            maskf = sb("maskf", [P, 2, P])
            rot = sb("rot", [P, 2, 2, S])
            nload += 5
        else:
            bq = sb("bq", [P, DC])
            bk = sb("bk", [P, DC])
            bv = sb("bv", [P, D])
            bo = sb("bo", [P, D])
            nload += 4
        if kind == "band":
            bias2 = sb("bias2", [P, DC])
            band = sb("band", [P, TT, S])
            nload += 2
        if cross:
            nload += 1
            ctx_sb = sb("ctx", [P, B, D])
            ctx_two = sb("ctx_two", [P, 2, D])
            ctxT = sb("ctxT", [P, DC, CTX])
        xn = sb("xn", [P, TT, D])
        xnT = sb("xnT", [P, DC, S])
        full = sb("full", [P, 2, S])
        rest = sb("rest", [P, S])
        part = sb("part", [P, NJ, 3, S], BF16)
        qs = sb("qs", [P, 2, HEADS, S], BF16)
        ks = sb("ks", [P, 2, HEADS, KS], BF16)
        va = sb("va", [P, 2, KT, HEADS, SLOT])
        nmax = sb("nmax", [P, TT, HEADS])
        nrest = sb("nrest", [CH, S])
        npart = sb("npart", [CH, 2, 3, S], BF16)
        probT = sb("probT", [P, 8, COLS])
        oq = sb("oq", [P, NQUAD, S])
        rr = sb("rr", [P, S])
        onT = sb("onT", [P, NQUAD, S])
        ytmp = sb("ytmp", [P, TT, D])
        warm = sb("warm", [P, 1])
        qscratch = nc.dram_tensor(f"{kind}_qscratch", (2, DC, 6, P, S), BF16).ap()
        kscratch = nc.dram_tensor(f"{kind}_kscratch", (2, DC, 3, P, KS), BF16).ap()
        nscratch = nc.dram_tensor(f"{kind}_nscratch", (2, 2, 3, CH, S), BF16).ap()

        ps_p = ps("ps_p", [P, 2, 512])
        ps_1 = ps("ps_1", [P, 2, 512])
        ps_2 = ps("ps_2", [P, 2, 512])
        ps_o = ps("ps_o", [P, 512])
        ps_n = ps("ps_n", [P, 512])

        weights = sem("weights")
        ready = sem("ready")
        xn_ready = sem("xn_ready")
        xt_done = sem("xt_done")
        xt_used = sem("xt_used")
        proj_done = sem("proj_done")
        proj_used = sem("proj_used")
        rest_ready = sem("rest_ready")
        split_ready = sem("split_ready")
        parts_out = sem("parts_out")
        stacked = [sem(f"stacked{c}") for c in range(DC)]
        v_done = sem("v_done")
        v_used = sem("v_used")
        s1_done = sem("s1_done")
        nmax_ready = sem("nmax_ready")
        nt_done = sem("nt_done")
        n_ready = sem("n_ready")
        n_out = sem("n_out")
        n_in = [sem(f"n_in{c}") for c in range(DC)]
        s2_done = sem("s2_done")
        p_ready = sem("p_ready")
        b_ready = sem("b_ready")
        pv_done = sem("pv_done")
        oq_ready = sem("oq_ready")
        packed = sem("packed")
        rr_ready = sem("rr_ready")
        spread_done = sem("spread_done")
        on_ready = sem("on_ready")
        y_done = sem("y_done")
        y_used = sem("y_used")
        step = sem("step")
        block = ctx.enter_context(nc.Block())

        def outs(b, j):
            return 16 * (DC * (len(QRUNS) + 1) * b + sum(1 if qk else len(QRUNS) for qk, _ in JOBS[:j + 1]))

        FIND = {8 + n: (2 * n, 2 * n + 2) for n in range(HEADS // 2)}

        def macro(e, b, par, first=False, last=False):
            for s in range(HEADS):
                e.head(b, par, s)
                if s > 0:
                    e.factor(b, par, s - 1)
                if not first:
                    if s == 0:
                        e.turn_max(b, par, 1)
                    if s == 1:
                        e.weigh(b - 1, 1 - par, NQUAD - 1)
                    if s == 2:
                        e.sums(b - 1, 2 * b + 2)
                    if s == 3:
                        e.normalise(b - 1)
                    if s == 6:
                        e.out(b - 1)
                if s % 4 == 1 and s > 1:
                    e.weigh(b, par, s // 4 - 1)
                if not last:
                    if s == 0:
                        e.turn(b + 1, 1 - par)
                    if 1 <= s <= NJ:
                        e.project(b + 1, 1 - par, s - 1)
                    if s == NJ + 1:
                        e.values(b + 1, 1 - par)
                    if s in FIND:
                        for h in range(*FIND[s]):
                            e.find(b + 1, 1 - par, h)
                    if s == 12:
                        e.turn_max(b + 1, 1 - par, 0)
            e.factor(b, par, HEADS - 1)
            e.end()

        def program(eng, e):
            e.turn(0, 0)
            for j in range(NJ):
                e.project(0, 0, j)
            e.values(0, 0)
            for h in range(HEADS):
                e.find(0, 0, h)
                if h % CH == CH - 1:
                    e.turn_max(0, 0, h // CH)
            macro(e, 0, 0, first=True)
            with eng.Fori(0, B // 2 - 1) as i:
                macro(e, 2 * i + 1, 1)
                macro(e, 2 * i + 2, 0)
            macro(e, B - 1, 1, last=True)
            e.weigh(B - 1, 1, NQUAD - 1)
            e.sums(B - 1, 2 * B)
            e.normalise(B - 1)
            e.out(B - 1)

        class Part:

            def turn(self, b, par): pass
            def project(self, b, par, j): pass
            def values(self, b, par): pass
            def find(self, b, par, h): pass
            def turn_max(self, b, par, c): pass
            def head(self, b, par, h): pass
            def factor(self, b, par, h): pass
            def weigh(self, b, par, j): pass
            def sums(self, b, turned): pass
            def normalise(self, b): pass
            def out(self, b): pass
            def end(self): pass

        @block.sync
        def _(sp):
            def chunks(ap):
                return ap.rearrange("(c p) n -> p c n", p=P)
            for n in w:
                sp.dma_start(w[n][:], chunks(d[f"{kind}_{n}"])).then_inc(weights, 16)
            sp.dma_start(pack[:], d["pack"]).then_inc(weights, 16)
            sp.dma_start(spread[:], d["spread"]).then_inc(weights, 16)
            if rope:
                for n in tab:
                    sp.dma_start(tab[n][:], d[f"{n}"]).then_inc(weights, 16)
                sp.dma_start(maskf[:], chunks(d["mask"])).then_inc(weights, 16)
            else:
                sp.dma_start(bq[:], d[f"{kind}_bq"]).then_inc(weights, 16)
                sp.dma_start(bk[:], d[f"{kind}_bk"]).then_inc(weights, 16)
                sp.dma_start(bv[:], d[f"{kind}_bv"].partition_broadcast(P)).then_inc(weights, 16)
                sp.dma_start(bo[:], d[f"{kind}_bo"].partition_broadcast(P)).then_inc(weights, 16)
            if cross:
                sp.dma_start(ctx_sb[0:CTX, :, :], d["ctx"].rearrange("b k c -> k b c")).then_inc(weights, 16)
            if kind == "band":
                sp.dma_start(bias2[:], d["band_bias"]).then_inc(weights, 16)
                sp.dma_start(band[:], chunks(d["band"])).then_inc(weights, 16)

            def settle(sem, value):
                wait(sp, sem, value)
                sp.wait_ge(weights, 16 * nload)

            class Sync(Part):
                def project(self, b, par, j):
                    qk, c = JOBS[j]
                    n = S if qk == 0 else KS
                    if j == 0:
                        settle(s2_done, HEADS * (b - 1))
                    settle(split_ready, NJ * b + j + 1)
                    def stack(ap):
                        return ap.rearrange("s (r h) t -> (s r) h t", h=CH)
                    mine = slice(c * CH, (c + 1) * CH)
                    if qk == 0:
                        for slot, slots, a in QRUNS:
                            sp.dma_start(qscratch[par, c, slot:slot + slots].rearrange("s p t -> p s t"),
                                         part[:, j, a:a + 1, :].broadcast_to((P, slots, S))).then_inc(parts_out, 16)
                        settle(parts_out, outs(b, j))
                        sp.dma_start(qs[0:ROWS, par, mine, :], stack(qscratch[par, c])).then_inc(stacked[c], 16)
                    else:
                        sp.dma_start(kscratch[par, c].rearrange("s p t -> p s t"), part[:, j, :, 0:n]).then_inc(parts_out, 16)
                        settle(parts_out, outs(b, j))
                        for slot, slots, a in KRUNS:
                            sp.dma_start(ks[slot * HD:(slot + slots) * HD, par, mine, :],
                                         stack(kscratch[par, c, a:a + slots])).then_inc(stacked[c], 16)

                def turn_max(self, b, par, c):
                    settle(n_ready, 2 * b + c + 1)
                    sp.dma_start(nscratch[par, c].rearrange("a h t -> h a t"), npart[:, c, :, :]).then_inc(n_out, 16)
                    settle(n_out, 16 * (2 * b + c + 1))
                    sp.dma_start(qs[ROWS:ROWS + 3, par, c * CH:(c + 1) * CH, :], nscratch[par, c]).then_inc(n_in[c], 16)
            program(sp, Sync())

        @block.tensor
        def _(pe):
            pe.wait_ge(weights, 16 * nload)
            pe.wait_ge(ready, 1)

            class Tensor(Part):
                def turn(self, b, par):
                    pe.wait_ge(xn_ready, b + 1)
                    pe.wait_ge(y_used, max(1, b - 1) if isinstance(b, int) else b - 1)
                    for t in range(TT):
                        for c in range(DC):
                            mm = nc.tensor.transpose(ps_p[:, 0, c * S + t * P:c * S + (t + 1) * P],
                                                     xn[:, t, c * P:(c + 1) * P], ident[:])
                    mm.then_inc(xt_done, 1)
                    if cross:
                        wait(pe, v_used, b)
                        for c in range(DC):
                            mm = nc.tensor.transpose(ps_p[:, 1, c * CTX:(c + 1) * CTX], ctx_two[0:CTX, par, c * P:(c + 1) * P],
                                                     ident[0:CTX, 0:CTX])
                        mm.then_inc(xt_done, 1)

                def project(self, b, par, j):
                    if j == 0:
                        pe.wait_ge(xt_used, (2 if cross else 1) * (b + 1))
                        wait(pe, v_used, b)
                    if j >= 2:
                        pe.wait_ge(proj_used, NJ * b + j - 1)
                    qk, chunk = JOBS[j]
                    src, n = (ctxT, CTX) if cross and qk else (xnT, S)
                    mine = [("wq", "wqs"), ("wk", "wks")] if rope else [("wq",), ("wk",)]
                    for k, name in enumerate(mine[qk]):
                        for c in range(DC):
                            mm = nc.tensor.matmul(ps_p[:, (j + 1) % 2, k * S:k * S + n],
                                                  w[name][:, c, chunk * P:(chunk + 1) * P], src[:, c, :],
                                                  start=(c == 0), stop=(c == DC - 1))
                    mm.then_inc(proj_done, 1)

                def values(self, b, par):
                    pe.wait_ge(proj_used, NJ * b + NJ - 1)
                    src = ctxT if cross else xnT
                    for k in range(KT):
                        for c in range(DC):
                            mm = nc.tensor.matmul(ps_p[0:KN, 1, k * D:(k + 1) * D], src[:, c, k * KN:(k + 1) * KN],
                                                  w["wv"][:, c, :], start=(c == 0), stop=(c == DC - 1))
                    mm.then_inc(v_done, 1)

                def find(self, b, par, h):
                    if h % CH == 0:
                        pe.wait_ge(stacked[h // CH], STACKED * (b + 1))
                    wait(pe, nmax_ready, HEADS * b + h - 1)
                    for q in range(TT):
                        c0, n = qcol[q], seen[q]
                        mm = nc.tensor.matmul(ps_1[:, h % 2, c0:c0 + n], qs[0:ROWS, par, h, q * P:(q + 1) * P],
                                              ks[0:ROWS, par, h, 0:n], start=True, stop=not rope)
                        if rope:
                            mm = nc.tensor.matmul(ps_1[:, h % 2, c0 + q * P:c0 + (q + 1) * P], ident16[:], mask[:, 0, :],
                                                  start=False, stop=True)
                    mm.then_inc(s1_done, 1)

                def turn_max(self, b, par, c):
                    pe.wait_ge(nmax_ready, HEADS * b + CH * (c + 1))
                    wait(pe, n_ready, 2 * b + c)
                    wait(pe, on_ready, 2 * (b - 1))
                    for t in range(TT):
                        mm = nc.tensor.transpose(ps_n[0:CH, t * P:(t + 1) * P], nmax[:, t, c * CH:(c + 1) * CH], ident[:])
                    mm.then_inc(nt_done, 1)

                def head(self, b, par, h):
                    if h % CH == 0:
                        pe.wait_ge(n_in[h // CH], 16 * (b + 1))
                    wait(pe, p_ready, HEADS * b + h - 1)
                    for k in range(KT):
                        c0, n = kcol[k], S - qfrom[k]
                        mm = nc.tensor.matmul(ps_2[0:KN, h % 2, c0:c0 + n], ks[0:ROWS + 3, par, h, k * KN:(k + 1) * KN],
                                              qs[0:ROWS + 3, par, h, qfrom[k]:S], start=True, stop=not rope)
                        if rope:
                            mm = nc.tensor.matmul(ps_2[:, h % 2, c0:c0 + P], ident16[:], mask[:, 1, :],
                                                  start=False, stop=True)
                    mm.then_inc(s2_done, 1)

                def weigh(self, b, par, j):
                    if j == 0:
                        pe.wait_ge(v_used, b + 1)
                    pe.wait_ge(b_ready if kind == "band" else p_ready, HEADS * b + 4 * j + 4)
                    wait(pe, oq_ready, NQUAD * b + j)
                    if j == 0:
                        wait(pe, on_ready, 2 * b)
                    for k in range(KT):
                        for g in range(4):
                            h = 4 * j + g
                            mm = nc.tensor.matmul(ps_o[SLOT * g:SLOT * (g + 1), qfrom[k]:S], va[0:KN, par, k, h, :],
                                                  probT[0:KN, h % 8, kcol[k]:kcol[k] + S - qfrom[k]],
                                                  start=(k == 0), stop=(k == KT - 1))
                    mm.then_inc(pv_done, 1)

                def sums(self, b, turned):
                    pe.wait_ge(oq_ready, NQUAD * (b + 1))
                    pe.wait_ge(n_ready, turned)
                    wait(pe, on_ready, 2 * b)
                    for j in range(NQUAD):
                        mm = nc.tensor.matmul(ps_n[SLOT * j:SLOT * (j + 1), 0:S], pack[:], oq[:, j, :], start=True, stop=True)
                    mm.then_inc(packed, 1)

                def normalise(self, b):
                    pe.wait_ge(rr_ready, b + 1)
                    for half, bank in enumerate((ps_n, ps_o)):
                        for n in range(2):
                            mm = nc.tensor.matmul(bank[:, n * S:(n + 1) * S], spread[:, 2 * half + n, :], rr[:],
                                                  start=True, stop=True)
                        mm.then_inc(spread_done, 1)

                def out(self, b):
                    pe.wait_ge(on_ready, 2 * (b + 1))
                    pe.wait_ge(proj_used, min(NJ * (b + 3), NJ * B) if isinstance(b, int) else NJ * (b + 3))
                    pe.wait_ge(y_used, b + 1)
                    for t in range(TT):
                        for j in range(NQUAD):
                            mm = nc.tensor.matmul(ps_p[:, 0, t * D:(t + 1) * D], onT[:, j, t * P:(t + 1) * P],
                                                  w["wo"][:, j, :], start=(j == 0), stop=(j == NQUAD - 1))
                    mm.then_inc(y_done, 1)
            program(pe, Tensor())

        @block.scalar
        def _(act):
            act.wait_ge(weights, 16 * nload)
            act.wait_ge(ready, 1)
            nc.scalar.activation(warm[:], ident[:, 0:1], ACT.Exp)

            class Scalar(Part):
                def turn(self, b, par):
                    act.wait_ge(xt_done, (2 if cross else 1) * b + 1)
                    nc.scalar.activation(xnT[:].rearrange("p c s -> p (c s)"), ps_p[:, 0, :], ACT.Copy).then_inc(xt_used, 1)
                    if cross:
                        act.wait_ge(xt_done, 2 * b + 2)
                        nc.scalar.activation(ctxT[:].rearrange("p c s -> p (c s)"), ps_p[:, 1, 0:DC * CTX],
                                             ACT.Copy).then_inc(xt_used, 1)

                def project(self, b, par, j):
                    if rope:
                        return
                    act.wait_ge(proj_done, NJ * b + j + 1)
                    wait(act, split_ready, NJ * b + j - 1)
                    wait(act, parts_out, outs(b - 1, j))
                    qk, c = JOBS[j]
                    n = S if qk == 0 else KS
                    for dst in (full[:, j % 2, 0:n], part[:, j, 0, 0:n]):
                        ins = nc.scalar.activation(dst, ps_p[:, (j + 1) % 2, 0:n], ACT.Identity,
                                                   bias=(bq, bk)[qk][:, c:c + 1], scale=(0.25, 1.0)[qk])
                    ins.then_inc(proj_used, 1)

                def values(self, b, par):
                    if not rope:
                        return
                    act.wait_ge(v_done, b + 1)
                    wait(act, pv_done, NQUAD * (b - 1))
                    for k in range(KT):
                        ins = nc.scalar.activation(va[:, par, k, :, 0:HD],
                                                   ps_p[:, 1, k * D:(k + 1) * D].rearrange("p (h e) -> p h e", h=HEADS),
                                                   ACT.Copy)
                    ins.then_inc(v_used, 1)

                def head(self, b, par, h):
                    act.wait_ge(s2_done, HEADS * b + h + 1)
                    wait(act, pv_done, NQUAD * b + h // 4 - 1)
                    nc.scalar.activation(probT[0:KN, h % 8, :], ps_2[0:KN, h % 2, 0:COLS], ACT.Exp).then_inc(p_ready, 1)

                def weigh(self, b, par, j):
                    act.wait_ge(pv_done, NQUAD * b + j + 1)
                    if j == 0:
                        wait(act, on_ready, 2 * b)
                    nc.scalar.activation(oq[:, j, :], ps_o[:, 0:S], ACT.Copy).then_inc(oq_ready, 1)
            program(act, Scalar())

        @block.gpsimd
        def _(pool):
            class Pool(Part):
                def project(self, b, par, j):
                    qk, c = JOBS[j]
                    n = S if qk == 0 else KS
                    src, high = full[:, j % 2, 0:n], part[:, j, 0, 0:n]
                    pool.wait_ge(proj_used, NJ * b + j + 1)
                    wait(pool, split_ready, NJ * b + j)
                    nc.gpsimd.tensor_tensor(rest[:, 0:n], src, high, ALU.subtract)
                    nc.gpsimd.tensor_tensor(part[:, j, 1, 0:n], src, high, ALU.subtract).then_inc(rest_ready, 1)
                    pool.wait_ge(rest_ready, NJ * b + j + 1)
                    nc.gpsimd.tensor_tensor(part[:, j, 2, 0:n], rest[:, 0:n], part[:, j, 1, 0:n],
                                            ALU.subtract).then_inc(split_ready, 1)
            program(pool, Pool())

        @block.vector
        def _(dve):
            dve.wait_ge(weights, 16 * nload)
            steps = Steps(dve, step)
            if rope:
                steps.link(nc.vector.tensor_copy(ident16[:], ident[:]))
                steps.link(nc.vector.tensor_copy(mask[:], maskf[:]))
            else:
                if kind == "band":
                    steps.link(nc.vector.tensor_tensor(bq[:], bq[:], bias2[:], ALU.add))
                steps.link(nc.vector.tensor_scalar(bq[:], bq[:], 0.25, None, ALU.mult))
            nc.vector.memset(ks[ROWS:ROWS + 3, :, :, :], 1.0).then_inc(y_used, 1)
            nc.vector.memset(va[:], 1.0).then_inc(ready, 1)
            dve.wait_ge(ready, 1)
            steps.again()

            class Vector(Part):
                def turn(self, b, par):
                    wait(dve, xt_done, (2 if cross else 1) * b)
                    if cross:
                        nc.vector.tensor_copy(ctx_two[0:CTX, par, :], ctx_sb[0:CTX, b, :])
                    for t in range(TT):
                        ins = nc.vector.tensor_scalar(xn[:, t, :], x_all[:, b * TT + t, :], mean[:, b * TT + t, :],
                                                      rstd[:, b * TT + t, :], ALU.subtract, ALU.mult)
                    ins.then_inc(xn_ready, 1)

                def project(self, b, par, j):
                    if not rope:
                        return
                    dve.wait_ge(proj_done, NJ * b + j + 1)
                    qk, c = JOBS[j]
                    bank = ps_p[:, (j + 1) % 2, :]
                    cs, sn = ("cosk", "sink") if qk else ("cosq", "sinq")
                    wait(dve, proj_used, NJ * b + j - 1)
                    nc.vector.tensor_tensor(rot[:, j % 2, 0, :], bank[:, 0:S], tab[cs][:], ALU.mult)
                    steps.link(nc.vector.tensor_tensor(rot[:, j % 2, 1, :], bank[:, S:2 * S], tab[sn][:], ALU.mult))
                    wait(dve, split_ready, NJ * b + j - 1)
                    wait(dve, parts_out, outs(b - 1, j))
                    for dst in (full[:, j % 2, :], part[:, j, 0, :]):
                        ins = nc.vector.tensor_tensor(dst, rot[:, j % 2, 0, :], rot[:, j % 2, 1, :], ALU.add)
                    ins.then_inc(proj_used, 1)

                def values(self, b, par):
                    if rope:
                        return
                    dve.wait_ge(v_done, b + 1)
                    wait(dve, pv_done, NQUAD * (b - 1))
                    for k in range(KT):
                        ins = nc.vector.tensor_tensor(
                            va[0:KN, par, k, :, 0:HD],
                            ps_p[0:KN, 1, k * D:(k + 1) * D].rearrange("p (h e) -> p h e", h=HEADS),
                            bv[0:KN, :].rearrange("p (h e) -> p h e", h=HEADS), ALU.add)
                    ins.then_inc(v_used, 1)

                def find(self, b, par, h):
                    dve.wait_ge(s1_done, HEADS * b + h + 1)
                    if rope:
                        for q in range(TT):
                            ins = nc.vector.tensor_reduce(nmax[:, q, h:h + 1], ps_1[:, h % 2, qcol[q]:qcol[q] + seen[q]],
                                                          AX.X, ALU.max, negate=True)
                    else:
                        ins = nc.vector.tensor_reduce(nmax[:, :, h],
                                                      ps_1[:, h % 2, 0:TT * KS].rearrange("p (q k) -> p q k", q=TT),
                                                      AX.X, ALU.max, negate=True)
                    ins.then_inc(nmax_ready, 1)

                def turn_max(self, b, par, c):
                    dve.wait_ge(nt_done, 2 * b + c + 1)
                    wait(dve, n_ready, 2 * b + c)
                    wait(dve, n_out, 16 * (2 * b + c - 1))
                    high, middle, low = (npart[:, c, a, :] for a in range(3))
                    steps.link(nc.vector.tensor_copy(high, ps_n[0:CH, 0:S]))
                    nc.vector.tensor_tensor(nrest[:], ps_n[0:CH, 0:S], high, ALU.subtract)
                    steps.link(nc.vector.tensor_tensor(middle, ps_n[0:CH, 0:S], high, ALU.subtract))
                    nc.vector.tensor_tensor(low, nrest[:], middle, ALU.subtract).then_inc(n_ready, 1)

                def factor(self, b, par, h):
                    if kind != "band":
                        return
                    dve.wait_ge(p_ready, HEADS * b + h + 1)
                    for k in range(KT):
                        lo, hi = near[k]
                        e = probT[:, h % 8, kcol[k] + lo:kcol[k] + hi]
                        ins = nc.vector.tensor_tensor(e, e, band[:, k, lo:hi], ALU.mult)
                    ins.then_inc(b_ready, 1)

                def sums(self, b, turned):
                    dve.wait_ge(packed, b + 1)
                    nc.vector.reciprocal(rr[:], ps_n[:, 0:S]).then_inc(rr_ready, 1)

                def normalise(self, b):
                    wait(dve, y_done, b)
                    for half, bank in enumerate((ps_n, ps_o)):
                        dve.wait_ge(spread_done, 2 * b + half + 1)
                        nc.vector.tensor_tensor(onT[:, 2 * half:2 * half + 2, :], oq[:, 2 * half:2 * half + 2, :],
                                                bank[:].rearrange("p (j s) -> p j s", j=2), ALU.mult).then_inc(on_ready, 1)

                def out(self, b):
                    dve.wait_ge(y_done, b + 1)
                    wait(dve, y_used, b + 1)
                    for t in range(TT):
                        src = ps_p[:, 0, t * D:(t + 1) * D]
                        if not rope:
                            steps.link(nc.vector.tensor_tensor(ytmp[:, t, :], src, bo[:], ALU.add))
                            src = ytmp[:, t, :]
                        xt = x_all[:, b * TT + t, :]
                        ins = nc.vector.tensor_tensor(xt, src, xt, ALU.add)
                    ins.then_inc(y_used, 1)

                def end(self):
                    steps.again()
            program(dve, Vector())


NQ = 8
HALF = 32
KEYS = 64
TOP = 10
EXPERTS = KEYS * KEYS
EV = 32
CHUNK = 16
NCH = P // CHUNK
PAIRS = [TOP // (a + 1) for a in range(TOP)]
NPAIR = sum(PAIRS)
LOW = -3.0e38


def peer_stage(nc, x_all, mean, rstd, ident, d):
    with ExitStack() as ctx:
        r = Room(nc, ctx, "peer")
        sb, ps, sem = r.sb, r.ps, r.sem
        SEL = NQ * TOP
        wq = sb("wq", [P, DC, 2 * NQ * HALF])
        bq = sb("bq", [P, 4])
        keys = sb("keys", [P, 4 * KEYS])
        down = sb("down", [P, DC, EV, P])
        up = sb("up", [P, EV, D])
        iota = sb("iota", [P, P])
        xn = sb("xn", [P, D])
        xnT = sb("xnT", [P, 2, DC, P])
        qT = sb("qT", [P, 4, P])
        s = sb("s", [P, 2 * NQ, KEYS])
        s2 = sb("s2", [P, 2 * NQ, KEYS])
        best = sb("best", [P, 2 * NQ, 16])
        besti = sb("besti", [P, 2 * NQ, 16], U32)
        i64 = sb("i64", [P, NQ, TOP])
        cand = sb("cand", [P, NQ, NPAIR])
        cand2 = sb("cand2", [P, NQ, NPAIR])
        code = sb("code", [P, NQ, NPAIR])
        tv = sb("tv", [P, NQ, 16])
        tp = sb("tp", [P, NQ, 16], U32)
        tpf = sb("tpf", [P, NQ, 16])
        eq = sb("eq", [P, NQ, TOP, NPAIR])
        ef = sb("ef", [P, SEL])
        ei = sb("ei", [P, SEL], I32)
        uvi = sb("uvi", [P, 2, SEL], I32)
        ew = sb("ew", [P, NQ, TOP])
        es = sb("es", [P, NQ, 1])
        er = sb("er", [P, NQ, 1])
        uvw = sb("uvw", [P, 3, SEL])
        uvT = sb("uvT", [P, 2, P], BF16)
        wT = sb("wT", [P, P])
        rest = sb("rest", [P, 2, P])
        parts = sb("parts", [P, 3, P], BF16)
        count = sb("count", [P, P, CHUNK], BF16)
        hot_u = sb("hot_u", [P, 2, P, CHUNK], BF16)
        hot_e = sb("hot_e", [P, 2, EV, CHUNK], BF16)
        hot_v = sb("hot_v", [P, 2, 3, EV, CHUNK], BF16)
        g = sb("g", [P, 2, EV, P])
        warm = sb("warm", [P, 1])

        ps_q = ps("ps_q", [P, 512])
        ps_s = ps("ps_s", [P, 2, 512])
        ps_h = ps("ps_h", [P, 2, 512])
        ps_w = ps("ps_w", [P, 2, 512])
        ps_u = ps("ps_u", [P, D])

        loaded = sem("loaded")
        xn_ready = sem("xn_ready")
        xt_done = sem("xt_done")
        xt_used = sem("xt_used")
        q_done = sem("q_done")
        q_used = sem("q_used")
        s_done = sem("s_done")
        s_used = sem("s_used")
        halves_done = sem("halves_done")
        exp_in = sem("exp_in")
        exp_out = sem("exp_out")
        sel_in = sem("sel_in")
        sel_out = sem("sel_out")
        uvw_ready = sem("uvw_ready")
        uvw_done = sem("uvw_done")
        uvw_used = sem("uvw_used")
        h_done = sem("h_done")
        g_ready = sem("g_ready")
        u_ready = sem("u_ready")
        e_ready = sem("e_ready")
        v_ready = sem("v_ready")
        w_done = sem("w_done")
        gw_ready = sem("gw_ready")
        up_done = sem("up_done")
        x_used = sem("x_used")
        step = sem("step")
        pstep = sem("pstep")
        block = ctx.enter_context(nc.Block())
        NLOAD = 6

        @block.sync
        def _(sp):
            for dst, name in ((wq, "peer_wq"), (down, "peer_down")):
                pat = "(c p) n -> p c n" if name == "peer_wq" else "(c p) v u -> p c v u"
                sp.dma_start(dst[:], d[name].rearrange(pat, p=P)).then_inc(loaded, 16)
            for dst, name in ((bq, "peer_bq"), (keys, "peer_keys"), (up, "peer_up"), (iota, "iota")):
                sp.dma_start(dst[:], d[name]).then_inc(loaded, 16)
            sp.wait_ge(loaded, 16 * NLOAD)

        def run(eng, first, macro):
            first()
            macro(0, 0, False)
            with eng.Fori(0, TILES // 2 - 1) as i:
                macro(2 * i + 1, 1, False)
                macro(2 * i + 2, 0, False)
            macro(TILES - 1, 1, True)

        @block.tensor
        def _(pe):
            pe.wait_ge(loaded, 16 * NLOAD)

            def turn_x(t):
                pe.wait_ge(xn_ready, t + 1)
                wait(pe, uvw_used, t)
                for c in range(DC):
                    mm = nc.tensor.transpose(ps_q[:, c * P:(c + 1) * P], xn[:, c * P:(c + 1) * P], ident[:])
                mm.then_inc(xt_done, 1)

            def queries(t, par):
                pe.wait_ge(xt_used, t + 1)
                for k in range(4):
                    for c in range(DC):
                        mm = nc.tensor.matmul(ps_q[:, k * P:(k + 1) * P], wq[:, c, k * P:(k + 1) * P],
                                              xnT[:, par, c, :], start=(c == 0), stop=(c == DC - 1))
                mm.then_inc(q_done, 1)

            def scores(t):
                pe.wait_ge(q_used, t + 1)
                wait(pe, s_used, t)
                for k in range(4):
                    mm = nc.tensor.matmul(ps_s[:, k // 2, (k % 2) * 256:(k % 2 + 1) * 256], qT[:, k, :], keys[:],
                                          start=True, stop=True)
                mm.then_inc(s_done, 1)

            def hidden(t, par, n):
                pe.wait_ge(xt_used, t + 1)
                wait(pe, g_ready, NCH * t + n - 1)
                for k in range(4):
                    for c in range(DC):
                        mm = nc.tensor.matmul(ps_h[:, n % 2, k * P:(k + 1) * P], down[:, c, 4 * n + k, :],
                                              xnT[:, par, c, :], start=(c == 0), stop=(c == DC - 1))
                mm.then_inc(h_done, 1)

            def weights(t, n):
                pe.wait_ge(u_ready, NCH * t + n + 1)
                pe.wait_ge(v_ready, NCH * t + n + 1)
                wait(pe, gw_ready, NCH * t + n - 1)
                for k in range(CHUNK):
                    for part in range(3):
                        mm = nc.tensor.matmul(ps_w[:, n % 2, k * EV:(k + 1) * EV], hot_u[0:SEL, n % 2, :, k],
                                              hot_v[0:SEL, n % 2, part, :, k], start=(part == 0), stop=(part == 2))
                mm.then_inc(w_done, 1)

            def output(t, par, a, b):
                if a == 0:
                    pe.wait_ge(gw_ready, NCH * (t + 1))
                    wait(pe, x_used, t)
                for v in range(a, b):
                    mm = nc.tensor.matmul(ps_u[:], g[:, par, v, :], up[:, v, :], start=(v == 0), stop=(v == EV - 1))
                if b == EV:
                    mm.then_inc(up_done, 1)

            def turn_uvw(t):
                pe.wait_ge(uvw_ready, t + 1)
                pe.wait_ge(q_used, t + 1)
                for k in range(3):
                    mm = nc.tensor.transpose(ps_q[0:SEL, k * P:(k + 1) * P], uvw[:, k, :], ident[:])
                mm.then_inc(uvw_done, 1)

            def first():
                turn_x(0)
                queries(0, 0)
                scores(0)
                for n in range(NCH):
                    hidden(0, 0, n)
                turn_uvw(0)

            def macro(t, par, last):
                for n in range(NCH):
                    if not last:
                        if n == 0:
                            turn_x(t + 1)
                        if n == 1:
                            queries(t + 1, 1 - par)
                        if n == 2:
                            scores(t + 1)
                        if n >= 2:
                            hidden(t + 1, 1 - par, n - 2)
                    weights(t, n)
                if not last:
                    hidden(t + 1, 1 - par, NCH - 2)
                    hidden(t + 1, 1 - par, NCH - 1)
                output(t, par, 0, 20)
                if not last:
                    turn_uvw(t + 1)
                output(t, par, 20, EV)

            run(pe, first, macro)

        @block.scalar
        def _(act):
            act.wait_ge(loaded, 16 * NLOAD)

            def take_x(t, par):
                act.wait_ge(xt_done, t + 1)
                nc.scalar.activation(xnT[:, par, :, :].rearrange("p c s -> p (c s)"), ps_q[:, 0:DC * P],
                                     ACT.Copy).then_inc(xt_used, 1)

            def take_q(t):
                act.wait_ge(q_done, t + 1)
                for k in range(4):
                    ins = nc.scalar.activation(qT[:, k, :], ps_q[:, k * P:(k + 1) * P], ACT.Identity, bias=bq[:, k:k + 1])
                ins.then_inc(q_used, 1)

            def take_s(t):
                act.wait_ge(s_done, t + 1)
                wait(act, halves_done, t)
                nc.scalar.activation(s[:].rearrange("p g k -> p (g k)"), ps_s[:].rearrange("p a k -> p (a k)"),
                                     ACT.Copy).then_inc(s_used, 1)

            def gelu(t, par, n):
                act.wait_ge(h_done, NCH * t + n + 1)
                wait(act, up_done, t - 1)
                nc.scalar.activation(g[:, par, 4 * n:4 * n + 4, :].rearrange("p v s -> p (v s)"), ps_h[:, n % 2, :],
                                     ACT.Gelu).then_inc(g_ready, 1)

            def exps(t):
                act.wait_ge(exp_in, t + 1)
                nc.scalar.activation(ew[:], ew[:], ACT.Exp).then_inc(exp_out, 1)

            def take_uvw(t):
                act.wait_ge(uvw_done, t + 1)
                wait(act, u_ready, NCH * t)
                wait(act, v_ready, NCH * t)
                nc.scalar.activation(uvT[0:SEL, :, :].rearrange("p k s -> p (k s)"), ps_q[0:SEL, 0:2 * P], ACT.Copy)
                nc.scalar.activation(parts[0:SEL, 0, :], ps_q[0:SEL, 2 * P:3 * P], ACT.Copy)
                nc.scalar.activation(wT[0:SEL, :], ps_q[0:SEL, 2 * P:3 * P], ACT.Copy).then_inc(uvw_used, 1)

            def choices(t, par):
                take_x(t, par)
                take_q(t)
                take_s(t)
                for n in range(NCH):
                    gelu(t, par, n)
                exps(t)
                take_uvw(t)

            def macro(t, par, last):
                if not last:
                    choices(t + 1, 1 - par)

            run(act, lambda: choices(0, 0), macro)

        @block.gpsimd
        def _(pool):
            pool.wait_ge(loaded, 16 * NLOAD)
            steps = Steps(pool, pstep)

            def split(t):
                pool.wait_ge(uvw_used, t + 1)
                steps.link(nc.gpsimd.tensor_tensor(rest[0:SEL, 0, :], wT[0:SEL, :], parts[0:SEL, 0, :], ALU.subtract))
                steps.link(nc.gpsimd.tensor_copy(parts[0:SEL, 1, :], rest[0:SEL, 0, :]))
                steps.link(nc.gpsimd.tensor_tensor(rest[0:SEL, 1, :], rest[0:SEL, 0, :], parts[0:SEL, 1, :], ALU.subtract))
                steps.link(nc.gpsimd.tensor_copy(parts[0:SEL, 2, :], rest[0:SEL, 1, :]))

            def hots(t, n):
                if n == 0:
                    split(t)
                pool.wait_ge(e_ready, NCH * t + n + 1)
                wait(pool, w_done, NCH * t + n - 1)
                for part in range(3):
                    w = parts[0:SEL, part, n * CHUNK:(n + 1) * CHUNK].unsqueeze(1).broadcast_to((SEL, EV, CHUNK))
                    ins = nc.gpsimd.tensor_tensor(hot_v[0:SEL, n % 2, part, :, :], hot_e[0:SEL, n % 2, :, :], w, ALU.mult)
                ins.then_inc(v_ready, 1)

            def select(t):
                pool.wait_ge(sel_in, t + 1)
                value = code[:].unsqueeze(2).broadcast_to((P, NQ, TOP, NPAIR))
                nc.gpsimd.tensor_tensor(eq[:], eq[:], value, ALU.mult).then_inc(sel_out, 1)
                steps.again()

            def first():
                select(0)
                hots(0, 0)

            def macro(t, par, last):
                for n in range(1, NCH):
                    hots(t, n)
                if not last:
                    select(t + 1)
                    hots(t + 1, 0)

            run(pool, first, macro)

        @block.vector
        def _(dve):
            dve.wait_ge(loaded, 16 * NLOAD)
            steps = Steps(dve, step)
            steps.link(nc.vector.tensor_copy(count[:], iota[:].unsqueeze(2).broadcast_to((P, P, CHUNK))))
            steps.again()

            def norm(t):
                wait(dve, xt_done, t)
                nc.vector.tensor_scalar(xn[:], x_all[:, t, :], mean[:, t, :], rstd[:, t, :], ALU.subtract,
                                        ALU.mult).then_inc(xn_ready, 1)

            def hots(t, n):
                if n == 0:
                    dve.wait_ge(uvw_used, t + 1)
                wait(dve, v_ready, NCH * t + n - 1)
                vt = uvT[0:SEL, 1, n * CHUNK:(n + 1) * CHUNK].unsqueeze(1).broadcast_to((SEL, EV, CHUNK))
                nc.vector.tensor_tensor(hot_e[0:SEL, n % 2, :, :], count[0:SEL, 0:EV, :], vt,
                                        ALU.is_equal).then_inc(e_ready, 1)
                wait(dve, w_done, NCH * t + n - 1)
                ut = uvT[0:SEL, 0, n * CHUNK:(n + 1) * CHUNK].unsqueeze(1).broadcast_to((SEL, P, CHUNK))
                nc.vector.tensor_tensor(hot_u[0:SEL, n % 2, :, :], count[0:SEL, :, :], ut,
                                        ALU.is_equal).then_inc(u_ready, 1)

            def weigh(t, par, n):
                if n == 0:
                    dve.wait_ge(g_ready, NCH * (t + 1))
                dve.wait_ge(w_done, NCH * t + n + 1)
                gs = g[:, par, :, n * CHUNK:(n + 1) * CHUNK]
                nc.vector.tensor_tensor(gs, ps_w[:, n % 2, :].rearrange("p (k v) -> p v k", v=EV), gs,
                                        ALU.mult).then_inc(gw_ready, 1)

            def halves(t, a, b):
                gr = range(a, b)
                if a == 0:
                    dve.wait_ge(s_used, t + 1)
                    steps.link(nc.vector.memset(tv[:], 0.0))
                for q in gr:
                    ins = nc.vector.max(best[:, q, 0:8], s[:, q, :])
                steps.link(ins)
                for q in gr:
                    nc.vector.max_index(besti[:, q, 0:8], best[:, q, 0:8], s[:, q, :])
                for q in gr:
                    ins = nc.vector.match_replace(s2[:, q, :], best[:, q, 0:8], s[:, q, :], LOW)
                steps.link(ins)
                for q in gr:
                    ins = nc.vector.max(best[:, q, 8:16], s2[:, q, :])
                steps.link(ins)
                for q in gr:
                    ins = nc.vector.max_index(besti[:, q, 8:16], best[:, q, 8:16], s2[:, q, :])
                steps.link(ins)
                if b == 2 * NQ:
                    nc.vector.tensor_scalar(i64[:], besti[:, 0:2 * NQ:2, 0:TOP], float(KEYS), None,
                                            ALU.mult).then_inc(halves_done, 1)

            def pairs(dst, first, second):
                off = 0
                a = 0
                while a < TOP:
                    nb = PAIRS[a]
                    na = sum(x == nb for x in PAIRS)
                    ins = nc.vector.tensor_tensor(
                        dst[:, :, off:off + na * nb].rearrange("p h (a b) -> p h a b", b=nb),
                        first[:, :, a:a + na].unsqueeze(3).broadcast_to((P, NQ, na, nb)),
                        second[:, :, 0:nb].unsqueeze(2).broadcast_to((P, NQ, na, nb)), ALU.add)
                    off += na * nb
                    a += na
                return ins

            def choose_a(t):
                dve.wait_ge(halves_done, t + 1)
                wait(dve, sel_out, t)
                pairs(cand, best[:, 0:2 * NQ:2, :], best[:, 1:2 * NQ:2, :])
                steps.link(pairs(code, i64[:], besti[:, 1:2 * NQ:2, :]))
                for h in range(NQ):
                    ins = nc.vector.max(tv[:, h, 0:8], cand[:, h, :])
                steps.link(ins)
                for h in range(NQ):
                    nc.vector.max_index(tp[:, h, 0:8], tv[:, h, 0:8], cand[:, h, :])
                for h in range(NQ):
                    ins = nc.vector.match_replace(cand2[:, h, :], tv[:, h, 0:8], cand[:, h, :], LOW)
                steps.link(ins)
                for h in range(NQ):
                    ins = nc.vector.max(tv[:, h, 8:16], cand2[:, h, :])
                steps.link(ins)
                for h in range(NQ):
                    ins = nc.vector.max_index(tp[:, h, 8:16], tv[:, h, 8:16], cand2[:, h, :])
                steps.link(ins)
                steps.link(nc.vector.tensor_copy(tpf[:], tp[:]))
                where = tpf[:, :, 0:TOP].unsqueeze(3).broadcast_to((P, NQ, TOP, NPAIR))
                number = iota[:, 0:NPAIR].unsqueeze(1).unsqueeze(1).broadcast_to((P, NQ, TOP, NPAIR))
                nc.vector.tensor_tensor(eq[:], number, where, ALU.is_equal).then_inc(sel_in, 1)
                nc.vector.tensor_tensor(ew[:], tv[:, :, 0:TOP], tv[:, :, 0:1].broadcast_to((P, NQ, TOP)),
                                        ALU.subtract).then_inc(exp_in, 1)

            def choose_b(t):
                dve.wait_ge(exp_out, t + 1)
                wait(dve, uvw_done, t)
                steps.link(nc.vector.tensor_reduce(es[:], ew[:], AX.X, ALU.add))
                steps.link(nc.vector.reciprocal(er[:], es[:]))
                nc.vector.tensor_tensor(uvw[:, 2, :].rearrange("p (h k) -> p h k", h=NQ), ew[:],
                                        er[:].broadcast_to((P, NQ, TOP)), ALU.mult)
                dve.wait_ge(sel_out, t + 1)
                steps.link(nc.vector.tensor_reduce(ef[:].rearrange("p (h k) -> p h k", h=NQ), eq[:], AX.X, ALU.add))
                steps.link(nc.vector.tensor_copy(ei[:], ef[:]))
                nc.vector.tensor_scalar(uvi[:, 0, :], ei[:], 5, None, ALU.logical_shift_right)
                steps.link(nc.vector.tensor_scalar(uvi[:, 1, :], ei[:], EV - 1, None, ALU.bitwise_and))
                nc.vector.tensor_copy(uvw[:, 0:2, :], uvi[:]).then_inc(uvw_ready, 1)
                dve.wait_ge(uvw_ready, t + 1)

            def add(t):
                dve.wait_ge(up_done, t + 1)
                nc.vector.tensor_tensor(x_all[:, t, :], ps_u[:], x_all[:, t, :], ALU.add).then_inc(x_used, 1)

            def first():
                norm(0)
                for a in range(0, 2 * NQ, 4):
                    halves(0, a, a + 4)
                choose_a(0)
                choose_b(0)
                hots(0, 0)
                steps.again()

            def macro(t, par, last):
                if not last:
                    norm(t + 1)
                if not (isinstance(t, int) and t == 0):
                    add(t - 1)
                for n in range(NCH):
                    if n < NCH - 1:
                        hots(t, n + 1)
                    if n >= 1:
                        weigh(t, par, n - 1)
                    if n >= 3 and not last:
                        halves(t + 1, 3 * (n - 3), 3 * (n - 2))
                weigh(t, par, NCH - 1)
                if not last:
                    halves(t + 1, 15, 16)
                    choose_a(t + 1)
                    choose_b(t + 1)
                    hots(t + 1, 0)
                if last:
                    add(t)
                steps.again()

            run(dve, first, macro)


def bidaf_stage(nc, x_all, mean, rstd, ident, d):
    with ExitStack() as ctx:
        r = Room(nc, ctx, "bidaf")
        NS = 2
        wl = r.sb("wl", [P, 4 * DC, D])
        bl = r.sb("bl", [P, D])
        vec = r.sb("vec", [P, 3, DC])
        b3 = r.sb("b3", [1, 3])
        bsum = r.sb("bsum", [1, 1])
        ones = r.sb("ones", [1, P])
        warm = r.sb("warm", [P, 1])
        loaded = r.sem("loaded")
        ready = r.sem("ready")
        step = r.sem("step")
        astep = r.sem("astep")


        class Stream:
            def __init__(self, k):
                self.k = k
                self.q = r.sb(f"q{k}", [P, D])
                self.c = r.sb(f"c{k}", [P, TT, D])
                self.cT = r.sb(f"cT{k}", [P, DC, S])
                self.qT = r.sb(f"qT{k}", [P, DC, CTX])
                self.m = r.sb(f"m{k}", [P, DC, CTX])
                self.qrow = r.sb(f"qrow{k}", [1, CTX])
                self.nmax = r.sb(f"nmax{k}", [P, TT])
                self.prob = r.sb(f"prob{k}", [P, TT, CTX])
                self.rs = r.sb(f"rs{k}", [P, TT])
                self.ri = r.sb(f"ri{k}", [P, TT])
                self.probT = r.sb(f"probT{k}", [P, S])
                self.negtop = r.sb(f"negtop{k}", [1, 1])
                self.erow = r.sb(f"erow{k}", [1, S])
                self.es = r.sb(f"es{k}", [1, 1])
                self.ei = r.sb(f"ei{k}", [1, 1])
                self.arow = r.sb(f"arow{k}", [1, S])
                self.acol = r.sb(f"acol{k}", [P, TT])
                self.q2c = r.sb(f"q2c{k}", [P, DC])
                self.wad = r.sb(f"wad{k}", [P, DC, D])
                self.aT = r.sb(f"aT{k}", [P, DC, S])
                self.caT = r.sb(f"caT{k}", [P, DC, S])
                self.z = r.sb(f"z{k}", [P, TT, D])
                self.p0 = r.ps(f"p0{k}", [P, 512])
                self.p1 = r.ps(f"p1{k}", [P, 512])
                self.p2 = r.ps(f"p2{k}", [P, 512])
                self.p3 = r.ps(f"p3{k}", [P, 512])
                self.q_in = r.sem(f"q_in{k}")
                self.c_ready = r.sem(f"c_ready{k}")
                self.t_done = r.sem(f"t_done{k}")
                self.t_used = r.sem(f"t_used{k}")
                self.m_ready = r.sem(f"m_ready{k}")
                self.row_done = r.sem(f"row_done{k}")
                self.row_ready = r.sem(f"row_ready{k}")
                self.s_done = r.sem(f"s_done{k}")
                self.max_ready = r.sem(f"max_ready{k}")
                self.exp_ready = r.sem(f"exp_ready{k}")
                self.prob_ready = r.sem(f"prob_ready{k}")
                self.top_done = r.sem(f"top_done{k}")
                self.top_ready = r.sem(f"top_ready{k}")
                self.eexp_ready = r.sem(f"eexp_ready{k}")
                self.arow_ready = r.sem(f"arow_ready{k}")
                self.acol_done = r.sem(f"acol_done{k}")
                self.acol_ready = r.sem(f"acol_ready{k}")
                self.q2c_done = r.sem(f"q2c_done{k}")
                self.wad_ready = r.sem(f"wad_ready{k}")
                self.pt_done = r.sem(f"pt_done{k}")
                self.pt_used = r.sem(f"pt_used{k}")
                self.a_done = r.sem(f"a_done{k}")
                self.a_used = r.sem(f"a_used{k}")
                self.ca_ready = r.sem(f"ca_ready{k}")
                self.z_done = r.sem(f"z_done{k}")
                self.z_used = r.sem(f"z_used{k}")

        streams = [Stream(k) for k in range(NS)]
        block = ctx.enter_context(nc.Block())
        NLOAD = 4

        def each(eng, parts):
            def pair(n):
                for part in parts:
                    for z in streams:
                        part(z, n, NS * n + z.k)
            pair(0)
            with eng.Fori(1, B // NS) as n:
                pair(n)

        @block.sync
        def _(sp):
            sp.dma_start(wl[:], d["bidaf_wl"].rearrange("(c p) n -> p c n", p=P)).then_inc(loaded, 16)
            sp.dma_start(bl[:], d["bidaf_bl"].partition_broadcast(P)).then_inc(loaded, 16)
            sp.dma_start(vec[:], d["bidaf_vec"]).then_inc(loaded, 16)
            sp.dma_start(b3[:], d["bidaf_b"]).then_inc(loaded, 16)

            def fetch(z, n, b):
                wait(sp, z.a_done, n)
                sp.wait_ge(loaded, 16 * NLOAD)
                sp.dma_start(z.q[0:CTX, :], d["ctx"][b]).then_inc(z.q_in, 16)
            each(sp, [fetch])
            for z in streams:
                sp.wait_ge(z.q_in, 16 * (B // NS))

        @block.tensor
        def _(pe):
            pe.wait_ge(loaded, 16 * NLOAD)
            pe.wait_ge(ready, 1)

            def turn(z, n, b):
                pe.wait_ge(z.c_ready, n + 1)
                pe.wait_ge(z.q_in, 16 * (n + 1))
                wait(pe, z.a_used, n)
                wait(pe, z.acol_ready, n)
                for t in range(TT):
                    for c in range(DC):
                        nc.tensor.transpose(z.p0[:, c * S + t * P:c * S + (t + 1) * P], z.c[:, t, c * P:(c + 1) * P], ident[:])
                for c in range(DC):
                    mm = nc.tensor.transpose(z.p1[:, c * CTX:(c + 1) * CTX], z.q[0:CTX, c * P:(c + 1) * P],
                                             ident[0:CTX, 0:CTX])
                mm.then_inc(z.t_done, 1)

            def row(z, n, b):
                pe.wait_ge(z.t_used, n + 1)
                wait(pe, z.wad_ready, n)
                for c in range(DC):
                    mm = nc.tensor.matmul(z.p2[0:1, 0:CTX], vec[:, 2, c:c + 1], z.qT[:, c, :], start=(c == 0),
                                          stop=(c == DC - 1))
                mm.then_inc(z.row_done, 1)

            def scores(z, n, b):
                pe.wait_ge(z.row_ready, n + 1)
                pe.wait_ge(z.m_ready, n + 1)
                for t in range(TT):
                    for c in range(DC):
                        nc.tensor.matmul(z.p1[:, t * CTX:(t + 1) * CTX], z.cT[:, c, t * P:(t + 1) * P], z.m[:, c, :],
                                         start=(c == 0), stop=False)
                    mm = nc.tensor.matmul(z.p1[:, t * CTX:(t + 1) * CTX], ones[:], z.qrow[:], start=False, stop=True)
                mm.then_inc(z.s_done, 1)

            def top(z, n, b):
                pe.wait_ge(z.max_ready, n + 1)
                for t in range(TT):
                    mm = nc.tensor.matmul(z.p2[0:1, t * P:(t + 1) * P], z.nmax[:, t:t + 1], ident[:], start=True, stop=True)
                mm.then_inc(z.top_done, 1)

            def turn_prob(z, n, b):
                pe.wait_ge(z.prob_ready, n + 1)
                wait(pe, z.z_used, n)
                for t in range(TT):
                    mm = nc.tensor.transpose(z.p3[0:CTX, t * P:(t + 1) * P], z.prob[:, t, :], ident[:])
                mm.then_inc(z.pt_done, 1)

            def attend(z, n, b):
                pe.wait_ge(z.pt_used, n + 1)
                for c in range(DC):
                    mm = nc.tensor.matmul(z.p0[:, c * S:(c + 1) * S], z.q[0:CTX, c * P:(c + 1) * P], z.probT[0:CTX, :],
                                          start=True, stop=True)
                mm.then_inc(z.a_done, 1)

            def col(z, n, b):
                pe.wait_ge(z.arow_ready, n + 1)
                for t in range(TT):
                    mm = nc.tensor.matmul(z.p1[:, t:t + 1], z.arow[0:1, t * P:(t + 1) * P], ones[0:1, 0:1], start=True, stop=True)
                mm.then_inc(z.acol_done, 1)

            def q2c(z, n, b):
                pe.wait_ge(z.acol_ready, n + 1)
                for c in range(DC):
                    for t in range(TT):
                        mm = nc.tensor.matmul(z.p2[:, c:c + 1], z.c[:, t, c * P:(c + 1) * P], z.acol[:, t:t + 1],
                                              start=(t == 0), stop=(t == TT - 1))
                mm.then_inc(z.q2c_done, 1)

            def project(z, n, b):
                pe.wait_ge(z.wad_ready, n + 1)
                pe.wait_ge(z.a_used, n + 1)
                pe.wait_ge(z.ca_ready, n + 1)
                for t in range(TT):
                    ops = [(z.cT, z.wad, 0), (z.aT, wl, DC), (z.caT, wl, 2 * DC)]
                    for k, (lhs, w, off) in enumerate(ops):
                        for c in range(DC):
                            mm = nc.tensor.matmul(z.p3[:, t * D:(t + 1) * D], lhs[:, c, t * P:(t + 1) * P], w[:, off + c, :],
                                                  start=(k == 0 and c == 0), stop=(k == 2 and c == DC - 1))
                mm.then_inc(z.z_done, 1)

            each(pe, [turn, row, scores, top, turn_prob, attend, col, q2c, project])

        @block.scalar
        def _(act):
            act.wait_ge(loaded, 16 * NLOAD)
            act.wait_ge(ready, 1)
            nc.scalar.activation(warm[:], ident[:, 0:1], ACT.Exp)

            def take(z, n, b):
                act.wait_ge(z.t_done, n + 1)
                wait(act, z.z_done, n)
                nc.scalar.activation(z.cT[:].rearrange("p c s -> p (c s)"), z.p0[:], ACT.Copy)
                nc.scalar.activation(z.qT[:].rearrange("p c s -> p (c s)"), z.p1[:, 0:DC * CTX], ACT.Copy).then_inc(z.t_used, 1)

            def exps(z, n, b):
                act.wait_ge(z.max_ready, n + 1)
                for t in range(TT):
                    ins = nc.scalar.activation(z.prob[:, t, :], z.p1[:, t * CTX:(t + 1) * CTX], ACT.Exp,
                                               bias=z.nmax[:, t:t + 1], accum_out=z.rs[:, t:t + 1])
                ins.then_inc(z.exp_ready, 1)

            def eexp(z, n, b):
                act.wait_ge(z.top_ready, n + 1)
                nc.scalar.activation(z.erow[:], z.p2[0:1, 0:S], ACT.Exp, bias=z.negtop[:], scale=-1.0,
                                     accum_out=z.es[:]).then_inc(z.eexp_ready, 1)

            def take_prob(z, n, b):
                act.wait_ge(z.pt_done, n + 1)
                nc.scalar.activation(z.probT[0:CTX, :], z.p3[0:CTX, 0:S], ACT.Copy).then_inc(z.pt_used, 1)

            def take_a(z, n, b):
                act.wait_ge(z.a_done, n + 1)
                nc.scalar.activation(z.aT[:].rearrange("p c s -> p (c s)"), z.p0[:], ACT.Copy).then_inc(z.a_used, 1)

            each(act, [take, exps, eexp, take_prob, take_a])

        @block.vector
        def _(dve):
            dve.wait_ge(loaded, 16 * NLOAD)
            steps = Steps(dve, step)
            steps.link(nc.vector.tensor_reduce(bsum[:], b3[:], AX.X, ALU.add))
            nc.vector.memset(ones[:], 1.0).then_inc(ready, 1)
            dve.wait_ge(ready, 1)
            steps.again()

            def norm(z, n, b):
                wait(dve, z.q2c_done, n)
                for t in range(TT):
                    ins = nc.vector.tensor_scalar(z.c[:, t, :], x_all[:, b * TT + t, :], mean[:, b * TT + t, :],
                                                  rstd[:, b * TT + t, :], ALU.subtract, ALU.mult)
                ins.then_inc(z.c_ready, 1)

            def make_m(z, n, b):
                dve.wait_ge(z.t_used, n + 1)
                wait(dve, z.s_done, n)
                for c in range(DC):
                    ins = nc.vector.tensor_scalar(z.m[:, c, :], z.qT[:, c, :], vec[:, 0, c:c + 1],
                                                  vec[:, 1, c:c + 1], ALU.mult, ALU.add)
                ins.then_inc(z.m_ready, 1)

            def make_row(z, n, b):
                dve.wait_ge(z.row_done, n + 1)
                nc.vector.tensor_scalar(z.qrow[:], z.p2[0:1, 0:CTX], bsum[:], None, ALU.add).then_inc(z.row_ready, 1)

            def rowmax(z, n, b):
                dve.wait_ge(z.s_done, n + 1)
                nc.vector.tensor_reduce(z.nmax[:], z.p1[:, 0:TT * CTX].rearrange("p (t q) -> p t q", t=TT), AX.X,
                                        ALU.max, negate=True).then_inc(z.max_ready, 1)

            def find_top(z, n, b):
                dve.wait_ge(z.top_done, n + 1)
                nc.vector.tensor_reduce(z.negtop[:], z.p2[0:1, 0:S], AX.X, ALU.min).then_inc(z.top_ready, 1)

            def normalise(z, n, b):
                dve.wait_ge(z.exp_ready, n + 1)
                steps.link(nc.vector.reciprocal(z.ri[:], z.rs[:]))
                for t in range(TT):
                    ins = nc.vector.tensor_scalar(z.prob[:, t, :], z.prob[:, t, :], z.ri[:, t:t + 1], None, ALU.mult)
                ins.then_inc(z.prob_ready, 1)

            def batch_row(z, n, b):
                dve.wait_ge(z.eexp_ready, n + 1)
                steps.link(nc.vector.reciprocal(z.ei[:], z.es[:]))
                nc.vector.tensor_scalar(z.arow[:], z.erow[:], z.ei[:], None, ALU.mult).then_inc(z.arow_ready, 1)

            def take_col(z, n, b):
                dve.wait_ge(z.acol_done, n + 1)
                nc.vector.tensor_copy(z.acol[:], z.p1[:, 0:TT]).then_inc(z.acol_ready, 1)

            def make_wad(z, n, b):
                dve.wait_ge(z.q2c_done, n + 1)
                steps.link(nc.vector.tensor_copy(z.q2c[:], z.p2[:, 0:DC]))
                for c in range(DC):
                    ins = nc.vector.scalar_tensor_tensor(z.wad[:, c, :], wl[:, 3 * DC + c, :], z.q2c[:, c:c + 1],
                                                         wl[:, c, :], ALU.mult, ALU.add)
                ins.then_inc(z.wad_ready, 1)

            def product(z, n, b):
                dve.wait_ge(z.a_used, n + 1)
                nc.vector.tensor_tensor(z.caT[:], z.aT[:], z.cT[:], ALU.mult).then_inc(z.ca_ready, 1)

            def add(z, n, b):
                dve.wait_ge(z.z_done, n + 1)
                wait(dve, z.z_used, n)
                steps.link(nc.vector.tensor_tensor(z.z[:], z.p3[:].rearrange("p (t c) -> p t c", t=TT),
                                                   bl[:].unsqueeze(1).broadcast_to((P, TT, D)), ALU.add))
                for t in range(TT):
                    xt = x_all[:, b * TT + t, :]
                    ins = nc.vector.tensor_tensor(xt, z.z[:, t, :], xt, ALU.add)
                ins.then_inc(z.z_used, 1)
                if z.k == NS - 1:
                    steps.again()

            each(dve, [norm, make_m, make_row, rowmax, find_top, normalise, batch_row, product, take_col, make_wad, add])


E = 8
HID = 4 * D
HC = HID // P
GT = 4
YB = GT // 2


def moe_stage(nc, x_all, mean, rstd, ident, d):
    with ExitStack() as ctx:
        r = Room(nc, ctx, "moe")
        sb, ps, sem = r.sb, r.ps, r.sem
        w1 = sb("w1", [P, E, DC, HID])
        w2 = sb("w2", [P, E, HC, D])
        b1 = sb("b1", [P, E, HC])
        b2 = sb("b2", [E, D])
        wr = sb("wr", [P, DC, E])
        br = sb("br", [P, E])
        iota = sb("iota", [P, P])
        xn = sb("xn", [P, GT, D])
        xnT = sb("xnT", [P, DC, GT * P])
        hT = sb("hT", [P, HC, GT * P])
        logit = sb("logit", [P, GT, E])
        top = sb("top", [P, GT, 8])
        topi = sb("topi", [P, GT, 8], U32)
        topf = sb("topf", [P, GT, 8])
        hot = sb("hot", [P, GT, 2, E])
        ew = sb("ew", [P, GT, E])
        es = sb("es", [P, GT, 1])
        er = sb("er", [P, GT, 1])
        rw = sb("rw", [P, GT, E])
        rwT = sb("rwT", [E, GT, P])
        ps_t = ps("ps_t", [P, 2, 512])
        ps_h = ps("ps_h", [P, 2, 512])
        ps_y = ps("ps_y", [P, 4, D])
        ps_r = ps("ps_r", [P, 512])
        ps_b = ps("ps_b", [P, D])

        loaded = sem("loaded")
        loaded2 = sem("loaded2")
        xn_ready = sem("xn_ready")
        xt_done = sem("xt_done")
        xt_used = sem("xt_used")
        r_done = sem("r_done")
        exp_in = sem("exp_in")
        exp_out = sem("exp_out")
        rw_ready = sem("rw_ready")
        rwt_done = sem("rwt_done")
        rwt_used = sem("rwt_used")
        b_done = sem("b_done")
        b_used = sem("b_used")
        h_done = sem("h_done")
        h_used = sem("h_used")
        y_done = sem("y_done")
        y_used = sem("y_used")
        stored = sem("stored")
        step = sem("step")
        block = ctx.enter_context(nc.Block())
        NLOAD = 6
        G = TILES // GT

        @block.sync
        def _(sp):
            sp.dma_start(wr[:], d["moe_wr"].rearrange("(c p) n -> p c n", p=P)).then_inc(loaded, 16)
            sp.dma_start(br[:], d["moe_br"].partition_broadcast(P)).then_inc(loaded, 16)
            sp.dma_start(b1[:], d["moe_b1"]).then_inc(loaded, 16)
            sp.dma_start(b2[:], d["moe_b2"]).then_inc(loaded, 16)
            sp.dma_start(iota[:], d["iota"]).then_inc(loaded, 16)
            sp.wait_ge(loaded, 16 * 5)
            for e in range(E):
                sp.dma_start(w1[:, e], d["moe_w1"][e].rearrange("(c p) n -> p c n", p=P)).then_inc(loaded2, 16)
                sp.dma_start(w2[:, e], d["moe_w2"][e].rearrange("(c p) n -> p c n", p=P)).then_inc(loaded2, 16)
                sp.wait_ge(loaded2, 32 * (e + 1))
            out = d["out"].rearrange("b (t p) c -> p (b t) c", p=P)
            with sp.Fori(0, G) as g:
                sp.wait_ge(y_used, YB * E * (g + 1))
                sp.wait_ge(loaded, 16 * 5)
                sp.dma_start(out[:, bass.ds(g * GT, GT), :], x_all[:, bass.ds(g * GT, GT), :]).then_inc(stored, 16)
            sp.wait_ge(stored, 16 * G)

        def loop(eng, body):
            body(0)
            with eng.Fori(1, G) as g:
                body(g)

        @block.tensor
        def _(pe):
            pe.wait_ge(loaded, 16 * 5)

            def body(g):
                pe.wait_ge(xn_ready, g + 1)
                for c in range(DC):
                    for t in range(GT):
                        mm = nc.tensor.transpose(ps_t[:, c, t * P:(t + 1) * P], xn[:, t, c * P:(c + 1) * P], ident[:])
                mm.then_inc(xt_done, 1)
                pe.wait_ge(xt_used, g + 1)
                wait(pe, rwt_used, g)
                for t in range(GT):
                    for c in range(DC):
                        mm = nc.tensor.matmul(ps_r[:, t * E:(t + 1) * E], xnT[:, c, t * P:(t + 1) * P], wr[:, c, :],
                                              start=(c == 0), stop=(c == DC - 1))
                mm.then_inc(r_done, 1)

                def hidden(e):
                    if isinstance(g, int) and g == 0:
                        pe.wait_ge(loaded2, 32 * (e + 1))
                    for m in range(HC):
                        n = HC * E * g + HC * e + m
                        wait(pe, h_used, n - 1)
                        for c in range(DC):
                            mm = nc.tensor.matmul(ps_h[:, m % 2, :], w1[:, e, c, m * P:(m + 1) * P], xnT[:, c, :],
                                                  start=(c == 0), stop=(c == DC - 1))
                        mm.then_inc(h_done, 1)

                def outputs(e):
                    pe.wait_ge(h_used, HC * E * g + HC * (e + 1))
                    for t in range(GT):
                        if t % 2 == 0:
                            wait(pe, y_used, YB * (E * g + e - 1) + t // 2 + 1)
                        for m in range(HC):
                            mm = nc.tensor.matmul(ps_y[:, t, :], hT[:, m, t * P:(t + 1) * P], w2[:, e, m, :],
                                                  start=(m == 0), stop=(m == HC - 1))
                        if t % 2 == 1:
                            mm.then_inc(y_done, 1)

                for e in range(E):
                    hidden(e)
                    if e == 0:
                        pe.wait_ge(rw_ready, g + 1)
                        for t in range(GT):
                            mm = nc.tensor.transpose(ps_r[0:E, t * P:(t + 1) * P], rw[:, t, :], ident[:])
                        mm.then_inc(rwt_done, 1)
                        pe.wait_ge(rwt_used, g + 1)
                        for t in range(GT):
                            wait(pe, b_used, GT * g + t)
                            nc.tensor.matmul(ps_b[:], rwT[:, t, :], b2[:], start=True, stop=True).then_inc(b_done, 1)
                    outputs(e)

            loop(pe, body)

        @block.scalar
        def _(act):
            act.wait_ge(loaded, 16 * 5)
            nc.scalar.activation(es[:, 0, :], ident[:, 0:1], ACT.Exp)

            def body(g):
                act.wait_ge(xt_done, g + 1)
                for c in range(DC):
                    ins = nc.scalar.activation(xnT[:, c, :], ps_t[:, c, :], ACT.Copy)
                ins.then_inc(xt_used, 1)

                def relus(e):
                    for m in range(HC):
                        act.wait_ge(h_done, HC * E * g + HC * e + m + 1)
                        nc.scalar.activation(hT[:, m, :], ps_h[:, m % 2, :], ACT.Relu,
                                             bias=b1[:, e, m:m + 1]).then_inc(h_used, 1)
                act.wait_ge(exp_in, g + 1)
                nc.scalar.activation(ew[:], ew[:], ACT.Exp).then_inc(exp_out, 1)
                relus(0)
                act.wait_ge(rwt_done, g + 1)
                nc.scalar.activation(rwT[:].rearrange("p t s -> p (t s)"), ps_r[0:E, :], ACT.Copy).then_inc(rwt_used, 1)
                for e in range(1, E):
                    relus(e)

            loop(act, body)

        @block.vector
        def _(dve):
            dve.wait_ge(loaded, 16 * 5)
            steps = Steps(dve, step)

            def body(g):
                wait(dve, xt_done, g)
                for t in range(GT):
                    ins = nc.vector.tensor_scalar(xn[:, t, :], x_all[:, g * GT + t, :], mean[:, g * GT + t, :],
                                                  rstd[:, g * GT + t, :], ALU.subtract, ALU.mult)
                ins.then_inc(xn_ready, 1)
                dve.wait_ge(r_done, g + 1)
                steps.link(nc.vector.tensor_tensor(logit[:], ps_r[:, 0:GT * E].rearrange("p (t e) -> p t e", e=E),
                                                   br[:].unsqueeze(1).broadcast_to((P, GT, E)), ALU.add))
                for t in range(GT):
                    ins = nc.vector.max(top[:, t, :], logit[:, t, :])
                steps.link(ins)
                nc.vector.tensor_tensor(ew[:], logit[:], top[:, :, 0:1].broadcast_to((P, GT, E)),
                                        ALU.subtract).then_inc(exp_in, 1)
                for t in range(GT):
                    ins = nc.vector.max_index(topi[:, t, :], top[:, t, :], logit[:, t, :])
                steps.link(ins)
                steps.link(nc.vector.tensor_copy(topf[:], topi[:]))
                steps.link(nc.vector.tensor_tensor(hot[:], iota[:, 0:E].unsqueeze(1).unsqueeze(1).broadcast_to((P, GT, 2, E)),
                                                   topf[:, :, 0:2].unsqueeze(3).broadcast_to((P, GT, 2, E)), ALU.is_equal))
                steps.link(nc.vector.tensor_tensor(hot[:, :, 0, :], hot[:, :, 0, :], hot[:, :, 1, :], ALU.add))
                dve.wait_ge(exp_out, g + 1)
                steps.link(nc.vector.tensor_tensor(ew[:], ew[:], hot[:, :, 0, :], ALU.mult))
                steps.link(nc.vector.tensor_reduce(es[:], ew[:], AX.X, ALU.add))
                steps.link(nc.vector.reciprocal(er[:], es[:]))
                wait(dve, y_used, YB * E * g)
                nc.vector.tensor_tensor(rw[:], ew[:], er[:].broadcast_to((P, GT, E)), ALU.mult).then_inc(rw_ready, 1)
                for t in range(GT):
                    dve.wait_ge(b_done, GT * g + t + 1)
                    xt = x_all[:, g * GT + t, :]
                    nc.vector.tensor_tensor(xt, ps_b[:], xt, ALU.add).then_inc(b_used, 1)
                dve.wait_ge(rw_ready, g + 1)
                dve.wait_ge(b_used, GT * (g + 1))
                for e in range(E):
                    for t in range(GT):
                        if t % 2 == 0:
                            dve.wait_ge(y_done, YB * (E * g + e) + t // 2 + 1)
                            if e > 0:
                                dve.wait_ge(y_used, YB * (E * g + e - 1) + t // 2 + 1)
                        xt = x_all[:, g * GT + t, :]
                        ins = nc.vector.scalar_tensor_tensor(xt, ps_y[:, t, :], rw[:, t, e:e + 1], xt, ALU.mult, ALU.add)
                        if t % 2 == 1:
                            ins.then_inc(y_used, 1)
                steps.again()

            loop(dve, body)



def _rows_first(np, wt):
    v = wt.reshape(wt.shape[:-1] + (DC, HEADS // DC, HD))
    return np.swapaxes(v, -1, -2).reshape(wt.shape)


def _slot_rows(np, wt):
    out = np.zeros((HEADS, SLOT, wt.shape[1]), wt.dtype)
    out[:, :HD] = wt.reshape(HEADS, HD, wt.shape[1])
    return out.reshape(HEADS * SLOT, wt.shape[1])


def _chunk_bias(np, b):
    return _rows_first(np, b).reshape(DC, P).T


def _pairs_swapped(wt):
    return wt.reshape(wt.shape[0], -1, 2)[:, :, ::-1].reshape(wt.shape)


def _constants(np):
    f = np.float32
    c = {"ident": np.eye(P, dtype=f), "iota": np.tile(np.arange(P, dtype=f), (P, 1))}
    freq = (1.0 / np.power(f(10000.0), np.arange(0, HD, 2, dtype=f) / f(HD))).astype(f)
    angle = np.arange(S, dtype=f)[None, :] * freq[:, None]
    cos, sin = np.cos(angle).astype(f), np.sin(angle).astype(f)
    ct, st = np.zeros((HD, S), f), np.zeros((HD, S), f)
    ct[0:HD:2], ct[1:HD:2] = cos, cos
    st[0:HD:2], st[1:HD:2] = -sin, sin
    ct, st = np.repeat(ct, HEADS // DC, 0), np.repeat(st, HEADS // DC, 0)
    c |= {"cosk": ct, "sink": st, "cosq": ct * f(0.25), "sinq": st * f(0.25)}
    far = np.full((P, P), -1e30, f)
    c["mask"] = np.concatenate([np.triu(far, 1), np.tril(far, -1)])
    row, col = np.arange(P)[:, None], np.arange(P)[None, :]
    c["pack"] = (row == col[:, :SLOT] % 4 * SLOT + HD).astype(f)
    c["spread"] = np.stack([row == SLOT * j + col // SLOT for j in range(4)], 1).astype(f)
    i = np.arange(S)
    near = np.abs(i[:, None] - i[None, :]) <= 2
    c["band"] = np.where(near, f(np.exp(0.1)), f(1.0)).astype(f)
    return c


def _lay_out(np, v):
    a = _constants(np)
    a["x"] = v["x"]
    a["ctx"] = v["ctx_1024"]
    wk, wq, wv = (m.T for m in np.split(v["L0_attn_W_KQV"], 3, axis=0))
    a |= {"causal_wq": _rows_first(np, wq), "causal_wk": _rows_first(np, wk), "causal_wv": wv,
          "causal_wqs": _rows_first(np, _pairs_swapped(wq)), "causal_wks": _rows_first(np, _pairs_swapped(wk)),
          "causal_wo": _slot_rows(np, v["L0_attn_W_O"].T)}
    for kind, name in (("cross", "L0_xattn"), ("band", "L1_attn")):
        a |= {f"{kind}_wq": _rows_first(np, v[f"{name}_Wq"].T), f"{kind}_wk": _rows_first(np, v[f"{name}_Wk"].T),
              f"{kind}_wv": v[f"{name}_Wv"].T, f"{kind}_wo": _slot_rows(np, v[f"{name}_Wo"].T),
              f"{kind}_bq": _chunk_bias(np, v[f"{name}_bq"]), f"{kind}_bk": _chunk_bias(np, v[f"{name}_bk"]),
              f"{kind}_bv": v[f"{name}_bv"], f"{kind}_bo": v[f"{name}_bo"]}
    a["band_bias"] = _chunk_bias(np, v["L1_attn_ocr_bias"])
    k1, k2 = v["L0_ffn_K1"].T, v["L0_ffn_K2"].T
    keys = np.zeros((4, HALF, 4, KEYS), k1.dtype)
    for n in range(4):
        keys[n, :, n, :] = (k1, k2)[n % 2]
    a |= {"peer_wq": v["L0_ffn_Wq"], "peer_bq": v["L0_ffn_bq"].reshape(4, P).T, "peer_keys": keys.reshape(P, 4 * KEYS),
          "peer_down": v["L0_ffn_W_down"][:EXPERTS].reshape(P, EV, D).transpose(2, 1, 0),
          "peer_up": v["L0_ffn_W_up"][:EXPERTS].reshape(P, EV, D)}
    wl = v["L1_xattn_W_l"].T
    a |= {"bidaf_wl": wl, "bidaf_bl": v["L1_xattn_b_l"],
          "bidaf_vec": np.stack([v["L1_xattn_w_cq"], v["L1_xattn_w_c"], v["L1_xattn_w_q"]]).reshape(3, DC, P).transpose(2, 0, 1),
          "bidaf_b": np.stack([v["L1_xattn_b_cq"], v["L1_xattn_b_c"], v["L1_xattn_b_q"]]).reshape(1, 3)}
    a |= {"moe_w1": v["L1_ffn_W1"], "moe_w2": v["L1_ffn_W2"], "moe_b2": v["L1_ffn_b2"], "moe_wr": v["L1_ffn_Wr"],
          "moe_br": v["L1_ffn_br"], "moe_b1": v["L1_ffn_b1"].reshape(E, HC, P).transpose(2, 0, 1)}
    return {k: np.ascontiguousarray(x) for k, x in a.items()}



def decoder(nc, d):
    with ExitStack() as ctx:
        def sb(name, shape):
            return ctx.enter_context(nc.sbuf_tensor(name, shape, F32))
        x_all = sb("x_all", [P, TILES, D])
        ident = sb("ident", [P, P])
        mean = sb("mean", [P, TILES, 1])
        rstd = sb("rstd", [P, TILES, 1])
        load_stage(nc, x_all, ident, d)
        norm_stage(nc, "norm0", x_all, mean, rstd)
        attention_stage(nc, "causal", x_all, mean, rstd, ident, d)
        norm_stage(nc, "norm1", x_all, mean, rstd)
        attention_stage(nc, "cross", x_all, mean, rstd, ident, d)
        norm_stage(nc, "norm2", x_all, mean, rstd)
        peer_stage(nc, x_all, mean, rstd, ident, d)
        norm_stage(nc, "norm3", x_all, mean, rstd)
        attention_stage(nc, "band", x_all, mean, rstd, ident, d)
        norm_stage(nc, "norm4", x_all, mean, rstd)
        bidaf_stage(nc, x_all, mean, rstd, ident, d)
        norm_stage(nc, "norm5", x_all, mean, rstd)
        moe_stage(nc, x_all, mean, rstd, ident, d)


def kernel(**inputs):
    import numpy as np
    import concourse.bacc as bacc
    from concourse.bass_utils import run_bass_kernel_spmd

    arrays = {f"in_{k}": v for k, v in _lay_out(np, {k: np.asarray(v) for k, v in inputs.items()}).items()}
    nc = bacc.Bacc("TRN2", target_bir_lowering=False, num_devices=1)
    d = {k[3:]: nc.dram_tensor(k, v.shape, mybir.dt.from_np(v.dtype), kind="ExternalInput").ap() for k, v in arrays.items()}
    d["out"] = nc.dram_tensor("out", (B, S, D), F32, kind="ExternalOutput").ap()
    decoder(nc, d)
    return run_bass_kernel_spmd(nc, [arrays], core_ids=[0]).results[0]["out"]
```

```python
from contextlib import ExitStack

import concourse.bass as bass
import numpy as np
from concourse import mybir

P = 128
ALU = mybir.AluOpType
ACT = mybir.ActivationFunctionType
AX = mybir.AxisListType
F32 = mybir.dt.float32
BF16 = mybir.dt.bfloat16
U32 = mybir.dt.uint32
I32 = mybir.dt.int32

B, S, D = 16, 256, 256
CTX = 120
HEADS, HD = 16, 16
SLOT = 32
QUADS = HEADS // 4
TT = S // P
TILES = B * TT
DC = D // P
EPS = 1e-5


def wait(eng, sem, value):
    if isinstance(value, int) and value <= 0:
        return
    eng.wait_ge(sem, value)


class Steps:

    def __init__(self, eng, sem):
        self.eng, self.sem, self.n = eng, sem, 0

    def link(self, instruction):
        self.n += 1
        instruction.then_inc(self.sem, 1)
        self.eng.wait_ge(self.sem, self.n)

    def again(self):
        if self.n:
            self.eng.sem_clear(self.sem)
            self.n = 0


class Room:

    def __init__(self, nc, ctx, stage):
        self.nc, self.ctx, self.stage = nc, ctx, stage
        self.sems = []
        ctx.callback(self.close)

    def close(self):
        self.nc.clear_and_free_semaphores(self.sems)
        self.nc.all_engine_barrier()

    def sb(self, name, shape, dt=F32):
        return self.ctx.enter_context(self.nc.sbuf_tensor(f"{self.stage}_{name}", shape, dt))

    def ps(self, name, shape, dt=F32):
        return self.ctx.enter_context(self.nc.psum_tensor(f"{self.stage}_{name}", shape, dt))

    def sem(self, name):
        self.sems.append(self.nc.alloc_semaphore(f"{self.stage}_{name}"))
        return self.sems[-1]


def load_stage(nc, x_all, ident, d):
    with ExitStack() as ctx:
        r = Room(nc, ctx, "load")
        loaded = r.sem("loaded")
        block = ctx.enter_context(nc.Block())

        @block.sync
        def _(sp):
            xv = d["x"].rearrange("b (t p) c -> p (b t) c", p=P)
            for k in range(4):
                n = TILES // 4
                sp.dma_start(x_all[:, k * n:(k + 1) * n, :], xv[:, k * n:(k + 1) * n, :]).then_inc(loaded, 16)
            sp.dma_start(ident[:], d["ident"]).then_inc(loaded, 16)
            sp.wait_ge(loaded, 16 * 5)


def norm_stage(nc, name, x_all, mean, rstd):
    with ExitStack() as ctx:
        r = Room(nc, ctx, name)
        moments = r.sb("moments", [P, TILES, 6])
        mv = r.sb("mv", [P, TILES, 2])
        var = r.sb("var", [P, TILES, 1])
        root = r.sb("root", [P, TILES, 1])
        guess = r.sb("guess", [P, TILES, 1])
        t0 = r.sb("t0", [P, TILES, 1])
        step = r.sem("step")
        var_ready = r.sem("var_ready")
        root_ready = r.sem("root_ready")
        block = ctx.enter_context(nc.Block())

        @block.scalar
        def _(act):
            act.wait_ge(var_ready, 1)
            nc.scalar.activation(root[:], var[:], ACT.Sqrt).then_inc(root_ready, 1)

        @block.vector
        def _(dve):
            steps = Steps(dve, step)
            with dve.Fori(0, TILES // 4) as i:
                for k in range(4):
                    t = 4 * i + k
                    nc.vector.bn_stats(moments[:, t, :], x_all[:, t, :])
            steps.link(nc.vector.drain())
            for t in range(TILES):
                ins = nc.vector.bn_aggr(mv[:, t, :], moments[:, t, :])
            steps.link(ins)
            nc.vector.tensor_copy(mean[:], mv[:, :, 0:1])
            nc.vector.tensor_scalar(var[:], mv[:, :, 1:2], EPS, None, ALU.add).then_inc(var_ready, 1)
            dve.wait_ge(root_ready, 1)
            steps.link(nc.vector.reciprocal(guess[:], root[:]))
            steps.link(nc.vector.tensor_tensor(t0[:], guess[:], guess[:], ALU.mult))
            steps.link(nc.vector.tensor_tensor(root[:], t0[:], var[:], ALU.mult))
            steps.link(nc.vector.tensor_scalar(t0[:], root[:], -0.5, 1.5, ALU.mult, ALU.add))
            steps.link(nc.vector.tensor_tensor(rstd[:], guess[:], t0[:], ALU.mult))


def attention_stage(nc, kind, x_all, mean, rstd, ident, d):
    rope = kind == "causal"
    cross = kind == "cross"
    KN = CTX if cross else P
    KT = 1 if cross else TT
    KS = KT * KN
    NQUAD = HEADS // 4
    CH = HEADS // DC
    JOBS = [(qk, c) for c in range(DC) for qk in range(2)]
    NJ = len(JOBS)
    QRUNS = [(0, 3, 0), (3, 2, 1), (5, 1, 2)]
    KRUNS = [(0, 3, 0), (3, 2, 0), (5, 1, 0)]
    OUTS = 16 * DC * (len(QRUNS) + 1)
    ROWS = 6 * HD
    STACKED = 16 * (1 + len(KRUNS))
    qfrom = {k: (k * P if rope else 0) for k in range(KT)}
    kcol = {k: sum(S - qfrom[i] for i in range(k)) for k in range(KT)}
    seen = {q: ((q + 1) * P if rope else KS) for q in range(TT)}
    qcol = {q: sum(seen[i] for i in range(q)) for q in range(TT)}
    COLS = sum(S - qfrom[k] for k in range(KT))
    REACH = 2
    near = {k: (max(0, k * P - REACH), min(S, (k + 1) * P + REACH)) for k in range(KT)}

    with ExitStack() as ctx:
        r = Room(nc, ctx, kind)
        sb, ps, sem = r.sb, r.ps, r.sem
        names = ["wq", "wqs", "wk", "wks", "wv"] if rope else ["wq", "wk", "wv"]
        w = {n: sb(n, [P, DC, D]) for n in names}
        w["wo"] = sb("wo", [P, NQUAD, D])
        pack = sb("pack", [P, SLOT])
        spread = sb("spread", [P, NQUAD, P])
        nload = len(w) + 2
        if rope:
            tab = {n: sb(n, [P, S]) for n in ("cosq", "sinq", "cosk", "sink")}
            ident16 = sb("ident16", [P, P], BF16)
            mask = sb("mask", [P, 2, P], BF16)
            maskf = sb("maskf", [P, 2, P])
            rot = sb("rot", [P, 2, 2, S])
            nload += 5
        else:
            bq = sb("bq", [P, DC])
            bk = sb("bk", [P, DC])
            bv = sb("bv", [P, D])
            bo = sb("bo", [P, D])
            nload += 4
        if kind == "band":
            bias2 = sb("bias2", [P, DC])
            band = sb("band", [P, TT, S])
            nload += 2
        if cross:
            nload += 1
            ctx_sb = sb("ctx", [P, B, D])
            ctx_one = sb("ctx_one", [P, D])
            ctxT = sb("ctxT", [P, 2, DC, CTX])
        xn = sb("xn", [P, TT, D])
        xnT = sb("xnT", [P, 2, DC, S])
        full = sb("full", [P, 2, S])
        rest = sb("rest", [P, S])
        part = sb("part", [P, NJ, 3, S], BF16)
        qs = sb("qs", [P, 2, HEADS, S], BF16)
        ks = sb("ks", [P, 2, HEADS, KS], BF16)
        va = sb("va", [P, 2, KT, HEADS, SLOT])
        nmax = sb("nmax", [P, TT, HEADS])
        nrest = sb("nrest", [CH, S])
        npart = sb("npart", [CH, 2, 3, S], BF16)
        probT = sb("probT", [P, 8, COLS])
        oq = sb("oq", [P, NQUAD, S])
        rr = sb("rr", [P, S])
        onT = sb("onT", [P, NQUAD, S])
        ytmp = sb("ytmp", [P, TT, D])
        warm = sb("warm", [P, 1])
        qscratch = nc.dram_tensor(f"{kind}_qscratch", (2, DC, 6, P, S), BF16).ap()
        kscratch = nc.dram_tensor(f"{kind}_kscratch", (2, DC, 3, P, KS), BF16).ap()
        nscratch = nc.dram_tensor(f"{kind}_nscratch", (2, 2, 3, CH, S), BF16).ap()

        ps_p = ps("ps_p", [P, 2, 512])
        ps_1 = ps("ps_1", [P, 2, 512])
        ps_2 = ps("ps_2", [P, 2, 512])
        ps_o = ps("ps_o", [P, 512])
        ps_n = ps("ps_n", [P, 512])

        weights = sem("weights")
        ready = sem("ready")
        xn_ready = sem("xn_ready")
        xt_done = sem("xt_done")
        xt_used = sem("xt_used")
        proj_done = sem("proj_done")
        proj_used = sem("proj_used")
        rest_ready = sem("rest_ready")
        split_ready = sem("split_ready")
        parts_out = sem("parts_out")
        stacked = [sem(f"stacked{c}") for c in range(DC)]
        v_done = sem("v_done")
        v_used = sem("v_used")
        s1_done = sem("s1_done")
        nmax_ready = sem("nmax_ready")
        nt_done = sem("nt_done")
        n_ready = sem("n_ready")
        n_out = sem("n_out")
        n_in = [sem(f"n_in{c}") for c in range(DC)]
        s2_done = sem("s2_done")
        p_ready = sem("p_ready")
        b_ready = sem("b_ready")
        pv_done = sem("pv_done")
        oq_ready = sem("oq_ready")
        packed = sem("packed")
        rr_ready = sem("rr_ready")
        spread_done = sem("spread_done")
        on_ready = sem("on_ready")
        y_done = sem("y_done")
        y_used = sem("y_used")
        step = sem("step")
        block = ctx.enter_context(nc.Block())

        def there(b):
            return not isinstance(b, int) or 0 <= b < B

        PROJECT, OUT, VALUES, STACK = (2, 4, 6, 8), 10, 12, 10

        def macro(e, b, par):
            for s in range(HEADS):
                e.head(b, par, s)
                if s > 0:
                    e.factor(b, par, s - 1)
                if s == 0:
                    if there(b - 1):
                        e.turn_max(b, par, 1)
                    if there(b + 1):
                        e.stack(b + 1, 1 - par, 1)
                if there(b - 1):
                    if s == 1:
                        e.weigh(b - 1, 1 - par, NQUAD - 1)
                    if s == 2:
                        e.sums(b - 1, 2 * b + 2)
                    if s == 3:
                        e.normalise(b - 1)
                if s % 4 == 1 and s > 1:
                    e.weigh(b, par, s // 4 - 1)
                if there(b + 2):
                    if s == 0:
                        e.norm(b + 2)
                    if s == 1:
                        e.turn(b + 2, par)
                    if s in PROJECT:
                        e.project(b + 2, par, PROJECT.index(s))
                if s == OUT and there(b - 1):
                    e.out(b - 1)
                if there(b + 1):
                    if s == VALUES:
                        e.values(b + 1, 1 - par)
                    e.find(b + 1, 1 - par, s)
                    if s == CH + 1:
                        e.turn_max(b + 1, 1 - par, 0)
                if s == STACK and there(b + 2):
                    e.stack(b + 2, par, 0)
            e.factor(b, par, HEADS - 1)
            e.end()

        def program(eng, e):
            e.norm(0)
            e.turn(0, 0)
            for j in range(NJ):
                e.project(0, 0, j)
            e.stack(0, 0, 0)
            e.stack(0, 0, 1)
            e.values(0, 0)
            e.norm(1)
            e.turn(1, 1)
            for j in range(NJ):
                e.project(1, 1, j)
            e.stack(1, 1, 0)
            for h in range(HEADS):
                e.find(0, 0, h)
                if h % CH == CH - 1:
                    e.turn_max(0, 0, h // CH)
            macro(e, 0, 0)
            with eng.Fori(0, B // 2 - 2) as i:
                macro(e, 2 * i + 1, 1)
                macro(e, 2 * i + 2, 0)
            macro(e, B - 3, 1)
            macro(e, B - 2, 0)
            macro(e, B - 1, 1)
            e.weigh(B - 1, 1, NQUAD - 1)
            e.sums(B - 1, 2 * B)
            e.normalise(B - 1)
            e.out(B - 1)

        class Part:

            def norm(self, b): pass
            def turn(self, b, par): pass
            def project(self, b, par, j): pass
            def stack(self, b, par, c): pass
            def values(self, b, par): pass
            def find(self, b, par, h): pass
            def turn_max(self, b, par, c): pass
            def head(self, b, par, h): pass
            def factor(self, b, par, h): pass
            def weigh(self, b, par, j): pass
            def sums(self, b, turned): pass
            def normalise(self, b): pass
            def out(self, b): pass
            def end(self): pass

        @block.sync
        def _(sp):
            def chunks(ap):
                return ap.rearrange("(c p) n -> p c n", p=P)
            for n in w:
                sp.dma_start(w[n][:], chunks(d[f"{kind}_{n}"])).then_inc(weights, 16)
            sp.dma_start(pack[:], d["pack"]).then_inc(weights, 16)
            sp.dma_start(spread[:], d["spread"]).then_inc(weights, 16)
            if rope:
                for n in tab:
                    sp.dma_start(tab[n][:], d[f"{n}"]).then_inc(weights, 16)
                sp.dma_start(maskf[:], chunks(d["mask"])).then_inc(weights, 16)
            else:
                sp.dma_start(bq[:], d[f"{kind}_bq"]).then_inc(weights, 16)
                sp.dma_start(bk[:], d[f"{kind}_bk"]).then_inc(weights, 16)
                sp.dma_start(bv[:], d[f"{kind}_bv"].partition_broadcast(P)).then_inc(weights, 16)
                sp.dma_start(bo[:], d[f"{kind}_bo"].partition_broadcast(P)).then_inc(weights, 16)
            if cross:
                sp.dma_start(ctx_sb[0:CTX, :, :], d["ctx"].rearrange("b k c -> k b c")).then_inc(weights, 16)
            if kind == "band":
                sp.dma_start(bias2[:], d["band_bias"]).then_inc(weights, 16)
                sp.dma_start(band[:], chunks(d["band"])).then_inc(weights, 16)

            def settle(sem, value):
                wait(sp, sem, value)
                sp.wait_ge(weights, 16 * nload)

            class Sync(Part):
                def project(self, b, par, j):
                    qk, c = JOBS[j]
                    settle(split_ready, NJ * b + j + 1)
                    if qk == 0:
                        for slot, slots, a in QRUNS:
                            sp.dma_start(qscratch[par, c, slot:slot + slots].rearrange("s p t -> p s t"),
                                         part[:, j, a:a + 1, :].broadcast_to((P, slots, S))).then_inc(parts_out, 16)
                    else:
                        sp.dma_start(kscratch[par, c].rearrange("s p t -> p s t"), part[:, j, :, 0:KS]).then_inc(parts_out, 16)

                def stack(self, b, par, c):
                    settle(parts_out, OUTS * (b + 1))

                    def by_head(ap):
                        return ap.rearrange("s (r h) t -> (s r) h t", h=CH)
                    mine = slice(c * CH, (c + 1) * CH)
                    sp.dma_start(qs[0:ROWS, par, mine, :], by_head(qscratch[par, c])).then_inc(stacked[c], 16)
                    for slot, slots, a in KRUNS:
                        sp.dma_start(ks[slot * HD:(slot + slots) * HD, par, mine, :],
                                     by_head(kscratch[par, c, a:a + slots])).then_inc(stacked[c], 16)

                def turn_max(self, b, par, c):
                    settle(n_ready, 2 * b + c + 1)
                    sp.dma_start(nscratch[par, c].rearrange("a h t -> h a t"), npart[:, c, :, :]).then_inc(n_out, 16)
                    settle(n_out, 16 * (2 * b + c + 1))
                    sp.dma_start(qs[ROWS:ROWS + 3, par, c * CH:(c + 1) * CH, :], nscratch[par, c]).then_inc(n_in[c], 16)
            program(sp, Sync())

        @block.tensor
        def _(pe):
            pe.wait_ge(weights, 16 * nload)
            pe.wait_ge(ready, 1)

            def values_before(b):
                return b - 1 if not isinstance(b, int) else min(b, max(1, b - 1))

            class Tensor(Part):
                def turn(self, b, par):
                    pe.wait_ge(xn_ready, b + 1)
                    wait(pe, proj_used, NJ * b)
                    pe.wait_ge(y_used, max(1, b - 2) if isinstance(b, int) else b - 2)
                    for t in range(TT):
                        for c in range(DC):
                            mm = nc.tensor.transpose(ps_p[:, 0, c * S + t * P:c * S + (t + 1) * P],
                                                     xn[:, t, c * P:(c + 1) * P], ident[:])
                    mm.then_inc(xt_done, 1)
                    if cross:
                        wait(pe, v_used, values_before(b))
                        for c in range(DC):
                            mm = nc.tensor.transpose(ps_p[:, 1, c * CTX:(c + 1) * CTX], ctx_one[0:CTX, c * P:(c + 1) * P],
                                                     ident[0:CTX, 0:CTX])
                        mm.then_inc(xt_done, 1)

                def project(self, b, par, j):
                    if j == 0:
                        pe.wait_ge(xt_used, (2 if cross else 1) * (b + 1))
                        wait(pe, v_used, values_before(b))
                    if j >= 2:
                        pe.wait_ge(proj_used, NJ * b + j - 1)
                    qk, chunk = JOBS[j]
                    src, n = (ctxT, CTX) if cross and qk else (xnT, S)
                    mine = [("wq", "wqs"), ("wk", "wks")] if rope else [("wq",), ("wk",)]
                    for k, name in enumerate(mine[qk]):
                        for c in range(DC):
                            mm = nc.tensor.matmul(ps_p[:, (j + 1) % 2, k * S:k * S + n],
                                                  w[name][:, c, chunk * P:(chunk + 1) * P], src[:, par, c, :],
                                                  start=(c == 0), stop=(c == DC - 1))
                    mm.then_inc(proj_done, 1)

                def values(self, b, par):
                    if isinstance(b, int) and b in (0, B - 1):
                        pe.wait_ge(proj_used, NJ * (b + 1) - (1 if b == 0 else 0))
                    else:
                        pe.wait_ge(proj_used, NJ * (b + 2) - 1)
                    wait(pe, v_used, b)
                    src = ctxT if cross else xnT
                    for k in range(KT):
                        for c in range(DC):
                            mm = nc.tensor.matmul(ps_p[0:KN, 1, k * D:(k + 1) * D], src[:, par, c, k * KN:(k + 1) * KN],
                                                  w["wv"][:, c, :], start=(c == 0), stop=(c == DC - 1))
                    mm.then_inc(v_done, 1)

                def find(self, b, par, h):
                    if h % CH == 0:
                        pe.wait_ge(stacked[h // CH], STACKED * (b + 1))
                    wait(pe, nmax_ready, HEADS * b + h - 1)
                    for q in range(TT):
                        c0, n = qcol[q], seen[q]
                        mm = nc.tensor.matmul(ps_1[:, h % 2, c0:c0 + n], qs[0:ROWS, par, h, q * P:(q + 1) * P],
                                              ks[0:ROWS, par, h, 0:n], start=True, stop=not rope)
                        if rope:
                            mm = nc.tensor.matmul(ps_1[:, h % 2, c0 + q * P:c0 + (q + 1) * P], ident16[:], mask[:, 0, :],
                                                  start=False, stop=True)
                    mm.then_inc(s1_done, 1)

                def turn_max(self, b, par, c):
                    pe.wait_ge(nmax_ready, HEADS * b + CH * (c + 1))
                    wait(pe, n_ready, 2 * b + c)
                    wait(pe, on_ready, 2 * (b - 1))
                    for t in range(TT):
                        mm = nc.tensor.transpose(ps_n[0:CH, t * P:(t + 1) * P], nmax[:, t, c * CH:(c + 1) * CH], ident[:])
                    mm.then_inc(nt_done, 1)

                def head(self, b, par, h):
                    if h % CH == 0:
                        pe.wait_ge(n_in[h // CH], 16 * (b + 1))
                    wait(pe, p_ready, HEADS * b + h - 1)
                    for k in range(KT):
                        c0, n = kcol[k], S - qfrom[k]
                        mm = nc.tensor.matmul(ps_2[0:KN, h % 2, c0:c0 + n], ks[0:ROWS + 3, par, h, k * KN:(k + 1) * KN],
                                              qs[0:ROWS + 3, par, h, qfrom[k]:S], start=True, stop=not rope)
                        if rope:
                            mm = nc.tensor.matmul(ps_2[:, h % 2, c0:c0 + P], ident16[:], mask[:, 1, :],
                                                  start=False, stop=True)
                    mm.then_inc(s2_done, 1)

                def weigh(self, b, par, j):
                    if j == 0:
                        pe.wait_ge(v_used, b + 1)
                    pe.wait_ge(b_ready if kind == "band" else p_ready, HEADS * b + 4 * j + 4)
                    wait(pe, oq_ready, NQUAD * b + j)
                    if j == 0:
                        wait(pe, on_ready, 2 * b)
                    for k in range(KT):
                        for g in range(4):
                            h = 4 * j + g
                            mm = nc.tensor.matmul(ps_o[SLOT * g:SLOT * (g + 1), qfrom[k]:S], va[0:KN, par, k, h, :],
                                                  probT[0:KN, h % 8, kcol[k]:kcol[k] + S - qfrom[k]],
                                                  start=(k == 0), stop=(k == KT - 1))
                    mm.then_inc(pv_done, 1)

                def sums(self, b, turned):
                    pe.wait_ge(oq_ready, NQUAD * (b + 1))
                    pe.wait_ge(n_ready, turned)
                    wait(pe, on_ready, 2 * b)
                    for j in range(NQUAD):
                        mm = nc.tensor.matmul(ps_n[SLOT * j:SLOT * (j + 1), 0:S], pack[:], oq[:, j, :], start=True, stop=True)
                    mm.then_inc(packed, 1)

                def normalise(self, b):
                    pe.wait_ge(rr_ready, b + 1)
                    for half, bank in enumerate((ps_n, ps_o)):
                        for n in range(2):
                            mm = nc.tensor.matmul(bank[:, n * S:(n + 1) * S], spread[:, 2 * half + n, :], rr[:],
                                                  start=True, stop=True)
                        mm.then_inc(spread_done, 1)

                def out(self, b):
                    pe.wait_ge(on_ready, 2 * (b + 1))
                    pe.wait_ge(proj_used, min(NJ * (b + 4), NJ * B) if isinstance(b, int) else NJ * (b + 4))
                    pe.wait_ge(y_used, b + 1)
                    for t in range(TT):
                        for j in range(NQUAD):
                            mm = nc.tensor.matmul(ps_p[:, 0, t * D:(t + 1) * D], onT[:, j, t * P:(t + 1) * P],
                                                  w["wo"][:, j, :], start=(j == 0), stop=(j == NQUAD - 1))
                    mm.then_inc(y_done, 1)
            program(pe, Tensor())

        @block.scalar
        def _(act):
            act.wait_ge(weights, 16 * nload)
            act.wait_ge(ready, 1)
            nc.scalar.activation(warm[:], ident[:, 0:1], ACT.Exp)

            class Scalar(Part):
                def turn(self, b, par):
                    act.wait_ge(xt_done, (2 if cross else 1) * b + 1)
                    nc.scalar.activation(xnT[:, par].rearrange("p c s -> p (c s)"), ps_p[:, 0, :], ACT.Copy).then_inc(xt_used, 1)
                    if cross:
                        act.wait_ge(xt_done, 2 * b + 2)
                        nc.scalar.activation(ctxT[:, par].rearrange("p c s -> p (c s)"), ps_p[:, 1, 0:DC * CTX],
                                             ACT.Copy).then_inc(xt_used, 1)

                def project(self, b, par, j):
                    if rope:
                        return
                    act.wait_ge(proj_done, NJ * b + j + 1)
                    wait(act, split_ready, NJ * b + j - 1)
                    wait(act, parts_out, OUTS * b)
                    qk, c = JOBS[j]
                    n = S if qk == 0 else KS
                    for dst in (full[:, j % 2, 0:n], part[:, j, 0, 0:n]):
                        ins = nc.scalar.activation(dst, ps_p[:, (j + 1) % 2, 0:n], ACT.Identity,
                                                   bias=(bq, bk)[qk][:, c:c + 1], scale=(0.25, 1.0)[qk])
                    ins.then_inc(proj_used, 1)

                def values(self, b, par):
                    if not rope:
                        return
                    act.wait_ge(v_done, b + 1)
                    wait(act, pv_done, NQUAD * (b - 1))
                    for k in range(KT):
                        ins = nc.scalar.activation(va[:, par, k, :, 0:HD],
                                                   ps_p[:, 1, k * D:(k + 1) * D].rearrange("p (h e) -> p h e", h=HEADS),
                                                   ACT.Copy)
                    ins.then_inc(v_used, 1)

                def head(self, b, par, h):
                    act.wait_ge(s2_done, HEADS * b + h + 1)
                    wait(act, pv_done, NQUAD * b + h // 4 - 1)
                    nc.scalar.activation(probT[0:KN, h % 8, :], ps_2[0:KN, h % 2, 0:COLS], ACT.Exp).then_inc(p_ready, 1)

                def weigh(self, b, par, j):
                    act.wait_ge(pv_done, NQUAD * b + j + 1)
                    if j == 0:
                        wait(act, on_ready, 2 * b)
                    nc.scalar.activation(oq[:, j, :], ps_o[:, 0:S], ACT.Copy).then_inc(oq_ready, 1)
            program(act, Scalar())

        @block.gpsimd
        def _(pool):
            class Pool(Part):
                def project(self, b, par, j):
                    qk, c = JOBS[j]
                    n = S if qk == 0 else KS
                    src, high = full[:, j % 2, 0:n], part[:, j, 0, 0:n]
                    pool.wait_ge(proj_used, NJ * b + j + 1)
                    wait(pool, split_ready, NJ * b + j)
                    nc.gpsimd.tensor_tensor(rest[:, 0:n], src, high, ALU.subtract)
                    nc.gpsimd.tensor_tensor(part[:, j, 1, 0:n], src, high, ALU.subtract).then_inc(rest_ready, 1)
                    pool.wait_ge(rest_ready, NJ * b + j + 1)
                    nc.gpsimd.tensor_tensor(part[:, j, 2, 0:n], rest[:, 0:n], part[:, j, 1, 0:n],
                                            ALU.subtract).then_inc(split_ready, 1)
            program(pool, Pool())

        @block.vector
        def _(dve):
            dve.wait_ge(weights, 16 * nload)
            steps = Steps(dve, step)
            if rope:
                steps.link(nc.vector.tensor_copy(ident16[:], ident[:]))
                steps.link(nc.vector.tensor_copy(mask[:], maskf[:]))
            else:
                if kind == "band":
                    steps.link(nc.vector.tensor_tensor(bq[:], bq[:], bias2[:], ALU.add))
                steps.link(nc.vector.tensor_scalar(bq[:], bq[:], 0.25, None, ALU.mult))
            nc.vector.memset(ks[ROWS:ROWS + 3, :, :, :], 1.0).then_inc(y_used, 1)
            nc.vector.memset(va[:], 1.0).then_inc(ready, 1)
            dve.wait_ge(ready, 1)
            steps.again()

            class Vector(Part):
                def norm(self, b):
                    wait(dve, xt_done, (2 if cross else 1) * b)
                    for t in range(TT):
                        ins = nc.vector.tensor_scalar(xn[:, t, :], x_all[:, b * TT + t, :], mean[:, b * TT + t, :],
                                                      rstd[:, b * TT + t, :], ALU.subtract, ALU.mult)
                    if cross:
                        ins = nc.vector.tensor_copy(ctx_one[0:CTX, :], ctx_sb[0:CTX, b, :])
                    ins.then_inc(xn_ready, 1)

                def project(self, b, par, j):
                    if not rope:
                        return
                    dve.wait_ge(proj_done, NJ * b + j + 1)
                    qk, c = JOBS[j]
                    bank = ps_p[:, (j + 1) % 2, :]
                    cs, sn = ("cosk", "sink") if qk else ("cosq", "sinq")
                    wait(dve, proj_used, NJ * b + j - 1)
                    nc.vector.tensor_tensor(rot[:, j % 2, 0, :], bank[:, 0:S], tab[cs][:], ALU.mult)
                    steps.link(nc.vector.tensor_tensor(rot[:, j % 2, 1, :], bank[:, S:2 * S], tab[sn][:], ALU.mult))
                    wait(dve, split_ready, NJ * b + j - 1)
                    wait(dve, parts_out, OUTS * b)
                    for dst in (full[:, j % 2, :], part[:, j, 0, :]):
                        ins = nc.vector.tensor_tensor(dst, rot[:, j % 2, 0, :], rot[:, j % 2, 1, :], ALU.add)
                    ins.then_inc(proj_used, 1)

                def values(self, b, par):
                    if rope:
                        return
                    dve.wait_ge(v_done, b + 1)
                    wait(dve, pv_done, NQUAD * (b - 1))
                    for k in range(KT):
                        ins = nc.vector.tensor_tensor(
                            va[0:KN, par, k, :, 0:HD],
                            ps_p[0:KN, 1, k * D:(k + 1) * D].rearrange("p (h e) -> p h e", h=HEADS),
                            bv[0:KN, :].rearrange("p (h e) -> p h e", h=HEADS), ALU.add)
                    ins.then_inc(v_used, 1)

                def find(self, b, par, h):
                    dve.wait_ge(s1_done, HEADS * b + h + 1)
                    if rope:
                        for q in range(TT):
                            ins = nc.vector.tensor_reduce(nmax[:, q, h:h + 1], ps_1[:, h % 2, qcol[q]:qcol[q] + seen[q]],
                                                          AX.X, ALU.max, negate=True)
                    else:
                        ins = nc.vector.tensor_reduce(nmax[:, :, h],
                                                      ps_1[:, h % 2, 0:TT * KS].rearrange("p (q k) -> p q k", q=TT),
                                                      AX.X, ALU.max, negate=True)
                    ins.then_inc(nmax_ready, 1)

                def turn_max(self, b, par, c):
                    dve.wait_ge(nt_done, 2 * b + c + 1)
                    wait(dve, n_ready, 2 * b + c)
                    wait(dve, n_out, 16 * (2 * b + c - 1))
                    high, middle, low = (npart[:, c, a, :] for a in range(3))
                    steps.link(nc.vector.tensor_copy(high, ps_n[0:CH, 0:S]))
                    nc.vector.tensor_tensor(nrest[:], ps_n[0:CH, 0:S], high, ALU.subtract)
                    steps.link(nc.vector.tensor_tensor(middle, ps_n[0:CH, 0:S], high, ALU.subtract))
                    nc.vector.tensor_tensor(low, nrest[:], middle, ALU.subtract).then_inc(n_ready, 1)

                def factor(self, b, par, h):
                    if kind != "band":
                        return
                    dve.wait_ge(p_ready, HEADS * b + h + 1)
                    for k in range(KT):
                        lo, hi = near[k]
                        e = probT[:, h % 8, kcol[k] + lo:kcol[k] + hi]
                        ins = nc.vector.tensor_tensor(e, e, band[:, k, lo:hi], ALU.mult)
                    ins.then_inc(b_ready, 1)

                def sums(self, b, turned):
                    dve.wait_ge(packed, b + 1)
                    nc.vector.reciprocal(rr[:], ps_n[:, 0:S]).then_inc(rr_ready, 1)

                def normalise(self, b):
                    wait(dve, y_done, b)
                    for half, bank in enumerate((ps_n, ps_o)):
                        dve.wait_ge(spread_done, 2 * b + half + 1)
                        nc.vector.tensor_tensor(onT[:, 2 * half:2 * half + 2, :], oq[:, 2 * half:2 * half + 2, :],
                                                bank[:].rearrange("p (j s) -> p j s", j=2), ALU.mult).then_inc(on_ready, 1)

                def out(self, b):
                    dve.wait_ge(y_done, b + 1)
                    wait(dve, y_used, b + 1)
                    for t in range(TT):
                        src = ps_p[:, 0, t * D:(t + 1) * D]
                        if not rope:
                            steps.link(nc.vector.tensor_tensor(ytmp[:, t, :], src, bo[:], ALU.add))
                            src = ytmp[:, t, :]
                        xt = x_all[:, b * TT + t, :]
                        ins = nc.vector.tensor_tensor(xt, src, xt, ALU.add)
                    ins.then_inc(y_used, 1)

                def end(self):
                    steps.again()
            program(dve, Vector())


NQ = 8
HALF = 32
KEYS = 64
TOP = 10
EXPERTS = KEYS * KEYS
EV = 32
CHUNK = 16
NCH = P // CHUNK
RING = 4
AHEAD = 2
PAIRS = [TOP // (a + 1) for a in range(TOP)]
NPAIR = sum(PAIRS)
VC = EV // NCH
LOW = -3.0e38
SELECT = 2


def peer_stage(nc, x_all, mean, rstd, ident, d):
    with ExitStack() as ctx:
        r = Room(nc, ctx, "peer")
        sb, ps, sem = r.sb, r.ps, r.sem
        SEL = NQ * TOP
        wq = sb("wq", [P, DC, 2 * NQ * HALF])
        bq = sb("bq", [P, 4])
        keys = sb("keys", [P, 4 * KEYS])
        down = sb("down", [P, DC, EV, P])
        up = sb("up", [P, EV, D])
        iota = sb("iota", [P, P])
        xn = sb("xn", [P, D])
        xnT = sb("xnT", [P, 2, DC, P])
        qT = sb("qT", [P, 4, P])
        s = sb("s", [P, 2 * NQ, KEYS])
        s2 = sb("s2", [P, 2 * NQ, KEYS])
        best = sb("best", [P, 2 * NQ, 16])
        besti = sb("besti", [P, 2 * NQ, 16], U32)
        i64 = sb("i64", [P, NQ, TOP])
        cand = sb("cand", [P, NQ, NPAIR])
        cand2 = sb("cand2", [P, NQ, NPAIR])
        code = sb("code", [P, NQ, NPAIR])
        tv = sb("tv", [P, NQ, 16])
        tp = sb("tp", [P, NQ, 16], U32)
        tpf = sb("tpf", [P, NQ, 16])
        eq = sb("eq", [P, NQ, TOP, NPAIR])
        ef = sb("ef", [P, SEL])
        ei = sb("ei", [P, SEL], I32)
        uvi = sb("uvi", [P, 2, SEL], I32)
        ew = sb("ew", [P, NQ, TOP])
        es = sb("es", [P, NQ, 1])
        er = sb("er", [P, NQ, 1])
        uvw = sb("uvw", [P, 3, SEL])
        uvT = sb("uvT", [P, 2, 2, P], BF16)
        wT = sb("wT", [P, P])
        rest = sb("rest", [P, 2, P])
        parts = sb("parts", [P, 2, 3, P], BF16)
        count = sb("count", [P, P, CHUNK], BF16)
        hot_u = sb("hot_u", [P, RING, P, CHUNK], BF16)
        hot_e = sb("hot_e", [P, RING, EV, CHUNK], BF16)
        hot_v = sb("hot_v", [P, RING, 3, EV, CHUNK], BF16)
        g = sb("g", [P, 2, EV, P])
        mark = sb("mark", [P, 1])

        ps_q = ps("ps_q", [P, 512])
        ps_s = ps("ps_s", [P, 2, 512])
        ps_h = ps("ps_h", [P, 2, 512])
        ps_w = ps("ps_w", [P, 2, 512])
        ps_u = ps("ps_u", [P, D])

        loaded = sem("loaded")
        down_in = sem("down_in")
        up_in = sem("up_in")
        xn_ready = sem("xn_ready")
        xt_done = sem("xt_done")
        xt_used = sem("xt_used")
        q_done = sem("q_done")
        q_used = sem("q_used")
        s_done = sem("s_done")
        s_used = sem("s_used")
        halves_done = sem("halves_done")
        exp_in = sem("exp_in")
        exp_out = sem("exp_out")
        sel_in = sem("sel_in")
        sel_out = sem("sel_out")
        uvw_ready = sem("uvw_ready")
        uvw_done = sem("uvw_done")
        uvw_used = sem("uvw_used")
        h_done = sem("h_done")
        g_ready = sem("g_ready")
        u_ready = sem("u_ready")
        e_ready = sem("e_ready")
        v_ready = sem("v_ready")
        w_done = sem("w_done")
        gw_ready = sem("gw_ready")
        up_done = sem("up_done")
        x_used = sem("x_used")
        step = sem("step")
        pstep = sem("pstep")
        block = ctx.enter_context(nc.Block())
        NLOAD = 4

        @block.sync
        def _(sp):
            sp.dma_start(wq[:], d["peer_wq"].rearrange("(c p) n -> p c n", p=P)).then_inc(loaded, 16)
            for dst, name in ((bq, "peer_bq"), (keys, "peer_keys"), (iota, "iota")):
                sp.dma_start(dst[:], d[name]).then_inc(loaded, 16)
            sp.dma_start(down[:], d["peer_down"].rearrange("(c p) v u -> p c v u", p=P)).then_inc(down_in, 16)
            sp.dma_start(up[:], d["peer_up"]).then_inc(up_in, 16)

        def run(eng, first, macro, rest):
            first()
            macro(0, 0)
            macro(1, 1)
            with eng.Fori(1, TILES // 2 - 1) as i:
                macro(2 * i, 0)
                macro(2 * i + 1, 1)
            macro(TILES - 2, 0)
            macro(TILES - 1, 1)
            rest()

        def there(t):
            return not isinstance(t, int) or 0 <= t < TILES

        @block.tensor
        def _(pe):
            pe.wait_ge(loaded, 16 * NLOAD)

            def turn_x(t):
                pe.wait_ge(xn_ready, t + 1)
                wait(pe, q_used, t)
                wait(pe, uvw_used, t - 1)
                for c in range(DC):
                    mm = nc.tensor.transpose(ps_q[:, c * P:(c + 1) * P], xn[:, c * P:(c + 1) * P], ident[:])
                mm.then_inc(xt_done, 1)

            def queries(t, par):
                pe.wait_ge(xt_used, t + 1)
                for k in range(4):
                    for c in range(DC):
                        mm = nc.tensor.matmul(ps_q[:, k * P:(k + 1) * P], wq[:, c, k * P:(k + 1) * P],
                                              xnT[:, par, c, :], start=(c == 0), stop=(c == DC - 1))
                mm.then_inc(q_done, 1)

            def scores(t):
                pe.wait_ge(q_used, t + 1)
                wait(pe, s_used, t)
                for k in range(4):
                    mm = nc.tensor.matmul(ps_s[:, k // 2, (k % 2) * 256:(k % 2 + 1) * 256], qT[:, k, :], keys[:],
                                          start=True, stop=True)
                mm.then_inc(s_done, 1)

            def hidden(t, par, n):
                pe.wait_ge(xt_used, t + 1)
                wait(pe, g_ready, NCH * t + n - 1)
                for k in range(4):
                    for c in range(DC):
                        mm = nc.tensor.matmul(ps_h[:, n % 2, k * P:(k + 1) * P], down[:, c, 4 * n + k, :],
                                              xnT[:, par, c, :], start=(c == 0), stop=(c == DC - 1))
                mm.then_inc(h_done, 1)

            def weights(t, n):
                pe.wait_ge(u_ready, NCH * t + n + 1)
                pe.wait_ge(v_ready, NCH * t + n + 1)
                wait(pe, gw_ready, NCH * t + n - 1)
                for k in range(CHUNK):
                    for part in range(3):
                        mm = nc.tensor.matmul(ps_w[:, n % 2, k * EV:(k + 1) * EV], hot_u[0:SEL, n % RING, :, k],
                                              hot_v[0:SEL, n % RING, part, :, k], start=(part == 0), stop=(part == 2))
                mm.then_inc(w_done, 1)

            def output(t, par, a, b):
                if a == 0:
                    pe.wait_ge(gw_ready, NCH * (t + 1))
                    wait(pe, x_used, t)
                for v in range(a, b):
                    mm = nc.tensor.matmul(ps_u[:], g[:, par, v, :], up[:, v, :], start=(v == 0), stop=(v == EV - 1))
                if b == EV:
                    mm.then_inc(up_done, 1)

            def turn_uvw(t):
                pe.wait_ge(uvw_ready, t + 1)
                pe.wait_ge(q_used, min(t + 2, TILES) if isinstance(t, int) else t + 2)
                for k in range(3):
                    mm = nc.tensor.transpose(ps_q[0:SEL, k * P:(k + 1) * P], uvw[:, k, :], ident[:])
                mm.then_inc(uvw_done, 1)

            def first():
                turn_x(0)
                queries(0, 0)
                scores(0)
                pe.wait_ge(down_in, 16)
                for n in range(NCH):
                    hidden(0, 0, n)
                turn_x(1)
                queries(1, 1)
                scores(1)
                turn_uvw(0)
                pe.wait_ge(up_in, 16)

            def macro(t, par):
                def experts(n):
                    if there(t - 1):
                        output(t - 1, 1 - par, VC * n, VC * (n + 1))
                    if there(t + 1):
                        hidden(t + 1, 1 - par, n)

                for n in range(NCH):
                    weights(t, n)
                    if there(t + 2):
                        if n == 1:
                            turn_x(t + 2)
                        if n == 2:
                            queries(t + 2, par)
                        if n == 3:
                            scores(t + 2)
                    if n > 0:
                        experts(n - 1)
                    if n == 5 and there(t + 1):
                        turn_uvw(t + 1)
                experts(NCH - 1)

            def rest():
                output(TILES - 1, 1, 0, EV)

            run(pe, first, macro, rest)

        @block.scalar
        def _(act):
            act.wait_ge(loaded, 16 * NLOAD)

            def take_x(t, par):
                act.wait_ge(xt_done, t + 1)
                nc.scalar.activation(xnT[:, par, :, :].rearrange("p c s -> p (c s)"), ps_q[:, 0:DC * P],
                                     ACT.Copy).then_inc(xt_used, 1)

            def take_q(t):
                act.wait_ge(q_done, t + 1)
                for k in range(4):
                    ins = nc.scalar.activation(qT[:, k, :], ps_q[:, k * P:(k + 1) * P], ACT.Identity, bias=bq[:, k:k + 1])
                ins.then_inc(q_used, 1)

            def take_s(t):
                act.wait_ge(s_done, t + 1)
                wait(act, halves_done, t)
                nc.scalar.activation(s[:].rearrange("p g k -> p (g k)"), ps_s[:].rearrange("p a k -> p (a k)"),
                                     ACT.Copy).then_inc(s_used, 1)

            def gelu(t, par, n):
                act.wait_ge(h_done, NCH * t + n + 1)
                nc.scalar.activation(g[:, par, 4 * n:4 * n + 4, :].rearrange("p v s -> p (v s)"), ps_h[:, n % 2, :],
                                     ACT.Gelu).then_inc(g_ready, 1)

            def exps(t):
                act.wait_ge(exp_in, t + 1)
                nc.scalar.activation(ew[:], ew[:], ACT.Exp).then_inc(exp_out, 1)

            def take_uvw(t, par):
                act.wait_ge(uvw_done, t + 1)
                wait(act, u_ready, NCH * (t - 1))
                wait(act, v_ready, NCH * (t - 1) + 1)
                nc.scalar.activation(uvT[0:SEL, par, :, :].rearrange("p k s -> p (k s)"), ps_q[0:SEL, 0:2 * P], ACT.Copy)
                nc.scalar.activation(parts[0:SEL, par, 0, :], ps_q[0:SEL, 2 * P:3 * P], ACT.Copy)
                nc.scalar.activation(wT[0:SEL, :], ps_q[0:SEL, 2 * P:3 * P], ACT.Copy).then_inc(uvw_used, 1)

            def first():
                for t in range(2):
                    take_x(t, t)
                    take_q(t)
                    take_s(t)
                    if t == 0:
                        for n in range(NCH):
                            gelu(0, 0, n)
                exps(0)
                take_uvw(0, 0)

            def macro(t, par):
                for n in range(NCH):
                    if there(t + 2):
                        if n == 1:
                            take_x(t + 2, par)
                        if n == 2:
                            take_q(t + 2)
                        if n == 3:
                            take_s(t + 2)
                    if there(t + 1):
                        if n > 0:
                            gelu(t + 1, 1 - par, n - 1)
                        if n == 3:
                            exps(t + 1)
                        if n == 5:
                            take_uvw(t + 1, 1 - par)
                if there(t + 1):
                    gelu(t + 1, 1 - par, NCH - 1)

            run(act, first, macro, lambda: None)

        @block.gpsimd
        def _(pool):
            pool.wait_ge(loaded, 16 * NLOAD)
            steps = Steps(pool, pstep)

            def split(t, par):
                pool.wait_ge(uvw_used, t + 1)
                steps.link(nc.gpsimd.tensor_tensor(rest[0:SEL, 0, :], wT[0:SEL, :], parts[0:SEL, par, 0, :], ALU.subtract))
                steps.link(nc.gpsimd.tensor_copy(parts[0:SEL, par, 1, :], rest[0:SEL, 0, :]))
                steps.link(nc.gpsimd.tensor_tensor(rest[0:SEL, 1, :], rest[0:SEL, 0, :], parts[0:SEL, par, 1, :], ALU.subtract))
                steps.link(nc.gpsimd.tensor_copy(parts[0:SEL, par, 2, :], rest[0:SEL, 1, :]))

            def hots(t, par, n):
                if n == 0:
                    split(t, par)
                pool.wait_ge(e_ready, NCH * t + n + 1)
                wait(pool, w_done, NCH * t + n + 1 - RING)
                for part in range(3):
                    w = parts[0:SEL, par, part, n * CHUNK:(n + 1) * CHUNK].unsqueeze(1).broadcast_to((SEL, EV, CHUNK))
                    ins = nc.gpsimd.tensor_tensor(hot_v[0:SEL, n % RING, part, :, :], hot_e[0:SEL, n % RING, :, :], w, ALU.mult)
                ins.then_inc(v_ready, 1)

            def select(t):
                pool.wait_ge(sel_in, t + 1)
                value = code[:].unsqueeze(2).broadcast_to((P, NQ, TOP, NPAIR))
                nc.gpsimd.tensor_tensor(eq[:], eq[:], value, ALU.mult).then_inc(sel_out, 1)
                steps.again()

            def first():
                select(0)
                for n in range(AHEAD):
                    hots(0, 0, n)

            def macro(t, par):
                for n in range(NCH):
                    if n < NCH - AHEAD:
                        hots(t, par, n + AHEAD)
                    elif there(t + 1):
                        hots(t + 1, 1 - par, n + AHEAD - NCH)
                    if n == SELECT and there(t + 1):
                        select(t + 1)

            run(pool, first, macro, lambda: None)

        @block.vector
        def _(dve):
            dve.wait_ge(loaded, 16 * NLOAD)
            steps = Steps(dve, step)
            steps.link(nc.vector.tensor_copy(count[:], iota[:].unsqueeze(2).broadcast_to((P, P, CHUNK))))
            steps.again()

            def norm(t):
                wait(dve, xt_done, t)
                nc.vector.tensor_scalar(xn[:], x_all[:, t, :], mean[:, t, :], rstd[:, t, :], ALU.subtract,
                                        ALU.mult).then_inc(xn_ready, 1)

            def hots(t, par, n):
                if n == 0:
                    dve.wait_ge(uvw_used, t + 1)
                wait(dve, v_ready, NCH * t + n + 1 - RING)
                vt = uvT[0:SEL, par, 1, n * CHUNK:(n + 1) * CHUNK].unsqueeze(1).broadcast_to((SEL, EV, CHUNK))
                nc.vector.tensor_tensor(hot_e[0:SEL, n % RING, :, :], count[0:SEL, 0:EV, :], vt,
                                        ALU.is_equal).then_inc(e_ready, 1)
                wait(dve, w_done, NCH * t + n + 1 - RING)
                ut = uvT[0:SEL, par, 0, n * CHUNK:(n + 1) * CHUNK].unsqueeze(1).broadcast_to((SEL, P, CHUNK))
                nc.vector.tensor_tensor(hot_u[0:SEL, n % RING, :, :], count[0:SEL, :, :], ut,
                                        ALU.is_equal).then_inc(u_ready, 1)

            def weigh(t, par, n):
                if n == 0:
                    dve.wait_ge(g_ready, NCH * (t + 1))
                dve.wait_ge(w_done, NCH * t + n + 1)
                gs = g[:, par, :, n * CHUNK:(n + 1) * CHUNK]
                nc.vector.tensor_tensor(gs, ps_w[:, n % 2, :].rearrange("p (k v) -> p v k", v=EV), gs,
                                        ALU.mult).then_inc(gw_ready, 1)

            def halves(t, a, b):
                gr = range(a, b)
                if a == 0:
                    dve.wait_ge(s_used, t + 1)
                    steps.link(nc.vector.memset(mark[:], 0.0))
                for q in gr:
                    ins = nc.vector.max(best[:, q, 0:8], s[:, q, :])
                steps.link(ins)
                for q in gr:
                    nc.vector.max_index(besti[:, q, 0:8], best[:, q, 0:8], s[:, q, :])
                for q in gr:
                    ins = nc.vector.match_replace(s2[:, q, :], best[:, q, 0:8], s[:, q, :], LOW)
                steps.link(ins)
                for q in gr:
                    ins = nc.vector.max(best[:, q, 8:16], s2[:, q, :])
                steps.link(ins)
                for q in gr:
                    ins = nc.vector.max_index(besti[:, q, 8:16], best[:, q, 8:16], s2[:, q, :])
                steps.link(ins)
                if b == 2 * NQ:
                    nc.vector.tensor_scalar(i64[:], besti[:, 0:2 * NQ:2, 0:TOP], float(KEYS), None,
                                            ALU.mult).then_inc(halves_done, 1)

            def pairs(dst, first, second):
                off = 0
                a = 0
                while a < TOP:
                    nb = PAIRS[a]
                    na = sum(x == nb for x in PAIRS)
                    ins = nc.vector.tensor_tensor(
                        dst[:, :, off:off + na * nb].rearrange("p h (a b) -> p h a b", b=nb),
                        first[:, :, a:a + na].unsqueeze(3).broadcast_to((P, NQ, na, nb)),
                        second[:, :, 0:nb].unsqueeze(2).broadcast_to((P, NQ, na, nb)), ALU.add)
                    off += na * nb
                    a += na
                return ins

            def candidates(t):
                dve.wait_ge(halves_done, t + 1)
                wait(dve, sel_out, t)
                pairs(cand, best[:, 0:2 * NQ:2, :], best[:, 1:2 * NQ:2, :])
                steps.link(pairs(code, i64[:], besti[:, 1:2 * NQ:2, :]))

            def best_eight():
                for h in range(NQ):
                    ins = nc.vector.max(tv[:, h, 0:8], cand[:, h, :])
                steps.link(ins)
                for h in range(NQ):
                    nc.vector.max_index(tp[:, h, 0:8], tv[:, h, 0:8], cand[:, h, :])
                for h in range(NQ):
                    ins = nc.vector.match_replace(cand2[:, h, :], tv[:, h, 0:8], cand[:, h, :], LOW)
                steps.link(ins)

            def next_eight():
                for h in range(NQ):
                    ins = nc.vector.max(tv[:, h, 8:16], cand2[:, h, :])
                steps.link(ins)
                for h in range(NQ):
                    ins = nc.vector.max_index(tp[:, h, 8:16], tv[:, h, 8:16], cand2[:, h, :])
                steps.link(ins)

            def places(t):
                steps.link(nc.vector.tensor_copy(tpf[:], tp[:]))
                where = tpf[:, :, 0:TOP].unsqueeze(3).broadcast_to((P, NQ, TOP, NPAIR))
                number = iota[:, 0:NPAIR].unsqueeze(1).unsqueeze(1).broadcast_to((P, NQ, TOP, NPAIR))
                nc.vector.tensor_tensor(eq[:], number, where, ALU.is_equal).then_inc(sel_in, 1)
                nc.vector.tensor_tensor(ew[:], tv[:, :, 0:TOP], tv[:, :, 0:1].broadcast_to((P, NQ, TOP)),
                                        ALU.subtract).then_inc(exp_in, 1)

            def choices(t):
                dve.wait_ge(exp_out, t + 1)
                wait(dve, uvw_done, t)
                steps.link(nc.vector.tensor_reduce(es[:], ew[:], AX.X, ALU.add))
                steps.link(nc.vector.reciprocal(er[:], es[:]))
                nc.vector.tensor_tensor(uvw[:, 2, :].rearrange("p (h k) -> p h k", h=NQ), ew[:],
                                        er[:].broadcast_to((P, NQ, TOP)), ALU.mult)
                dve.wait_ge(sel_out, t + 1)
                steps.link(nc.vector.tensor_reduce(ef[:].rearrange("p (h k) -> p h k", h=NQ), eq[:], AX.X, ALU.add))
                steps.link(nc.vector.tensor_copy(ei[:], ef[:]))
                nc.vector.tensor_scalar(uvi[:, 0, :], ei[:], 5, None, ALU.logical_shift_right)
                steps.link(nc.vector.tensor_scalar(uvi[:, 1, :], ei[:], EV - 1, None, ALU.bitwise_and))
                nc.vector.tensor_copy(uvw[:, 0:2, :], uvi[:]).then_inc(uvw_ready, 1)
                dve.wait_ge(uvw_ready, t + 1)

            def add(t):
                dve.wait_ge(up_done, t + 1)
                nc.vector.tensor_tensor(x_all[:, t, :], ps_u[:], x_all[:, t, :], ALU.add).then_inc(x_used, 1)

            HALVES = {3: (0, 2), 4: (2, 4), 5: (4, 8), 6: (8, 12), 7: (12, 16)}

            def first():
                norm(0)
                norm(1)
                for a in range(0, 2 * NQ, 4):
                    halves(0, a, a + 4)
                candidates(0)
                best_eight()
                next_eight()
                places(0)
                choices(0)
                for a in range(0, 2 * NQ, 4):
                    halves(1, a, a + 4)
                for n in range(AHEAD):
                    hots(0, 0, n)
                steps.again()

            def macro(t, par):
                if there(t - 2):
                    add(t - 2)
                if there(t + 2):
                    norm(t + 2)
                for n in range(NCH):
                    if n < NCH - AHEAD:
                        hots(t, par, n + AHEAD)
                    elif there(t + 1):
                        hots(t + 1, 1 - par, n + AHEAD - NCH)
                    if n >= 1:
                        weigh(t, par, n - 1)
                    if there(t + 2) and n in HALVES:
                        halves(t + 2, *HALVES[n])
                    if there(t + 1):
                        if n == 0:
                            candidates(t + 1)
                        if n == 1:
                            best_eight()
                        if n == 2:
                            next_eight()
                            places(t + 1)
                        if n == 4:
                            choices(t + 1)
                weigh(t, par, NCH - 1)
                steps.again()

            def rest():
                add(TILES - 2)
                add(TILES - 1)

            run(dve, first, macro, rest)


def bidaf_stage(nc, x_all, mean, rstd, ident, d):
    with ExitStack() as ctx:
        r = Room(nc, ctx, "bidaf")
        NS = 2
        wl = r.sb("wl", [P, 4 * DC, D])
        bl = r.sb("bl", [P, D])
        vec = r.sb("vec", [P, 3, DC])
        b3 = r.sb("b3", [1, 3])
        bsum = r.sb("bsum", [1, 1])
        ones = r.sb("ones", [1, P])
        warm = r.sb("warm", [P, 1])
        loaded = r.sem("loaded")
        ready = r.sem("ready")
        step = r.sem("step")
        astep = r.sem("astep")


        class Stream:
            def __init__(self, k):
                self.k = k
                self.q = r.sb(f"q{k}", [P, D])
                self.c = r.sb(f"c{k}", [P, TT, D])
                self.cT = r.sb(f"cT{k}", [P, DC, S])
                self.qT = r.sb(f"qT{k}", [P, DC, CTX])
                self.m = r.sb(f"m{k}", [P, DC, CTX])
                self.qrow = r.sb(f"qrow{k}", [1, CTX])
                self.nmax = r.sb(f"nmax{k}", [P, TT])
                self.prob = r.sb(f"prob{k}", [P, TT, CTX])
                self.rs = r.sb(f"rs{k}", [P, TT])
                self.ri = r.sb(f"ri{k}", [P, TT])
                self.probT = r.sb(f"probT{k}", [P, S])
                self.negtop = r.sb(f"negtop{k}", [1, 1])
                self.erow = r.sb(f"erow{k}", [1, S])
                self.es = r.sb(f"es{k}", [1, 1])
                self.ei = r.sb(f"ei{k}", [1, 1])
                self.arow = r.sb(f"arow{k}", [1, S])
                self.acol = r.sb(f"acol{k}", [P, TT])
                self.q2c = r.sb(f"q2c{k}", [P, DC])
                self.wad = r.sb(f"wad{k}", [P, DC, D])
                self.aT = r.sb(f"aT{k}", [P, DC, S])
                self.caT = r.sb(f"caT{k}", [P, DC, S])
                self.z = r.sb(f"z{k}", [P, TT, D])
                self.p0 = r.ps(f"p0{k}", [P, 512])
                self.p1 = r.ps(f"p1{k}", [P, 512])
                self.p2 = r.ps(f"p2{k}", [P, 512])
                self.p3 = r.ps(f"p3{k}", [P, 512])
                self.q_in = r.sem(f"q_in{k}")
                self.c_ready = r.sem(f"c_ready{k}")
                self.t_done = r.sem(f"t_done{k}")
                self.t_used = r.sem(f"t_used{k}")
                self.m_ready = r.sem(f"m_ready{k}")
                self.row_done = r.sem(f"row_done{k}")
                self.row_ready = r.sem(f"row_ready{k}")
                self.s_done = r.sem(f"s_done{k}")
                self.max_ready = r.sem(f"max_ready{k}")
                self.exp_ready = r.sem(f"exp_ready{k}")
                self.prob_ready = r.sem(f"prob_ready{k}")
                self.top_done = r.sem(f"top_done{k}")
                self.top_ready = r.sem(f"top_ready{k}")
                self.eexp_ready = r.sem(f"eexp_ready{k}")
                self.arow_ready = r.sem(f"arow_ready{k}")
                self.acol_done = r.sem(f"acol_done{k}")
                self.acol_ready = r.sem(f"acol_ready{k}")
                self.q2c_done = r.sem(f"q2c_done{k}")
                self.wad_ready = r.sem(f"wad_ready{k}")
                self.pt_done = r.sem(f"pt_done{k}")
                self.pt_used = r.sem(f"pt_used{k}")
                self.a_done = r.sem(f"a_done{k}")
                self.a_used = r.sem(f"a_used{k}")
                self.ca_ready = r.sem(f"ca_ready{k}")
                self.z_done = r.sem(f"z_done{k}")
                self.z_used = r.sem(f"z_used{k}")

        streams = [Stream(k) for k in range(NS)]
        block = ctx.enter_context(nc.Block())
        NLOAD = 4

        def each(eng, parts):
            def pair(n):
                for part in parts:
                    for z in streams:
                        part(z, n, NS * n + z.k)
            pair(0)
            with eng.Fori(1, B // NS) as n:
                pair(n)

        @block.sync
        def _(sp):
            sp.dma_start(wl[:], d["bidaf_wl"].rearrange("(c p) n -> p c n", p=P)).then_inc(loaded, 16)
            sp.dma_start(bl[:], d["bidaf_bl"].partition_broadcast(P)).then_inc(loaded, 16)
            sp.dma_start(vec[:], d["bidaf_vec"]).then_inc(loaded, 16)
            sp.dma_start(b3[:], d["bidaf_b"]).then_inc(loaded, 16)

            def fetch(z, n, b):
                wait(sp, z.a_done, n)
                sp.wait_ge(loaded, 16 * NLOAD)
                sp.dma_start(z.q[0:CTX, :], d["ctx"][b]).then_inc(z.q_in, 16)
            each(sp, [fetch])
            for z in streams:
                sp.wait_ge(z.q_in, 16 * (B // NS))

        @block.tensor
        def _(pe):
            pe.wait_ge(loaded, 16 * NLOAD)
            pe.wait_ge(ready, 1)

            def turn(z, n, b):
                pe.wait_ge(z.c_ready, n + 1)
                pe.wait_ge(z.q_in, 16 * (n + 1))
                wait(pe, z.a_used, n)
                wait(pe, z.acol_ready, n)
                for t in range(TT):
                    for c in range(DC):
                        nc.tensor.transpose(z.p0[:, c * S + t * P:c * S + (t + 1) * P], z.c[:, t, c * P:(c + 1) * P], ident[:])
                for c in range(DC):
                    mm = nc.tensor.transpose(z.p1[:, c * CTX:(c + 1) * CTX], z.q[0:CTX, c * P:(c + 1) * P],
                                             ident[0:CTX, 0:CTX])
                mm.then_inc(z.t_done, 1)

            def row(z, n, b):
                pe.wait_ge(z.t_used, n + 1)
                wait(pe, z.wad_ready, n)
                for c in range(DC):
                    mm = nc.tensor.matmul(z.p2[0:1, 0:CTX], vec[:, 2, c:c + 1], z.qT[:, c, :], start=(c == 0),
                                          stop=(c == DC - 1))
                mm.then_inc(z.row_done, 1)

            def scores(z, n, b):
                pe.wait_ge(z.row_ready, n + 1)
                pe.wait_ge(z.m_ready, n + 1)
                for t in range(TT):
                    for c in range(DC):
                        nc.tensor.matmul(z.p1[:, t * CTX:(t + 1) * CTX], z.cT[:, c, t * P:(t + 1) * P], z.m[:, c, :],
                                         start=(c == 0), stop=False)
                    mm = nc.tensor.matmul(z.p1[:, t * CTX:(t + 1) * CTX], ones[:], z.qrow[:], start=False, stop=True)
                mm.then_inc(z.s_done, 1)

            def top(z, n, b):
                pe.wait_ge(z.max_ready, n + 1)
                for t in range(TT):
                    mm = nc.tensor.matmul(z.p2[0:1, t * P:(t + 1) * P], z.nmax[:, t:t + 1], ident[:], start=True, stop=True)
                mm.then_inc(z.top_done, 1)

            def turn_prob(z, n, b):
                pe.wait_ge(z.prob_ready, n + 1)
                wait(pe, z.z_used, n)
                for t in range(TT):
                    mm = nc.tensor.transpose(z.p3[0:CTX, t * P:(t + 1) * P], z.prob[:, t, :], ident[:])
                mm.then_inc(z.pt_done, 1)

            def attend(z, n, b):
                pe.wait_ge(z.pt_used, n + 1)
                for c in range(DC):
                    mm = nc.tensor.matmul(z.p0[:, c * S:(c + 1) * S], z.q[0:CTX, c * P:(c + 1) * P], z.probT[0:CTX, :],
                                          start=True, stop=True)
                mm.then_inc(z.a_done, 1)

            def col(z, n, b):
                pe.wait_ge(z.arow_ready, n + 1)
                for t in range(TT):
                    mm = nc.tensor.matmul(z.p1[:, t:t + 1], z.arow[0:1, t * P:(t + 1) * P], ones[0:1, 0:1], start=True, stop=True)
                mm.then_inc(z.acol_done, 1)

            def q2c(z, n, b):
                pe.wait_ge(z.acol_ready, n + 1)
                for c in range(DC):
                    for t in range(TT):
                        mm = nc.tensor.matmul(z.p2[:, c:c + 1], z.c[:, t, c * P:(c + 1) * P], z.acol[:, t:t + 1],
                                              start=(t == 0), stop=(t == TT - 1))
                mm.then_inc(z.q2c_done, 1)

            def project(z, n, b):
                pe.wait_ge(z.wad_ready, n + 1)
                pe.wait_ge(z.a_used, n + 1)
                pe.wait_ge(z.ca_ready, n + 1)
                for t in range(TT):
                    ops = [(z.cT, z.wad, 0), (z.aT, wl, DC), (z.caT, wl, 2 * DC)]
                    for k, (lhs, w, off) in enumerate(ops):
                        for c in range(DC):
                            mm = nc.tensor.matmul(z.p3[:, t * D:(t + 1) * D], lhs[:, c, t * P:(t + 1) * P], w[:, off + c, :],
                                                  start=(k == 0 and c == 0), stop=(k == 2 and c == DC - 1))
                mm.then_inc(z.z_done, 1)

            each(pe, [turn, row, scores, top, turn_prob, attend, col, q2c, project])

        @block.scalar
        def _(act):
            act.wait_ge(loaded, 16 * NLOAD)
            act.wait_ge(ready, 1)
            nc.scalar.activation(warm[:], ident[:, 0:1], ACT.Exp)

            def take(z, n, b):
                act.wait_ge(z.t_done, n + 1)
                wait(act, z.z_done, n)
                nc.scalar.activation(z.cT[:].rearrange("p c s -> p (c s)"), z.p0[:], ACT.Copy)
                nc.scalar.activation(z.qT[:].rearrange("p c s -> p (c s)"), z.p1[:, 0:DC * CTX], ACT.Copy).then_inc(z.t_used, 1)

            def exps(z, n, b):
                act.wait_ge(z.max_ready, n + 1)
                for t in range(TT):
                    ins = nc.scalar.activation(z.prob[:, t, :], z.p1[:, t * CTX:(t + 1) * CTX], ACT.Exp,
                                               bias=z.nmax[:, t:t + 1], accum_out=z.rs[:, t:t + 1])
                ins.then_inc(z.exp_ready, 1)

            def eexp(z, n, b):
                act.wait_ge(z.top_ready, n + 1)
                nc.scalar.activation(z.erow[:], z.p2[0:1, 0:S], ACT.Exp, bias=z.negtop[:], scale=-1.0,
                                     accum_out=z.es[:]).then_inc(z.eexp_ready, 1)

            def take_prob(z, n, b):
                act.wait_ge(z.pt_done, n + 1)
                nc.scalar.activation(z.probT[0:CTX, :], z.p3[0:CTX, 0:S], ACT.Copy).then_inc(z.pt_used, 1)

            def take_a(z, n, b):
                act.wait_ge(z.a_done, n + 1)
                nc.scalar.activation(z.aT[:].rearrange("p c s -> p (c s)"), z.p0[:], ACT.Copy).then_inc(z.a_used, 1)

            each(act, [take, exps, eexp, take_prob, take_a])

        @block.vector
        def _(dve):
            dve.wait_ge(loaded, 16 * NLOAD)
            steps = Steps(dve, step)
            steps.link(nc.vector.tensor_reduce(bsum[:], b3[:], AX.X, ALU.add))
            nc.vector.memset(ones[:], 1.0).then_inc(ready, 1)
            dve.wait_ge(ready, 1)
            steps.again()

            def norm(z, n, b):
                wait(dve, z.q2c_done, n)
                for t in range(TT):
                    ins = nc.vector.tensor_scalar(z.c[:, t, :], x_all[:, b * TT + t, :], mean[:, b * TT + t, :],
                                                  rstd[:, b * TT + t, :], ALU.subtract, ALU.mult)
                ins.then_inc(z.c_ready, 1)

            def make_m(z, n, b):
                dve.wait_ge(z.t_used, n + 1)
                wait(dve, z.s_done, n)
                for c in range(DC):
                    ins = nc.vector.tensor_scalar(z.m[:, c, :], z.qT[:, c, :], vec[:, 0, c:c + 1],
                                                  vec[:, 1, c:c + 1], ALU.mult, ALU.add)
                ins.then_inc(z.m_ready, 1)

            def make_row(z, n, b):
                dve.wait_ge(z.row_done, n + 1)
                nc.vector.tensor_scalar(z.qrow[:], z.p2[0:1, 0:CTX], bsum[:], None, ALU.add).then_inc(z.row_ready, 1)

            def rowmax(z, n, b):
                dve.wait_ge(z.s_done, n + 1)
                nc.vector.tensor_reduce(z.nmax[:], z.p1[:, 0:TT * CTX].rearrange("p (t q) -> p t q", t=TT), AX.X,
                                        ALU.max, negate=True).then_inc(z.max_ready, 1)

            def find_top(z, n, b):
                dve.wait_ge(z.top_done, n + 1)
                nc.vector.tensor_reduce(z.negtop[:], z.p2[0:1, 0:S], AX.X, ALU.min).then_inc(z.top_ready, 1)

            def normalise(z, n, b):
                dve.wait_ge(z.exp_ready, n + 1)
                steps.link(nc.vector.reciprocal(z.ri[:], z.rs[:]))
                for t in range(TT):
                    ins = nc.vector.tensor_scalar(z.prob[:, t, :], z.prob[:, t, :], z.ri[:, t:t + 1], None, ALU.mult)
                ins.then_inc(z.prob_ready, 1)

            def batch_row(z, n, b):
                dve.wait_ge(z.eexp_ready, n + 1)
                steps.link(nc.vector.reciprocal(z.ei[:], z.es[:]))
                nc.vector.tensor_scalar(z.arow[:], z.erow[:], z.ei[:], None, ALU.mult).then_inc(z.arow_ready, 1)

            def take_col(z, n, b):
                dve.wait_ge(z.acol_done, n + 1)
                nc.vector.tensor_copy(z.acol[:], z.p1[:, 0:TT]).then_inc(z.acol_ready, 1)

            def make_wad(z, n, b):
                dve.wait_ge(z.q2c_done, n + 1)
                steps.link(nc.vector.tensor_copy(z.q2c[:], z.p2[:, 0:DC]))
                for c in range(DC):
                    ins = nc.vector.scalar_tensor_tensor(z.wad[:, c, :], wl[:, 3 * DC + c, :], z.q2c[:, c:c + 1],
                                                         wl[:, c, :], ALU.mult, ALU.add)
                ins.then_inc(z.wad_ready, 1)

            def product(z, n, b):
                dve.wait_ge(z.a_used, n + 1)
                nc.vector.tensor_tensor(z.caT[:], z.aT[:], z.cT[:], ALU.mult).then_inc(z.ca_ready, 1)

            def add(z, n, b):
                dve.wait_ge(z.z_done, n + 1)
                wait(dve, z.z_used, n)
                steps.link(nc.vector.tensor_tensor(z.z[:], z.p3[:].rearrange("p (t c) -> p t c", t=TT),
                                                   bl[:].unsqueeze(1).broadcast_to((P, TT, D)), ALU.add))
                for t in range(TT):
                    xt = x_all[:, b * TT + t, :]
                    ins = nc.vector.tensor_tensor(xt, z.z[:, t, :], xt, ALU.add)
                ins.then_inc(z.z_used, 1)
                if z.k == NS - 1:
                    steps.again()

            each(dve, [norm, make_m, make_row, rowmax, find_top, normalise, batch_row, product, take_col, make_wad, add])


E = 8
TOPE = 2
HID = 4 * D
HC = HID // P
HB = HC // 2
GT = 4
TOKENS = B * S
JT = (TOKENS * TOPE + E * (P - 1)) // P
JT += JT % 2
MAXT = TOKENS // P


def moe_stage(nc, x_all, mean, rstd, ident, d):
    with ExitStack() as ctx:
        r = Room(nc, ctx, "moe")
        sb, ps, sem = r.sb, r.ps, r.sem
        w1 = sb("w1", [P, E, DC, HID])
        w2 = sb("w2", [P, E, HC, D])
        b1 = sb("b1", [P, E, HC])
        b2 = sb("b2", [E, D])
        wr = sb("wr", [P, DC, E])
        br = sb("br", [P, E])
        iota = sb("iota", [P, P])
        pid = sb("pid", [P, 1])
        tri = sb("tri", [P, 2, P], BF16)
        xn = sb("xn", [P, GT, D])
        xnT = sb("xnT", [P, DC, GT * P])
        logit = sb("logit", [P, GT, E])
        top = sb("top", [P, GT, 8])
        topi = sb("topi", [P, GT, 8], U32)
        topf = sb("topf", [P, GT, 8])
        ew = sb("ew", [P, GT, TOPE])
        es = sb("es", [P, GT, 1])
        er = sb("er", [P, GT, 1])
        rw = sb("rw", [P, GT, TOPE, E])
        rwT = sb("rwT", [E, GT * P])
        hot = sb("hot", [P, TILES, TOPE, E], BF16)
        count = sb("count", [P, TILES, E], BF16)
        weight = sb("weight", [P, TILES, TOPE])
        slot = sb("slot", [P, TILES, TOPE], I32)
        token = sb("token", [P, JT], I32)
        expert = sb("expert", [1, JT], I32)
        column = sb("column", [P, 2], I32)

        room = x_all[:].rearrange("p t c -> p (t c)")

        def view(start, *shape):
            names = "abcd"[:len(shape)]
            ap = room[:, start:start + int(np.prod(shape))]
            return ap.rearrange(f"p ({' '.join(names)}) -> p {' '.join(names)}", **dict(zip(names[1:], shape[1:])))
        at = 0
        xg = view(at, 2, D)
        at += 2 * D
        xgT = view(at, 2, DC, P)
        at += 2 * D
        h = view(at, 2, HID)
        at += 2 * HID
        hT = view(at, 2, HC, P)
        at += 2 * HID
        y = view(at, 2, D)
        at += 2 * D
        pair = view(at, 2, 2, TOPE, D)
        xr = view(0, 2, 2, D)
        at = 0
        full = view(at, TILES, E)
        at += TILES * E
        picked = view(at, TILES, TOPE, E)
        at += TILES * TOPE * E
        slotf = view(at, TILES, TOPE)
        at += TILES * TOPE
        tilef = view(at, TILES, TOPE)
        at += TILES * TOPE
        rowf = view(at, TILES, TOPE)
        at += TILES * TOPE
        total = view(at, E)
        at += E
        steps128 = view(at, MAXT)
        at += MAXT
        above = view(at, E, MAXT)
        at += E * MAXT
        ntile = view(at, E)
        at += E
        below = view(at, E, E)
        at += E * E
        prior = view(at, E, E)
        at += E * E
        first = view(at, E)
        at += E
        start = view(at, E)
        at += E
        tokf = view(at, JT)
        at += JT
        passed = view(at, JT, E)
        at += JT * E
        expf = view(at, JT)
        slot_int = sb("slot_int", [P, 2, TILES, TOPE], I32)
        rowhot = sb("rowhot", [P, 2, P], BF16)
        tilehot = sb("tilehot", [P, 2, 2, JT], BF16)

        xn_dram = nc.dram_tensor("moe_xn_rows", (TOKENS, D), F32).ap()
        x_dram = nc.dram_tensor("moe_x_rows", (TOKENS, D), F32).ap()
        y_dram = nc.dram_tensor("moe_y_rows", (JT * P, D), F32).ap()

        ps_x = ps("ps_x", [P, 512])
        ps_h = ps("ps_h", [P, 2, 512])
        ps_t = ps("ps_t", [P, 2, 512])
        ps_y = ps("ps_y", [P, 2, 512])

        loaded = sem("loaded")
        weights = sem("weights")
        const_ready = sem("const_ready")
        xn_ready = sem("xn_ready")
        xn_out = sem("xn_out")
        xt_done = sem("xt_done")
        xt_used = sem("xt_used")
        r_done = sem("r_done")
        exp_in = sem("exp_in")
        exp_out = sem("exp_out")
        rw_ready = sem("rw_ready")
        rwt_done = sem("rwt_done")
        rwt_used = sem("rwt_used")
        b_done = sem("b_done")
        b_used = sem("b_used")
        x_out = sem("x_out")
        rank_done = sem("rank_done")
        hot_ready = sem("hot_ready")
        hot_used = sem("hot_used")
        table_ready = sem("table_ready")
        column_ready = sem("column_ready")
        gathered = [sem(f"gathered{p}") for p in range(2)]
        xgt_done = sem("xgt_done")
        xgt_used = sem("xgt_used")
        h_done = sem("h_done")
        h_used = [sem(f"h_used{p}") for p in range(2)]
        ht_done = sem("ht_done")
        bias_ready = sem("bias_ready")
        relu_ready = sem("relu_ready")
        y_done = sem("y_done")
        y_used = sem("y_used")
        y_out = [sem(f"y_out{p}") for p in range(2)]
        xr_in = [sem(f"xr_in{p}") for p in range(2)]
        paired = [sem(f"paired{p}") for p in range(2)]
        sum_ready = sem("sum_ready")
        stored = [sem(f"stored{p}") for p in range(2)]
        step = sem("step")
        block = ctx.enter_context(nc.Block())
        NLOAD = 7
        G = TILES // GT
        assert G == E
        PAIRS = TILES // 2
        ROWS_G = GT * P


        def route_all(eng, e):
            e.norm(0)
            e.norm(1)
            e.route(0)
            with eng.Fori(1, G - 1) as g:
                e.norm(g + 1)
                e.route(g)
            e.route(G - 1)

        def tile_step(e, i, par, forward=(True, True), back=True):
            nxt = (i + 1, 0) if par else (i, 1)
            prv = (i, 0) if par else (i - 1, 1)
            if forward[1]:
                e.gather(i + 1, par)
            if forward[0]:
                e.turn(*nxt)
            e.hidden(i, par)
            if back:
                e.result(*prv)
            e.turn_hidden(i, par)

        def all_tiles(eng, e):
            e.gather(0, 0)
            e.gather(0, 1)
            e.turn(0, 0)
            tile_step(e, 0, 0, back=False)
            tile_step(e, 0, 1)
            tile_step(e, 1, 0)
            tile_step(e, 1, 1)
            with eng.Fori(2, JT // 2 - 1) as i:
                tile_step(e, i, 0)
                tile_step(e, i, 1)
            tile_step(e, JT // 2 - 1, 0, forward=(True, False))
            tile_step(e, JT // 2 - 1, 1, forward=(False, False))
            e.result(JT // 2 - 1, 1)

        class Part:

            def norm(self, g): pass
            def route(self, g): pass
            def gather(self, i, par): pass
            def turn(self, i, par): pass
            def hidden(self, i, par): pass
            def turn_hidden(self, i, par): pass
            def result(self, i, par): pass

        @block.sync
        def _(sp):
            def after(sem, value):
                sp.wait_ge(sem, value)
                sp.wait_ge(loaded, 16 * NLOAD)

            sp.dma_start(wr[:], d["moe_wr"].rearrange("(c p) n -> p c n", p=P)).then_inc(loaded, 16)
            sp.dma_start(br[:], d["moe_br"].partition_broadcast(P)).then_inc(loaded, 16)
            sp.dma_start(iota[:], d["iota"]).then_inc(loaded, 16)
            sp.dma_start(pid[:], d["pid"]).then_inc(loaded, 16)
            sp.dma_start(xn[:, 0, 0:P], d["tri"]).then_inc(loaded, 16)
            sp.dma_start(b1[:], d["moe_b1"]).then_inc(loaded, 16)
            sp.dma_start(b2[:], d["moe_b2"]).then_inc(loaded, 16)
            w1_in = d["moe_w1"].rearrange("e (c p) n -> p e c n", p=P)
            w2_in = d["moe_w2"].rearrange("e (c p) n -> p e c n", p=P)

            def tiles_of(dram):
                return dram.rearrange("(t p) c -> p t c", p=P)

            class Sync(Part):
                def norm(self, g):
                    after(xn_ready, g + 1)
                    sp.dma_start(tiles_of(xn_dram)[:, bass.ds(g * GT, GT), :], xn[:]).then_inc(xn_out, 16)

                def route(self, g):
                    after(b_used, GT * (g + 1))
                    sp.dma_start(tiles_of(x_dram)[:, bass.ds(g * GT, GT), :],
                                 x_all[:, bass.ds(g * GT, GT), :]).then_inc(x_out, 16)
                    sp.dma_start(w1[:, bass.ds(g, 1)], w1_in[:, bass.ds(g, 1)]).then_inc(weights, 16)
                    sp.dma_start(w2[:, bass.ds(g, 1)], w2_in[:, bass.ds(g, 1)]).then_inc(weights, 16)

                def result(self, i, par):
                    after(y_used, 2 * i + par + 1)
                    sp.dma_start(tiles_of(y_dram)[:, bass.ds(2 * i + par, 1), :],
                                 y[:, par:par + 1, :]).then_inc(y_out[par], 16)
            e = Sync()
            route_all(sp, e)
            all_tiles(sp, e)

            out = d["out"].rearrange("b (t p) c -> p (b t) c", p=P)

            def fetch(i, par):
                sp.dma_start(xr[:, par], tiles_of(x_dram)[:, bass.ds(4 * i + 2 * par, 2), :]).then_inc(xr_in[par], 16)

            def store(i, par):
                after(sum_ready, 2 * i + par + 1)
                sp.dma_start(out[:, bass.ds(4 * i + 2 * par, 2), :], xr[:, par]).then_inc(stored[par], 16)
            sp.wait_ge(y_used, JT)
            sp.wait_ge(x_out, 16 * G)
            fetch(0, 0)
            fetch(0, 1)
            with sp.Fori(0, PAIRS // 2 - 1) as i:
                for par in range(2):
                    store(i, par)
                    after(stored[par], 16 * (i + 1))
                    fetch(i + 1, par)
            for par in range(2):
                store(PAIRS // 2 - 1, par)
            for par in range(2):
                sp.wait_ge(stored[par], 16 * (PAIRS // 2))

        @block.tensor
        def _(pe):
            pe.wait_ge(loaded, 16 * NLOAD)
            pe.wait_ge(const_ready, 1)

            class Tensor(Part):
                def norm(self, g):
                    pe.wait_ge(xn_ready, g + 1)
                    for c in range(DC):
                        for t in range(GT):
                            mm = nc.tensor.transpose(ps_t[:, c, t * P:(t + 1) * P], xn[:, t, c * P:(c + 1) * P], ident[:])
                    mm.then_inc(xt_done, 1)
                    pe.wait_ge(xt_used, g + 1)
                    wait(pe, exp_in, g)
                    for t in range(GT):
                        for c in range(DC):
                            mm = nc.tensor.matmul(ps_h[:, 0, t * E:(t + 1) * E], xnT[:, c, t * P:(t + 1) * P], wr[:, c, :],
                                                  start=(c == 0), stop=(c == DC - 1))
                    mm.then_inc(r_done, 1)

                def route(self, g):
                    pe.wait_ge(rw_ready, g + 1)
                    for t in range(GT):
                        mm = nc.tensor.transpose(ps_x[0:E, t * P:(t + 1) * P], rw[:, t, 0, :], ident[:])
                    mm.then_inc(rwt_done, 1)
                    pe.wait_ge(rwt_used, g + 1)
                    for t in range(GT):
                        wait(pe, b_used, GT * g + t - 1)
                        nc.tensor.matmul(ps_y[:, t % 2, 0:D], rwT[:, t * P:(t + 1) * P], b2[:],
                                         start=True, stop=True).then_inc(b_done, 1)

                def turn(self, i, par):
                    pe.wait_ge(gathered[par], 16 * (i + 1))
                    wait(pe, xgt_used, 2 * i + par)
                    for c in range(DC):
                        mm = nc.tensor.transpose(ps_x[:, c * P:(c + 1) * P], xg[:, par, c * P:(c + 1) * P], ident[:])
                    mm.then_inc(xgt_done, 1)

                def hidden(self, i, par):
                    ex = pe.value_load(expert[0:1, bass.ds(2 * i + par, 1)], min_val=0, max_val=E - 1)
                    pe.wait_ge(xgt_used, 2 * i + par + 1)
                    for half in range(2):
                        wait(pe, h_used[half], 2 * i + par)
                        for c in range(DC):
                            mm = nc.tensor.matmul(ps_h[:, half, :], xgT[:, par, c, :],
                                                  w1[:, ex, c, half * HB * P:(half + 1) * HB * P],
                                                  start=(c == 0), stop=(c == DC - 1))
                        mm.then_inc(h_done, 1)

                def turn_hidden(self, i, par):
                    for half in range(2):
                        pe.wait_ge(h_used[half], 2 * i + par + 1)
                        wait(pe, bias_ready, 2 * (2 * i + par) + half - 1)
                        for m in range(HB):
                            mm = nc.tensor.transpose(ps_t[:, half, m * P:(m + 1) * P],
                                                     h[:, par, (half * HB + m) * P:(half * HB + m + 1) * P], ident[:])
                        mm.then_inc(ht_done, 1)

                def result(self, i, par):
                    ex = pe.value_load(expert[0:1, bass.ds(2 * i + par, 1)], min_val=0, max_val=E - 1)
                    pe.wait_ge(relu_ready, 2 * (2 * i + par + 1))
                    wait(pe, y_used, 2 * i + par - 1)
                    for m in range(HC):
                        mm = nc.tensor.matmul(ps_y[:, par, 0:D], hT[:, par, m, :], w2[:, ex, m, :],
                                              start=(m == 0), stop=(m == HC - 1))
                    mm.then_inc(y_done, 1)
            e = Tensor()
            route_all(pe, e)

            pe.wait_ge(rw_ready, G)
            cnt = count[:].rearrange("p t e -> p (t e)")
            nc.tensor.matmul(ps_h[:, 0, 0:TILES * E], tri[:, 0, :], cnt, start=True, stop=False)
            for t in range(TILES - 1):
                later = TILES - 1 - t
                nc.tensor.matmul(ps_h[:, 0, (t + 1) * E:TILES * E], tri[:, 1, :],
                                 count[:, t:t + 1, :].broadcast_to((P, later, E)), start=False, stop=(t == TILES - 2))
            for t in range(TILES):
                mm = nc.tensor.matmul(ps_h[:, 1, 0:E], tri[:, 1, :], count[:, t, :], start=(t == 0), stop=(t == TILES - 1))
            mm.then_inc(rank_done, 1)

            def place(t, **ends):
                for k in range(TOPE):
                    pe.wait_ge(hot_ready, TOPE * t + k + 1)
                    nc.tensor.matmul(ps_y[:, 0, 0:2 * JT], rowhot[:, k, :], tilehot[:, k, :, :].rearrange("p a j -> p (a j)"),
                                     start=ends.get("start", False) and k == 0,
                                     stop=ends.get("stop", False) and k == TOPE - 1).then_inc(hot_used, 1)
            place(0, start=True)
            with pe.Fori(1, TILES - 1) as t:
                place(t)
            place(TILES - 1, stop=True)
            pe.wait_ge(table_ready, 1)
            pe.wait_ge(weights, 16 * 2 * E)
            all_tiles(pe, e)

        @block.scalar
        def _(act):
            act.wait_ge(loaded, 16 * NLOAD)
            nc.scalar.activation(es[:, 0, :], ident[:, 0:1], ACT.Exp)

            class Scalar(Part):
                def norm(self, g):
                    act.wait_ge(xt_done, g + 1)
                    wait(act, r_done, g)
                    for c in range(DC):
                        ins = nc.scalar.activation(xnT[:, c, :], ps_t[:, c, :], ACT.Copy)
                    ins.then_inc(xt_used, 1)

                def route(self, g):
                    act.wait_ge(exp_in, g + 1)
                    nc.scalar.activation(ew[:], ew[:], ACT.Exp).then_inc(exp_out, 1)
                    act.wait_ge(rwt_done, g + 1)
                    wait(act, b_done, GT * g)
                    nc.scalar.activation(rwT[:], ps_x[0:E, :], ACT.Copy).then_inc(rwt_used, 1)

                def turn(self, i, par):
                    act.wait_ge(xgt_done, 2 * i + par + 1)
                    wait(act, h_done, 2 * (2 * i + par - 1))
                    nc.scalar.activation(xgT[:, par].rearrange("p c q -> p (c q)"), ps_x[:, 0:D], ACT.Copy).then_inc(xgt_used, 1)

                def hidden(self, i, par):
                    act.wait_ge(h_done, 2 * (2 * i + par) + 1)
                    wait(act, ht_done, 2 * (2 * i + par - 1))
                    nc.scalar.activation(h[:, par, 0:HB * P], ps_h[:, 0, :], ACT.Copy).then_inc(h_used[0], 1)

                def turn_hidden(self, i, par):
                    for half in range(2):
                        act.wait_ge(bias_ready, 2 * (2 * i + par) + half + 1)
                        v = hT[:, par, half * HB:(half + 1) * HB, :]
                        nc.scalar.activation(v, v, ACT.Relu).then_inc(relu_ready, 1)
            e = Scalar()
            route_all(act, e)
            act.wait_ge(table_ready, 1)
            all_tiles(act, e)

        @block.gpsimd
        def _(pool):
            pool.wait_ge(table_ready, 1)
            pool.wait_ge(xn_out, 16 * G)
            for j in range(JT):
                pool.wait_ge(column_ready, j + 1)
                wait(pool, xgt_done, j - 1)
                nc.gpsimd.indirect_dma_start(xg[:, j % 2, :], None, xn_dram,
                                             bass.IndirectOffsetOnAxis(column[:, j % 2:j % 2 + 1], 0)).then_inc(gathered[j % 2], 16)
            for p in range(2):
                pool.wait_ge(y_out[p], 16 * (JT // 2))
            for q in range(PAIRS):
                wait(pool, sum_ready, q - 1)
                for u in range(2):
                    for k in range(TOPE):
                        nc.gpsimd.indirect_dma_start(pair[:, q % 2, u, k, :], None, y_dram,
                                                     bass.IndirectOffsetOnAxis(slot[:, 2 * q + u, k:k + 1], 0)).then_inc(paired[q % 2], 16)

        @block.vector
        def _(dve):
            dve.wait_ge(loaded, 16 * NLOAD)
            steps = Steps(dve, step)
            nc.vector.memset(tri[:, 1, :], 1.0)
            nc.vector.tensor_copy(tri[:, 0, :], xn[:, 0, 0:P]).then_inc(const_ready, 1)
            dve.wait_ge(const_ready, 1)

            class Vector(Part):
                def norm(self, g):
                    wait(dve, xt_done, g)
                    wait(dve, xn_out, 16 * g)
                    for t in range(GT):
                        ins = nc.vector.tensor_scalar(xn[:, t, :], x_all[:, g * GT + t, :], mean[:, g * GT + t, :],
                                                      rstd[:, g * GT + t, :], ALU.subtract, ALU.mult)
                    ins.then_inc(xn_ready, 1)

                def route(self, g):
                    group = bass.ds(g * GT, GT)
                    dve.wait_ge(r_done, g + 1)
                    steps.link(nc.vector.tensor_tensor(logit[:], ps_h[:, 0, 0:GT * E].rearrange("p (t e) -> p t e", e=E),
                                                       br[:].unsqueeze(1).broadcast_to((P, GT, E)), ALU.add))
                    for t in range(GT):
                        ins = nc.vector.max(top[:, t, :], logit[:, t, :])
                    steps.link(ins)
                    nc.vector.tensor_tensor(ew[:], top[:, :, 0:TOPE], top[:, :, 0:1].broadcast_to((P, GT, TOPE)),
                                            ALU.subtract).then_inc(exp_in, 1)
                    for t in range(GT):
                        ins = nc.vector.max_index(topi[:, t, :], top[:, t, :], logit[:, t, :])
                    steps.link(ins)
                    steps.link(nc.vector.tensor_copy(topf[:], topi[:]))
                    steps.link(nc.vector.tensor_tensor(hot[:, group, :, :],
                                                       iota[:, 0:E].unsqueeze(1).unsqueeze(1).broadcast_to((P, GT, TOPE, E)),
                                                       topf[:, :, 0:TOPE].unsqueeze(3).broadcast_to((P, GT, TOPE, E)), ALU.is_equal))
                    nc.vector.tensor_tensor(count[:, group, :], hot[:, group, 0, :], hot[:, group, 1, :], ALU.add)
                    dve.wait_ge(exp_out, g + 1)
                    steps.link(nc.vector.tensor_reduce(es[:], ew[:], AX.X, ALU.add))
                    steps.link(nc.vector.reciprocal(er[:], es[:]))
                    steps.link(nc.vector.tensor_tensor(weight[:, group, :], ew[:], er[:].broadcast_to((P, GT, TOPE)), ALU.mult))
                    wait(dve, rwt_done, g)
                    steps.link(nc.vector.tensor_tensor(rw[:], hot[:, group, :, :],
                                                       weight[:, group, :].unsqueeze(3).broadcast_to((P, GT, TOPE, E)), ALU.mult))
                    nc.vector.tensor_tensor(rw[:, :, 0, :], rw[:, :, 0, :], rw[:, :, 1, :], ALU.add).then_inc(rw_ready, 1)
                    for t in range(GT):
                        dve.wait_ge(b_done, GT * g + t + 1)
                        xt = x_all[:, g * GT + t, :]
                        nc.vector.tensor_tensor(xt, ps_y[:, t % 2, 0:D], xt, ALU.add).then_inc(b_used, 1)
                    steps.again()

                def gather(self, i, par):
                    wait(dve, gathered[par], 16 * i)
                    nc.vector.tensor_copy(column[:, par:par + 1], token[:, bass.ds(2 * i + par, 1)]).then_inc(column_ready, 1)

                def hidden(self, i, par):
                    dve.wait_ge(h_done, 2 * (2 * i + par) + 2)
                    wait(dve, ht_done, 2 * (2 * i + par - 1))
                    nc.vector.tensor_copy(h[:, par, HB * P:HID], ps_h[:, 1, :]).then_inc(h_used[1], 1)

                def turn_hidden(self, i, par):
                    ex = dve.value_load(expert[0:1, bass.ds(2 * i + par, 1)], min_val=0, max_val=E - 1)
                    wait(dve, y_done, 2 * i + par - 1)
                    for half in range(2):
                        dve.wait_ge(ht_done, 2 * (2 * i + par) + half + 1)
                        chunks = slice(half * HB, (half + 1) * HB)
                        nc.vector.tensor_tensor(hT[:, par, chunks, :], ps_t[:, half, :].rearrange("p (m q) -> p m q", m=HB),
                                                b1[:, ex, chunks].unsqueeze(2).broadcast_to((P, HB, P)),
                                                ALU.add).then_inc(bias_ready, 1)

                def result(self, i, par):
                    dve.wait_ge(y_done, 2 * i + par + 1)
                    wait(dve, y_out[par], 16 * i)
                    nc.vector.tensor_copy(y[:, par, :], ps_y[:, par, 0:D]).then_inc(y_used, 1)
            e = Vector()
            route_all(dve, e)

            dve.wait_ge(rank_done, 1)
            dve.wait_ge(x_out, 16 * G)
            nc.vector.tensor_scalar(steps128, iota[:, 0:MAXT], float(P), None, ALU.mult)
            nc.vector.tensor_tensor(below, iota[:, 0:E].unsqueeze(2).broadcast_to((P, E, E)),
                                    iota[:, 0:E].unsqueeze(1).broadcast_to((P, E, E)), ALU.is_gt)
            steps.link(nc.vector.tensor_copy(total, ps_h[:, 1, 0:E]))
            steps.link(nc.vector.tensor_tensor(above, total.unsqueeze(2).broadcast_to((P, E, MAXT)),
                                               steps128.unsqueeze(1).broadcast_to((P, E, MAXT)), ALU.is_gt))
            steps.link(nc.vector.tensor_reduce(ntile, above, AX.X, ALU.add))
            steps.link(nc.vector.tensor_tensor(prior, ntile.unsqueeze(1).broadcast_to((P, E, E)), below, ALU.mult))
            steps.link(nc.vector.tensor_reduce(first, prior, AX.X, ALU.add))
            steps.link(nc.vector.tensor_scalar(start, first, float(P), None, ALU.mult))
            steps.link(nc.vector.tensor_tensor(full, ps_h[:, 0, 0:TILES * E].rearrange("p (t e) -> p t e", e=E),
                                               start.unsqueeze(1).broadcast_to((P, TILES, E)), ALU.add))
            steps.link(nc.vector.tensor_tensor(picked, hot[:], full.unsqueeze(2).broadcast_to((P, TILES, TOPE, E)), ALU.mult))
            steps.link(nc.vector.tensor_reduce(slotf, picked, AX.X, ALU.add))
            steps.link(nc.vector.tensor_copy(slot[:], slotf))
            nc.vector.tensor_scalar(slot_int[:, 0], slot[:], P.bit_length() - 1, None, ALU.logical_shift_right)
            steps.link(nc.vector.tensor_scalar(slot_int[:, 1], slot[:], P - 1, None, ALU.bitwise_and))
            nc.vector.tensor_copy(tilef, slot_int[:, 0])
            steps.link(nc.vector.tensor_copy(rowf, slot_int[:, 1]))

            def place(t):
                for k in range(TOPE):
                    wait(dve, hot_used, TOPE * t + k - 1)
                    nc.vector.tensor_scalar(rowhot[:, k, :], iota[:], rowf[:, t, k:k + 1], None, ALU.is_equal)
                    nc.vector.tensor_scalar(tilehot[:, k, 0, :], iota[:, 0:JT], tilef[:, t, k:k + 1], iota[:, bass.ds(t, 1)],
                                            ALU.is_equal, ALU.mult)
                    nc.vector.tensor_scalar(tilehot[:, k, 1, :], iota[:, 0:JT], tilef[:, t, k:k + 1], pid[:],
                                            ALU.is_equal, ALU.mult).then_inc(hot_ready, 1)
            place(0)
            with dve.Fori(1, TILES) as t:
                place(t)
            steps.link(nc.vector.tensor_tensor(passed[0:1], iota[0:1, 0:JT].unsqueeze(2).broadcast_to((1, JT, E)),
                                               first[0:1].unsqueeze(1).broadcast_to((1, JT, E)), ALU.is_ge))
            steps.link(nc.vector.tensor_reduce(expf[0:1], passed[0:1], AX.X, ALU.add))
            steps.link(nc.vector.tensor_scalar(expert[:], expf[0:1], -1.0, None, ALU.add))
            dve.wait_ge(hot_used, TOPE * TILES)
            steps.link(nc.vector.tensor_copy(tokf, ps_y[:, 0, JT:2 * JT]))
            steps.link(nc.vector.scalar_tensor_tensor(tokf, ps_y[:, 0, 0:JT], float(P), tokf, ALU.mult, ALU.add))
            nc.vector.tensor_copy(token[:], tokf).then_inc(table_ready, 1)
            dve.wait_ge(table_ready, 1)

            all_tiles(dve, e)
            steps.again()

            def add(i, par):
                dve.wait_ge(xr_in[par], 16 * (i + 1))
                dve.wait_ge(paired[par], 16 * 2 * TOPE * (i + 1))
                for k in range(TOPE):
                    for u in range(2):
                        t = 4 * i + 2 * par + u
                        ins = nc.vector.scalar_tensor_tensor(xr[:, par, u, :], pair[:, par, u, k, :], weight[:, t, k:k + 1],
                                                             xr[:, par, u, :], ALU.mult, ALU.add)
                    if k == 0:
                        steps.link(ins)
                ins.then_inc(sum_ready, 1)
            with dve.Fori(0, PAIRS // 2) as i:
                add(i, 0)
                add(i, 1)
                steps.again()



def _rows_first(np, wt):
    v = wt.reshape(wt.shape[:-1] + (DC, HEADS // DC, HD))
    return np.swapaxes(v, -1, -2).reshape(wt.shape)


def _slot_rows(np, wt):
    out = np.zeros((HEADS, SLOT, wt.shape[1]), wt.dtype)
    out[:, :HD] = wt.reshape(HEADS, HD, wt.shape[1])
    return out.reshape(HEADS * SLOT, wt.shape[1])


def _chunk_bias(np, b):
    return _rows_first(np, b).reshape(DC, P).T


def _pairs_swapped(wt):
    return wt.reshape(wt.shape[0], -1, 2)[:, :, ::-1].reshape(wt.shape)


def _constants(np):
    f = np.float32
    c = {"ident": np.eye(P, dtype=f), "iota": np.tile(np.arange(P, dtype=f), (P, 1))}
    freq = (1.0 / np.power(f(10000.0), np.arange(0, HD, 2, dtype=f) / f(HD))).astype(f)
    angle = np.arange(S, dtype=f)[None, :] * freq[:, None]
    cos, sin = np.cos(angle).astype(f), np.sin(angle).astype(f)
    ct, st = np.zeros((HD, S), f), np.zeros((HD, S), f)
    ct[0:HD:2], ct[1:HD:2] = cos, cos
    st[0:HD:2], st[1:HD:2] = -sin, sin
    ct, st = np.repeat(ct, HEADS // DC, 0), np.repeat(st, HEADS // DC, 0)
    c |= {"cosk": ct, "sink": st, "cosq": ct * f(0.25), "sinq": st * f(0.25)}
    far = np.full((P, P), -1e30, f)
    c["mask"] = np.concatenate([np.triu(far, 1), np.tril(far, -1)])
    row, col = np.arange(P)[:, None], np.arange(P)[None, :]
    c["pack"] = (row == col[:, :SLOT] % 4 * SLOT + HD).astype(f)
    c["spread"] = np.stack([row == SLOT * j + col // SLOT for j in range(4)], 1).astype(f)
    c["pid"] = np.arange(P, dtype=f)[:, None]
    c["tri"] = (row < col).astype(f)
    i = np.arange(S)
    near = np.abs(i[:, None] - i[None, :]) <= 2
    c["band"] = np.where(near, f(np.exp(0.1)), f(1.0)).astype(f)
    return c


def _lay_out(np, v):
    a = _constants(np)
    a["x"] = v["x"]
    a["ctx"] = v["ctx_1024"]
    wk, wq, wv = (m.T for m in np.split(v["L0_attn_W_KQV"], 3, axis=0))
    a |= {"causal_wq": _rows_first(np, wq), "causal_wk": _rows_first(np, wk), "causal_wv": wv,
          "causal_wqs": _rows_first(np, _pairs_swapped(wq)), "causal_wks": _rows_first(np, _pairs_swapped(wk)),
          "causal_wo": _slot_rows(np, v["L0_attn_W_O"].T)}
    for kind, name in (("cross", "L0_xattn"), ("band", "L1_attn")):
        a |= {f"{kind}_wq": _rows_first(np, v[f"{name}_Wq"].T), f"{kind}_wk": _rows_first(np, v[f"{name}_Wk"].T),
              f"{kind}_wv": v[f"{name}_Wv"].T, f"{kind}_wo": _slot_rows(np, v[f"{name}_Wo"].T),
              f"{kind}_bq": _chunk_bias(np, v[f"{name}_bq"]), f"{kind}_bk": _chunk_bias(np, v[f"{name}_bk"]),
              f"{kind}_bv": v[f"{name}_bv"], f"{kind}_bo": v[f"{name}_bo"]}
    a["band_bias"] = _chunk_bias(np, v["L1_attn_ocr_bias"])
    k1, k2 = v["L0_ffn_K1"].T, v["L0_ffn_K2"].T
    keys = np.zeros((4, HALF, 4, KEYS), k1.dtype)
    for n in range(4):
        keys[n, :, n, :] = (k1, k2)[n % 2]
    a |= {"peer_wq": v["L0_ffn_Wq"], "peer_bq": v["L0_ffn_bq"].reshape(4, P).T, "peer_keys": keys.reshape(P, 4 * KEYS),
          "peer_down": v["L0_ffn_W_down"][:EXPERTS].reshape(P, EV, D).transpose(2, 1, 0),
          "peer_up": v["L0_ffn_W_up"][:EXPERTS].reshape(P, EV, D)}
    wl = v["L1_xattn_W_l"].T
    a |= {"bidaf_wl": wl, "bidaf_bl": v["L1_xattn_b_l"],
          "bidaf_vec": np.stack([v["L1_xattn_w_cq"], v["L1_xattn_w_c"], v["L1_xattn_w_q"]]).reshape(3, DC, P).transpose(2, 0, 1),
          "bidaf_b": np.stack([v["L1_xattn_b_cq"], v["L1_xattn_b_c"], v["L1_xattn_b_q"]]).reshape(1, 3)}
    a |= {"moe_w1": v["L1_ffn_W1"], "moe_w2": v["L1_ffn_W2"], "moe_b2": v["L1_ffn_b2"], "moe_wr": v["L1_ffn_Wr"],
          "moe_br": v["L1_ffn_br"], "moe_b1": v["L1_ffn_b1"].reshape(E, HC, P).transpose(2, 0, 1)}
    return {k: np.ascontiguousarray(x) for k, x in a.items()}



def decoder(nc, d):
    with ExitStack() as ctx:
        def sb(name, shape):
            return ctx.enter_context(nc.sbuf_tensor(name, shape, F32))
        x_all = sb("x_all", [P, TILES, D])
        ident = sb("ident", [P, P])
        mean = sb("mean", [P, TILES, 1])
        rstd = sb("rstd", [P, TILES, 1])
        load_stage(nc, x_all, ident, d)
        norm_stage(nc, "norm0", x_all, mean, rstd)
        attention_stage(nc, "causal", x_all, mean, rstd, ident, d)
        norm_stage(nc, "norm1", x_all, mean, rstd)
        attention_stage(nc, "cross", x_all, mean, rstd, ident, d)
        norm_stage(nc, "norm2", x_all, mean, rstd)
        peer_stage(nc, x_all, mean, rstd, ident, d)
        norm_stage(nc, "norm3", x_all, mean, rstd)
        attention_stage(nc, "band", x_all, mean, rstd, ident, d)
        norm_stage(nc, "norm4", x_all, mean, rstd)
        bidaf_stage(nc, x_all, mean, rstd, ident, d)
        norm_stage(nc, "norm5", x_all, mean, rstd)
        moe_stage(nc, x_all, mean, rstd, ident, d)


def kernel(**inputs):
    import numpy as np
    import concourse.bacc as bacc
    from concourse.bass_utils import run_bass_kernel_spmd

    arrays = {f"in_{k}": v for k, v in _lay_out(np, {k: np.asarray(v) for k, v in inputs.items()}).items()}
    nc = bacc.Bacc("TRN2", target_bir_lowering=False, num_devices=1)
    d = {k[3:]: nc.dram_tensor(k, v.shape, mybir.dt.from_np(v.dtype), kind="ExternalInput").ap() for k, v in arrays.items()}
    d["out"] = nc.dram_tensor("out", (B, S, D), F32, kind="ExternalOutput").ap()
    decoder(nc, d)
    return run_bass_kernel_spmd(nc, [arrays], core_ids=[0]).results[0]["out"]
```
